# Optimizing a Trainium2 kernel written in Bass

```python
import numpy as np
import jax
import jax.numpy as jnp

def _softmax(x, axis=-1):
    return jax.nn.softmax(x, axis=axis)

def _gelu(x):
    return jax.nn.gelu(x, approximate=True)

def _silu(x):
    return jax.nn.silu(x)

def _sigmoid(x):
    return jax.nn.sigmoid(x)

def _layernorm(x, axis=-1, eps=1e-05):
    m = jnp.mean(x, axis=axis, keepdims=True)
    v = jnp.var(x, axis=axis, keepdims=True)
    return (x - m) / jnp.sqrt(v + eps)

def _scatter_add(tgt, idx, src, axis=0):
    return tgt.at[idx].add(src)

def _segment_sum(src, seg, n):
    return jax.ops.segment_sum(src, seg, n)
kernel_name = 'mk_prb_d1_jaxref_r8_62fd6f'

def setup_inputs(seed: int=0):
    np.random.seed(seed)
    _w = jnp.asarray

    def _L0_attn_setup():
        import jax, jax.numpy as jnp
        import numpy as np
        N_HEAD = 16
        LATENT = 32

        def _rotate_half(x):
            xe = x[..., ::2]
            xo = x[..., 1::2]
            return jnp.stack((-xo, xe), axis=-1).reshape(x.shape)

        def _rope_tables(T, latent_dim, dtype):
            inv_freq = 1.0 / 10000.0 ** (jnp.arange(0, latent_dim, 2, dtype=jnp.float32) / latent_dim)
            t = jnp.arange(T, dtype=jnp.float32)
            freqs = jnp.outer(t, inv_freq)
            cos = jnp.repeat(jnp.cos(freqs), 2, axis=-1)[:, :latent_dim]
            sin = jnp.repeat(jnp.sin(freqs), 2, axis=-1)[:, :latent_dim]
            return (cos.astype(dtype), sin.astype(dtype))
        key = jax.random.key(seed)
        ks = jax.random.split(key, 14)
        C = 128
        hd = C // N_HEAD
        L = LATENT
        s = 0.02
        return {'x': jax.random.normal(ks[0], (4, 256, C), jnp.float32), 'c_attn_w': jax.random.normal(ks[1], (3 * C, C), jnp.float32) * s, 'c_attn_b': jnp.zeros((3 * C,), jnp.float32), 'q2l_w': jax.random.normal(ks[2], (L, hd), jnp.float32) * s, 'q2l_b': jnp.zeros((L,), jnp.float32), 'kv2l_w': jax.random.normal(ks[3], (L, hd), jnp.float32) * s, 'kv2l_b': jnp.zeros((L,), jnp.float32), 'l2o_w': jax.random.normal(ks[4], (hd, L), jnp.float32) * s, 'l2o_b': jnp.zeros((hd,), jnp.float32), 'wqk_w': jax.random.normal(ks[5], (L, L), jnp.float32) * s, 'wqk_b': jnp.zeros((L,), jnp.float32), 'cproj_w': jax.random.normal(ks[6], (C, C), jnp.float32) * s, 'cproj_b': jnp.zeros((C,), jnp.float32)}
    _L0_attn_in = _L0_attn_setup()

    def _L0_ffn_setup():
        import jax, jax.numpy as jnp
        import numpy as np
        H, I, E_ROUTED, TOP_K = (128, 352, 7, 2)
        B, S = (4, 256)

        def _expert(h, g, u, d):
            return jnp.einsum('...i,hi->...h', jax.nn.silu(h @ g.T) * (h @ u.T), d)
        key = jax.random.key(seed)
        ks = jax.random.split(key, 10)
        sc = 0.02
        return {'x': jax.random.normal(ks[0], (B, S, H), dtype=jnp.float32), 'sg': jax.random.normal(ks[1], (I, H), dtype=jnp.float32) * sc, 'su': jax.random.normal(ks[2], (I, H), dtype=jnp.float32) * sc, 'sd': jax.random.normal(ks[3], (H, I), dtype=jnp.float32) * sc, 'rg': jax.random.normal(ks[4], (E_ROUTED, I, H), dtype=jnp.float32) * sc, 'ru': jax.random.normal(ks[5], (E_ROUTED, I, H), dtype=jnp.float32) * sc, 'rd': jax.random.normal(ks[6], (E_ROUTED, H, I), dtype=jnp.float32) * sc, 'wr': jax.random.normal(ks[7], (E_ROUTED, H), dtype=jnp.float32) * sc, 'rb': jnp.zeros((E_ROUTED,), dtype=jnp.float32)}
    _L0_ffn_in = _L0_ffn_setup()
    _d = {'L0_attn_x': _L0_attn_in['x'], 'L0_attn_c_attn_w': _L0_attn_in['c_attn_w'], 'L0_attn_c_attn_b': _L0_attn_in['c_attn_b'], 'L0_attn_q2l_w': _L0_attn_in['q2l_w'], 'L0_attn_q2l_b': _L0_attn_in['q2l_b'], 'L0_attn_kv2l_w': _L0_attn_in['kv2l_w'], 'L0_attn_kv2l_b': _L0_attn_in['kv2l_b'], 'L0_attn_l2o_w': _L0_attn_in['l2o_w'], 'L0_attn_l2o_b': _L0_attn_in['l2o_b'], 'L0_attn_wqk_w': _L0_attn_in['wqk_w'], 'L0_attn_wqk_b': _L0_attn_in['wqk_b'], 'L0_attn_cproj_w': _L0_attn_in['cproj_w'], 'L0_attn_cproj_b': _L0_attn_in['cproj_b'], 'L0_ffn_sg': _L0_ffn_in['sg'], 'L0_ffn_su': _L0_ffn_in['su'], 'L0_ffn_sd': _L0_ffn_in['sd'], 'L0_ffn_rg': _L0_ffn_in['rg'], 'L0_ffn_ru': _L0_ffn_in['ru'], 'L0_ffn_rd': _L0_ffn_in['rd'], 'L0_ffn_wr': _L0_ffn_in['wr'], 'L0_ffn_rb': _L0_ffn_in['rb']}
    _x0 = _d['L0_attn_x']
    _d['L0_attn_x'] = jax.random.normal(jax.random.fold_in(jax.random.key(seed), 1), (16, 512, 128), dtype=_x0.dtype)
    del _x0
    return _d

def reference(L0_attn_x, L0_attn_c_attn_w, L0_attn_c_attn_b, L0_attn_q2l_w, L0_attn_q2l_b, L0_attn_kv2l_w, L0_attn_kv2l_b, L0_attn_l2o_w, L0_attn_l2o_b, L0_attn_wqk_w, L0_attn_wqk_b, L0_attn_cproj_w, L0_attn_cproj_b, L0_ffn_sg, L0_ffn_su, L0_ffn_sd, L0_ffn_rg, L0_ffn_ru, L0_ffn_rd, L0_ffn_wr, L0_ffn_rb):

    def _L0_attn_ref(x, c_attn_w, c_attn_b, q2l_w, q2l_b, kv2l_w, kv2l_b, l2o_w, l2o_b, wqk_w, wqk_b, cproj_w, cproj_b):
        import jax, jax.numpy as jnp
        import numpy as np
        N_HEAD = 16
        LATENT = 32

        def _rotate_half(x):
            xe = x[..., ::2]
            xo = x[..., 1::2]
            return jnp.stack((-xo, xe), axis=-1).reshape(x.shape)

        def _rope_tables(T, latent_dim, dtype):
            inv_freq = 1.0 / 10000.0 ** (jnp.arange(0, latent_dim, 2, dtype=jnp.float32) / latent_dim)
            t = jnp.arange(T, dtype=jnp.float32)
            freqs = jnp.outer(t, inv_freq)
            cos = jnp.repeat(jnp.cos(freqs), 2, axis=-1)[:, :latent_dim]
            sin = jnp.repeat(jnp.sin(freqs), 2, axis=-1)[:, :latent_dim]
            return (cos.astype(dtype), sin.astype(dtype))
        B, T, C = x.shape
        H = N_HEAD
        hd = C // H
        L = q2l_w.shape[0]
        qkv = x @ c_attn_w.T + c_attn_b
        q, k, v = jnp.split(qkv, 3, axis=2)

        def heads(t):
            return t.reshape(B, T, H, hd).transpose(0, 2, 1, 3)
        q, k, v = (heads(q), heads(k), heads(v))
        q_lat = q @ q2l_w.T + q2l_b
        k_lat = k @ kv2l_w.T + kv2l_b
        v_lat = v @ kv2l_w.T + kv2l_b
        cos, sin = _rope_tables(T, L, x.dtype)
        cos = cos[None, None]
        sin = sin[None, None]
        q_lat = q_lat * cos + _rotate_half(q_lat) * sin
        k_lat = k_lat * cos + _rotate_half(k_lat) * sin
        q_for_k = q_lat @ wqk_w.T + wqk_b
        att = jnp.einsum('bhql,bhkl->bhqk', q_for_k, k_lat) * L ** (-0.5)
        causal = jnp.tril(jnp.ones((T, T), dtype=bool))
        att = jnp.where(causal[None, None], att, -jnp.inf)
        att = jax.nn.softmax(att, axis=-1)
        y_lat = jnp.einsum('bhqk,bhkl->bhql', att, v_lat)
        y = y_lat @ l2o_w.T + l2o_b
        y = y.transpose(0, 2, 1, 3).reshape(B, T, C)
        return y @ cproj_w.T + cproj_b

    def _L0_ffn_ref(x, sg, su, sd, rg, ru, rd, wr, rb):
        import jax, jax.numpy as jnp
        import numpy as np
        H, I, E_ROUTED, TOP_K = (128, 352, 7, 2)
        B, S = (4, 256)

        def _expert(h, g, u, d):
            return jnp.einsum('...i,hi->...h', jax.nn.silu(h @ g.T) * (h @ u.T), d)
        shared_out = _expert(x, sg, su, sd)
        logits = x @ wr.T + rb
        probs = jax.nn.softmax(logits, axis=-1)
        scores, idx = jax.lax.top_k(probs, TOP_K)
        scores = scores / scores.sum(axis=-1, keepdims=True)
        w = jnp.sum(scores[..., None] * jax.nn.one_hot(idx, E_ROUTED, dtype=x.dtype), axis=-2)
        out = shared_out
        for e in range(E_ROUTED):
            out = out + w[..., e:e + 1] * _expert(x, rg[e], ru[e], rd[e])
        return out
    x = L0_attn_x
    xn = _layernorm(x, axis=-1)
    x = x + _L0_attn_ref(xn, L0_attn_c_attn_w, L0_attn_c_attn_b, L0_attn_q2l_w, L0_attn_q2l_b, L0_attn_kv2l_w, L0_attn_kv2l_b, L0_attn_l2o_w, L0_attn_l2o_b, L0_attn_wqk_w, L0_attn_wqk_b, L0_attn_cproj_w, L0_attn_cproj_b) + _L0_ffn_ref(xn, L0_ffn_sg, L0_ffn_su, L0_ffn_sd, L0_ffn_rg, L0_ffn_ru, L0_ffn_rd, L0_ffn_wr, L0_ffn_rb)
    return x

_drawn_inputs = setup_inputs


def setup_inputs(seed=0):
    import zlib

    import numpy as np

    out = dict(_drawn_inputs(seed))
    spreads = {'L0_attn_c_attn_b': (0.0, 2.0),
     'L0_attn_q2l_b': (0.0, 2.0),
     'L0_attn_kv2l_b': (0.0, 2.0),
     'L0_attn_l2o_b': (0.0, 1.581),
     'L0_attn_wqk_b': (0.0, 2.0),
     'L0_attn_cproj_b': (0.0, 0.475),
     'L0_ffn_rb': (0.0, 0.8)}
    factors = {'L0_attn_c_attn_w': 64.0,
     'L0_attn_q2l_w': 64.0,
     'L0_attn_kv2l_w': 28.926,
     'L0_attn_l2o_w': 21.518,
     'L0_attn_wqk_w': 64.0,
     'L0_ffn_sg': 5.776,
     'L0_ffn_su': 5.666,
     'L0_ffn_sd': 5.699,
     'L0_ffn_rg': 8.0,
     'L0_ffn_ru': 8.0,
     'L0_ffn_rd': 8.0,
     'L0_ffn_wr': 8.0}
    for name, (base, spread) in spreads.items():
        noise = np.random.default_rng([zlib.crc32(name.encode()), seed]).standard_normal(out[name].shape)
        drawn = base * np.exp(spread * noise) if base else spread * noise
        out[name] = jnp.asarray(drawn.astype(out[name].dtype))
    for name, factor in factors.items():
        out[name] = (out[name] * factor).astype(out[name].dtype)
    return out
```

```python
from contextlib import ExitStack

import numpy as np

import concourse.bass as bass
from concourse import mybir

F32 = mybir.dt.float32
F32R = mybir.dt.float32r
BF16 = mybir.dt.bfloat16
ALU = mybir.AluOpType
ACT = mybir.ActivationFunctionType
X_AXIS = mybir.AxisListType.X

P = 128
B, T, C = 16, 512, 128
NT = T // P
H, HD, LAT = 16, 8, 32
GH = P // LAT
G = H // GH
LT = H * LAT
ROUTED, I = 7, 352
E = ROUTED + 1
CHUNKS = [(0, 128), (128, 128), (256, I - 256)]
EPS = 1e-5
SCALE = float(LAT) ** -0.5
MASKED = -1e30
SUM = HD

UNITS = G * NT * GH
HALF_UNITS = UNITS // 2
HG = G // 2
SLOTS = E * len(CHUNKS)
LAST_SLOT_STEP = 60
FIRST_PROJECT_AFTER = 1
TURN_LAG = 2
DOWN_LAG = 3
PROBS = 4


def step_plan():
    plan = {5: [("o_turned", G - 1, -1)], 8: [("y", 0, -1)]}
    for g in range(G - 1):
        plan[GH * NT * (g + 1) + 5] = [("o_turned", g, 0)]
    project = []
    for half in range(2):
        pair = (HG * half, HG * half + 1)
        keys = [[("k", t, 1), ("k_turned", t, 1)] for t in pair]
        queries, queries_wqk = [("q", t, 1) for t in pair], [("q_wqk", t, 1) for t in pair]
        project += [keys[0], queries, keys[1], queries_wqk] + ([[("v", 0, 1)]] if half == 0 else [])
    order = []
    for e in range(E):
        if e >= FIRST_PROJECT_AFTER + 1:
            order.append(project[e - FIRST_PROJECT_AFTER - 1])
        order += [[("gate", k, 0), ("up", k, 0)] for k in range(e * len(CHUNKS), (e + 1) * len(CHUNKS))]
    order += project[E - FIRST_PROJECT_AFTER - 1:]
    steps = [s for s in range(LAST_SLOT_STEP + 1) if s not in plan]
    for n, uses in enumerate(order):
        plan[steps[n * len(steps) // len(order)]] = uses
    return dict(sorted(plan.items())), project


PLAN, PROJECT = step_plan()
BANK = {"k": 0, "k_turned": 1, "gate": 0, "up": 1, "v": 1, "y": 0}


def bank_of(what, i):
    return BANK[what] if what in BANK else i % 2


BODY_USES = [use for uses in PLAN.values() for use in uses]
FIRST_USES = [(what, i, 0) for uses in PROJECT for what, i, _ in uses]


def use_before(b, what, i, off):
    bank = bank_of(what, i)
    if b == "first":
        uses, at, body = FIRST_USES, FIRST_USES.index((what, i, off)), "first"
    else:
        uses, at, body = BODY_USES, BODY_USES.index((what, i, off)), 0
    while True:
        at -= 1
        if at < 0:
            if body == "first":
                return None
            body -= 1
            if b is not None and b + body < 0:
                uses, body = FIRST_USES, "first"
            at = len(uses) - 1
        w, n, o = uses[at]
        if bank_of(w, n) != bank:
            continue
        if body == "first":
            return w, n, (0 if b == "first" else -b)
        owner = body + o
        if b is not None and not 0 <= b + owner < B:
            continue
        return w, n, owner


USE_STEP = {(what, i): s for s, uses in PLAN.items() for what, i, _ in uses}
GATE_STEP = {i: s for s, uses in PLAN.items() for what, i, _ in uses if what == "gate"}
DOWN_AT = {s + DOWN_LAG: k for k, s in GATE_STEP.items()}
CPROJ_AFTER = next(e for e in range(E) if GATE_STEP[3 * e + 2] + DOWN_LAG >= USE_STEP["y", 0] + 1)
CPROJ_STEP = GATE_STEP[3 * CPROJ_AFTER + 2] + DOWN_LAG + 1
assert CPROJ_STEP < GATE_STEP[3 * CPROJ_AFTER + 3] + DOWN_LAG and max(DOWN_AT) < UNITS
EXPERT_TAKEN = {GATE_STEP[3 * e + 2] + DOWN_LAG: e for e in range(E)}
SPLIT_LAG = 3
ACC_STEPS = ROUTED * NT + 1
ROUTE_STEPS = 18
GAP_STEP = 8
TAIL = CPROJ_STEP + 2


def on_act(u):
    return u % GH != 0


ACT_TAKES = [u for u in range(UNITS) if on_act(u)]
DVE_TAKES = [u for u in range(UNITS) if not on_act(u)]


class Batch:

    def __init__(self, pair, c):
        self.b, self.pair, self.c = pair * 2 + c, pair, c
        self.known = self.b if isinstance(self.b, int) else None

    def par(self, off=0):
        return (self.c + off) % 2

    def alike(self, off=0):
        return self.pair + (self.c + off) // 2 + 1

    def exists(self, off=0):
        return self.known is None or 0 <= self.known + off < B

    def back(self, step):
        return (0, step) if step >= 0 else (-1, step + UNITS)


def heads_at(step):
    q, r = divmod(step - (GH - 1) - TURN_LAG - 2, GH)
    if r:
        return None
    off, q = (0, q) if q >= 0 else (-1, q + G * NT)
    return (off, *divmod(q, NT))


def group_end(step):
    h = heads_at(step)
    return (h[0], h[1]) if h and h[2] == NT - 1 else None


def build(nc, x, gate_up, down, attn_w, bd_q, bd_kv, bd_qk, bd_o, cproj, biases, out_bias, router_w, router_b, ranks,
          ident, mask, rot, rot_t, cos, sin, out):
    xn_dram = nc.dram_tensor("normed_transposed", (B, P, T), F32, kind="Internal").ap()
    x_tiles = x.rearrange("b (t p) c -> p (b t) c", p=P)
    x_by_batch = x.rearrange("b (t p) c -> b p t c", p=P)
    out_tiles = out.rearrange("b (t p) c -> b p t c", p=P)
    TILES = B * NT

    with ExitStack() as ctx:
        def sb(name, shape, dt=F32):
            return ctx.enter_context(nc.sbuf_tensor(name, shape, dt))

        def psum(name, shape=(P, 512)):
            return ctx.enter_context(nc.psum_tensor(name, list(shape), F32))

        def sem(name):
            return ctx.enter_context(nc.semaphore(name))

        with ExitStack() as ahead:
            def early(name, shape, dt=F32):
                return ahead.enter_context(nc.sbuf_tensor(name, shape, dt))

            x_all = early("x_all", [P, TILES, C])
            attn_rows = early("attn_rows", [P, 3, C])
            bdq = early("bdq", [P, LT])
            bdkv = early("bdkv", [P, LT])
            bdo = early("bdo", [P, G, C])
            out_bias_rows = early("out_bias_rows", [P, C])
            mask_f = early("mask_f", [P, P])
            rot_sb = early("rot_sb", [P, P])
            rot_t_sb = early("rot_t_sb", [P, P])
            w_v_lat = early("w_v_lat", [P, G, C])
            o_spread = early("o_spread", [P, P])
            stats = early("stats", [P, TILES, 6])
            mean = early("mean", [P, TILES])
            spread = early("spread", [P, 4, TILES])
            rstd = early("rstd", [P, TILES])
            xn = early("xn", [P, 2, NT, C])
            xn_t = early("xn_t", [P, 2, T])
            logits = early("logits", [P, TILES, ROUTED])
            rt = early("rt", [P, 4, TILES, ROUTED])
            tops = early("tops", [P, 8, TILES])
        q_stack = sb("q_stack", [P, 2, GH, HG, T], F32R)
        k_stack = sb("k_stack", [P, 2, GH, HG, T], F32R)
        k_high = sb("k_high", [P, HG, T], F32R)
        k_low = sb("k_low", [P, HG, T], F32R)
        q_high = sb("q_high", [P, HG, T], F32R)
        q_low = sb("q_low", [P, HG, T], F32R)
        gate_up_w = sb("gate_up_w", [P, 2, E * I])
        down_w = sb("down_w", [P, E, len(CHUNKS), C])
        bdqk = sb("bdqk", [P, P])
        cproj_w = sb("cproj_w", [P, C])
        bias_cols = sb("bias_cols", [P, 8])
        wr = sb("wr", [P, ROUTED])
        rb = sb("rb", [P, ROUTED])
        identity = sb("identity", [P, P])
        identity_bf = sb("identity_bf", [P, P], BF16)
        mask_bf = sb("mask_bf", [P, P], BF16)
        cos_sb = sb("cos_sb", [P, T])
        sin_sb = sb("sin_sb", [P, T])
        rank = sb("rank", [P, ROUTED])
        w_q = sb("w_q", [P, LT])
        w_k = sb("w_k", [P, LT])
        w_k_turned = sb("w_k_turned", [P, LT])
        w_qk_turned = sb("w_qk_turned", [P, P])
        w_v = sb("w_v", [P, C])
        q_col = sb("q_col", [P, G])
        k_col = sb("k_col", [P, G])
        k_col_turned = sb("k_col_turned", [P, G])
        v_col = sb("v_col", [P, G])
        o_col = sb("o_col", [P, 1])
        out_add = sb("out_add", [P, C])
        weights = sb("weights", [P, TILES, ROUTED])
        xb = sb("xb", [P, 2, T])
        acc = sb("acc", [P, 2, NT, C])
        w_tok = sb("w_tok", [P, NT, ROUTED])
        k_lat = sb("k_lat", [P, T])
        k_sin = sb("k_sin", [P, T])
        q_cos = sb("q_cos", [P, 2, T])
        q_sin = sb("q_sin", [P, 2, T])
        q_lat = sb("q_lat", [P, 2, T])
        values = sb("values", [P, 2, NT * H, LAT])
        neg_max = sb("neg_max", [P, 8])
        probs = sb("probs", [P, PROBS, T])
        probs_t = sb("probs_t", [P, 2, GH, T])
        o_sb = sb("o_sb", [P, 2, T])
        o_rec = sb("o_rec", [P, 2, NT, GH])
        y_sb = sb("y_sb", [P, NT, C])
        y_t = sb("y_t", [P, T])
        hidden = sb("hidden", [P, 3, T])

        scores = [psum(f"scores{i}") for i in range(2)]
        turned = [psum(f"turned{i}") for i in range(2)]
        work = [psum(f"work{i}") for i in range(2)]
        o_ps = psum("o_ps")
        down_ps = psum("down_ps")

        consts_in = sem("consts_in")
        weights_in = sem("weights_in")
        down_in = sem("down_in")
        down_halved = sem("down_halved")
        o_col_ready = sem("o_col_ready")
        x_in = [sem(f"x_in{i}") for i in range(4)]
        zeroed = sem("zeroed")
        prep_products = sem("prep_products")
        prep_done = sem("prep_done")
        stats_done = sem("stats_done")
        mean_steps = sem("mean_steps")
        std_done = sem("std_done")
        rstd_steps = sem("rstd_steps")
        xn_ready = sem("xn_ready")
        xn_turned = sem("xn_turned")
        xn_t_ready = sem("xn_t_ready")
        xn_stored = [sem(f"xn_stored{i}") for i in range(2)]
        logits_ps = sem("logits_ps")
        logits_taken = sem("logits_taken")
        route_steps = sem("route_steps")
        gap_ready = sem("gap_ready")
        gap_exp = sem("gap_exp")
        xb_in = [sem(f"xb_in{i}") for i in range(2)]
        acc_in = [sem(f"acc_in{i}") for i in range(2)]
        acc_ready = sem("acc_ready")
        expert_added = sem("expert_added")
        attention_added = sem("attention_added")
        stored = [sem(f"stored{i}") for i in range(2)]
        k_ps = sem("k_ps")
        q_ps = sem("q_ps")
        q_wqk_ps = sem("q_wqk_ps")
        v_ps = sem("v_ps")
        gate_ps = sem("gate_ps")
        up_ps = sem("up_ps")
        o_turned_ps = sem("o_turned_ps")
        y_ps = sem("y_ps")
        k_parts = sem("k_parts")
        k_ready = sem("k_ready")
        k_high_ready = sem("k_high_ready")
        k_low_ready = sem("k_low_ready")
        q_parts = sem("q_parts")
        q_ready = sem("q_ready")
        q_high_ready = sem("q_high_ready")
        q_low_ready = sem("q_low_ready")
        stack_in = [sem(f"stack_in{i}") for i in range(2)]
        values_ready = sem("values_ready")
        w_tok_ready = sem("w_tok_ready")
        scores_ready = sem("scores_ready")
        max_ready = sem("max_ready")
        probs_ready = sem("probs_ready")
        probs_turned = sem("probs_turned")
        taken_act = sem("taken_act")
        taken_dve = sem("taken_dve")
        pv_done = sem("pv_done")
        o_taken = sem("o_taken")
        o_rec_ready = sem("o_rec_ready")
        y_parts = sem("y_parts")
        y_t_ready = sem("y_t_ready")
        cproj_done = sem("cproj_done")
        tanh_ready = sem("tanh_ready")
        tanh_used = sem("tanh_used")
        hidden_ready = sem("hidden_ready")
        down_done = sem("down_done")
        block = ctx.enter_context(nc.Block())

        def wait(eng, s, value):
            if not isinstance(value, int) or value > 0:
                eng.wait_ge(s, value)

        def batches(engine, batch):
            for b in range(2):
                batch(b, b, 0)
            with engine.Fori(1, B // 2) as pair:
                for par in range(2):
                    batch(pair * 2 + par, par, pair)

        def bodies(engine, body):
            body(Batch(0, 0))
            with engine.Fori(0, B // 2 - 1) as pair:
                for c in (1, 2):
                    body(Batch(pair, c))
            body(Batch(0, B - 1))
            body(Batch(0, B))

        def body_steps(n):
            return range(TAIL if n.known == B else UNITS)

        def taken(eng, b, u):
            if u < 0:
                b, u = b - 1, u + UNITS
            if on_act(u):
                wait(eng, taken_act, b * len(ACT_TAKES) + ACT_TAKES.index(u) + 1)
            else:
                wait(eng, taken_dve, b * len(DVE_TAKES) + DVE_TAKES.index(u) + 1)

        def take_probs(eng, copy, done, b, u):
            quad = u // GH
            n = P * (quad % NT + 1)
            wait(eng, probs_turned, b * UNITS + u + 1)
            wait(eng, pv_done, b * G * NT + quad - 1)
            copy(probs_t[:, quad % 2, u % GH, 0:n], turned[u % 2][:, 0:n]).then_inc(done, 1)

        def filled(eng, what, i, b):
            s, count = {
                "k": (k_ps, 2 * (b * G + i) + 1), "k_turned": (k_ps, 2 * (b * G + i) + 2), "q": (q_ps, b * G + i + 1),
                "q_wqk": (q_wqk_ps, b * G + i + 1), "v": (v_ps, b + 1), "gate": (gate_ps, b * SLOTS + i + 1),
                "up": (up_ps, b * SLOTS + i + 1), "o_turned": (o_turned_ps, b * G + i + 1), "y": (y_ps, b + 1)}[what]
            wait(eng, s, count)
            return work[bank_of(what, i)]

        def stacks_copied(eng, b, t):
            if t < HG:
                wait(eng, stack_in[1], b * STACK_COPIES * 16)
            else:
                wait(eng, stack_in[0], (b + 1) * STACK_COPIES * 16)

        STACK_COPIES = 2 * GH * 4

        CONST_LOADS = (
            (attn_rows[:], attn_w.rearrange("a p c -> p a c")), (bdq[:], bd_q), (bdkv[:], bd_kv), (bdqk[:], bd_qk),
            (bdo[:], bd_o.rearrange("(g p) c -> p g c", p=P)), (cproj_w[:], cproj), (bias_cols[:], biases),
            (out_bias_rows[:], out_bias.to_broadcast([P, C])), (wr[:], router_w), (rb[:], router_b.to_broadcast([P, ROUTED])),
            (rank[:], ranks.to_broadcast([P, ROUTED])), (identity[:], ident), (mask_f[:], mask),
            (rot_sb[:], rot), (rot_t_sb[:], rot_t), (cos_sb[:], cos), (sin_sb[:], sin),
        )
        PREP_COLUMNS = 12
        PREP_SPREAD = 15
        PREP_ALL = 16

        @block.sync
        def _(sp):
            n = TILES // len(x_in)
            for c, loaded in enumerate(x_in):
                sp.dma_start(x_all[:, c * n:(c + 1) * n, :], x_tiles[:, c * n:(c + 1) * n, :]).then_inc(loaded, 16)
            for dst, src in CONST_LOADS:
                sp.dma_start(dst, src).then_inc(consts_in, 16)
            sp.dma_start(gate_up_w[:], gate_up.rearrange("a p n -> p a n")).then_inc(weights_in, 16)
            for n, (first, m) in enumerate(CHUNKS):
                sp.dma_start(down_w[0:m, :, n, :], down[:, first:first + m, :].rearrange("e p c -> p e c")).then_inc(down_in, 16)

            def store_xn(b, par, turn):
                wait(sp, xn_t_ready, b + 1)
                sp.dma_start(xn_dram[bass.ds(b, 1)].rearrange("a p n -> p (a n)"), xn_t[:, par, :]).then_inc(xn_stored[par], 16)

            batches(sp, store_xn)
            for par in range(2):
                sp.wait_ge(xn_stored[par], 16 * (B // 2))

            def load_xb(n, off):
                src = xn_dram[bass.ds(n.b + off, 1)].rearrange("a p n -> p (a n)")
                if off:
                    wait(sp, up_ps, (n.b + off - 1) * SLOTS)
                sp.dma_start(xb[:, n.par(off), :], src).then_inc(xb_in[n.par(off)], 16)

            def load_acc(n, off):
                src = x_by_batch[bass.ds(n.b + off, 1)].rearrange("a p t c -> p (a t) c")
                if off and n.exists(off - 2):
                    wait(sp, stored[n.par(off)], n.alike(off - 2) * 16)
                sp.dma_start(acc[:, n.par(off)], src).then_inc(acc_in[n.par(off)], 16)

            counts = [nc.sync.alloc_register(f"count{i}") for i in range(4)]

            def counted(value, reg):
                if isinstance(value, int):
                    return value
                nc.sync.reg_mov(counts[reg], value)
                return nc.sync.snap(counts[reg])

            def copy_stacks(half, read, split):
                wait(sp, scores_ready, read)
                wait(sp, k_low_ready, split)
                wait(sp, q_low_ready, split)
                for stack, parts in ((q_stack, (q_high, q_high, q_low, q_low)), (k_stack, (k_high, k_low, k_high, k_low))):
                    for r in range(GH):
                        for n, part in enumerate(parts):
                            sp.dma_start(stack[n * LAT:(n + 1) * LAT, half, r].bitcast(F32),
                                         part[r * LAT:(r + 1) * LAT].bitcast(F32)).then_inc(stack_in[half], 16)

            def store_out(n, off):
                dst = out_tiles[bass.ds(n.b + off, 1)].rearrange("a p t c -> p (a t) c")
                wait(sp, attention_added, n.b + off + 1)
                sp.dma_start(dst, acc[:, n.par(off)]).then_inc(stored[n.par(off)], 16)

            def body(n):
                b = n.b
                read_low = counted(b * UNITS, 0)
                split_low = counted((b + 1) * G, 1)
                read_high = counted(b * UNITS + HALF_UNITS, 2)
                split_high = counted((b + 1) * G + HG, 3)
                if n.exists(1):
                    load_xb(n, 1)
                if n.exists():
                    copy_stacks(1, read_low, split_low)
                if n.exists(-1):
                    store_out(n, -1)
                if n.exists(1):
                    load_acc(n, 1)
                    copy_stacks(0, read_high, split_high)

            first = Batch(0, 0)
            load_xb(first, 0)
            load_acc(first, 0)
            wait(sp, route_steps, ROUTE_STEPS)
            copy_stacks(0, 0, HG)
            bodies(sp, body)
            for par in range(2):
                sp.wait_ge(stored[par], 16 * (B // 2))

        @block.gpsimd
        def _(pool):
            pool.memset(values[:], 0.0).then_inc(zeroed, 1)
            pool.wait_ge(zeroed, 1)
            pool.memset(values[:, :, :, SUM:SUM + 1], 1.0).then_inc(zeroed, 1)
            pool.wait_ge(prep_done, PREP_ALL)

            def add_residual(n, off):
                mine = acc[:, n.par(off)]
                wait(pool, acc_in[n.par(off)], n.alike(off) * 16)
                pool.tensor_tensor(mine, mine, out_add[:].unsqueeze(1).to_broadcast([P, NT, C]), ALU.add).then_inc(acc_ready, 1)

            def key_tile(b, t):
                wait(pool, k_parts, 2 * (b * G + t + 1))
                pool.tensor_tensor(k_lat[:], k_lat[:], k_sin[:], ALU.add).then_inc(k_ready, 1)
                wait(pool, k_high_ready, b * G + t + 1)
                pool.tensor_tensor(k_low[:, t % HG, :], k_lat[:], k_high[:, t % HG, :].bitcast(F32), ALU.subtract).then_inc(k_low_ready, 1)

            def query_tile(b, t):
                wait(pool, q_high_ready, b * G + t + 1)
                pool.tensor_tensor(q_low[:, t % HG, :], q_lat[:, t % 2, :], q_high[:, t % HG, :].bitcast(F32), ALU.subtract).then_inc(q_low_ready, 1)

            def split(b):
                for uses in PROJECT:
                    what = uses[0][0]
                    for _, t, _ in uses:
                        if what == "q_wqk":
                            query_tile(b, t)
                    if what == "k":
                        key_tile(b, uses[0][1])

            def body(n):
                if n.exists(1):
                    split(n.b + 1)
                    add_residual(n, 1)

            add_residual(Batch(0, 0), 0)
            split(0)
            bodies(pool, body)

        @block.scalar
        def _(act):
            A = nc.scalar
            act.wait_ge(rstd_steps, 1)
            A.activation(spread[:, 1, :], spread[:, 0, :], ACT.Sqrt).then_inc(std_done, 1)

            def take_xn(b, par, turn):
                wait(act, xn_turned, b + 1)
                wait(act, logits_ps, b - 1)
                wait(act, xn_stored[par], turn * 16)
                A.copy(xn_t[:, par, :], work[par][:]).then_inc(xn_t_ready, 1)

            batches(act, take_xn)
            act.wait_ge(route_steps, GAP_STEP)
            A.activation(tops[:, 3, :], tops[:, 2, :], ACT.Exp).then_inc(gap_exp, 1)

            def split_high(b, what, t):
                lat, high, ready, done = (k_lat, k_high, k_ready, k_high_ready) if what == "k" else (q_lat, q_high, q_ready, q_high_ready)
                wait(act, ready, b * G + t + 1)
                stacks_copied(act, b, t)
                A.copy(high[:, t % HG, :], lat[:] if what == "k" else lat[:, t % 2, :]).then_inc(done, 1)

            def body(n):
                b = n.b
                for s in body_steps(n):
                    if n.exists():
                        w = P * ((s // GH) % NT + 1)
                        wait(act, max_ready, b * UNITS + s + 1)
                        wait(act, probs_turned, b * UNITS + s - PROBS + 1)
                        A.activation(probs[:, s % PROBS, 0:w], scores[s % 2][:, 0:w], ACT.Exp,
                                     bias=neg_max[:, s % 8:s % 8 + 1]).then_inc(probs_ready, 1)
                    off, u = n.back(s - TURN_LAG)
                    if n.exists(off) and on_act(u):
                        take_probs(act, A.copy, taken_act, b + off, u)
                    for what, k, _ in PLAN.get(s, ()):
                        if what == "gate" and n.exists():
                            m = CHUNKS[k % 3][1]
                            bank = filled(act, "gate", k, b)
                            wait(act, down_done, b * SLOTS + k - 2)
                            A.activation(hidden[0:m, k % 3, :], bank[0:m, :], ACT.Tanh, scale=0.5).then_inc(tanh_ready, 1)
                    for what, t, off in PLAN.get(s - SPLIT_LAG, ()):
                        if n.exists(off) and what in ("k", "q_wqk"):
                            split_high(b + off, what, t)
                    end = group_end(s)
                    if end is not None and n.exists(end[0]):
                        off, g = end
                        wait(act, pv_done, (b + off) * G * NT + NT * (g + 1))
                        wait(act, o_turned_ps, (b + off) * G + g - 1)
                        A.copy(o_sb[:, g % 2, :], o_ps[:]).then_inc(o_taken, 1)

            for uses in PROJECT:
                for what, t, _ in uses:
                    if what in ("k", "q_wqk"):
                        split_high(0, what, t)
            bodies(act, body)

        @block.vector
        def _(dve):
            V = nc.vector

            for c, loaded in enumerate(x_in):
                dve.wait_ge(loaded, 16)
                n = TILES // len(x_in)
                with dve.Fori(c * n, (c + 1) * n) as tile:
                    V.bn_stats(stats[:, bass.ds(tile, 1), :].rearrange("p a n -> p (a n)"),
                               x_all[:, bass.ds(tile, 1), :].rearrange("p a n -> p (a n)")).then_inc(stats_done, 1)
            dve.wait_ge(stats_done, TILES)
            even, odd, even_sq, odd_sq = (stats[:, :, n:n + 1].rearrange("p n a -> p (n a)") for n in (1, 4, 2, 5))
            both, apart, summed, varied = (spread[:, n, :] for n in (1, 2, 3, 0))
            V.tensor_tensor(both, even, odd, ALU.add).then_inc(mean_steps, 1)
            V.tensor_tensor(apart, even, odd, ALU.subtract).then_inc(mean_steps, 1)
            V.tensor_tensor(summed, even_sq, odd_sq, ALU.add).then_inc(mean_steps, 1)
            dve.wait_ge(mean_steps, 3)
            V.tensor_scalar(mean[:], both, 0.5, None, ALU.mult).then_inc(mean_steps, 1)
            V.scalar_tensor_tensor(apart, apart, 0.25, apart, ALU.mult, ALU.mult).then_inc(mean_steps, 1)
            V.tensor_scalar(summed, summed, 1.0 / C, EPS, ALU.mult, ALU.add).then_inc(mean_steps, 1)
            dve.wait_ge(mean_steps, 6)
            V.tensor_tensor(varied, summed, apart, ALU.add).then_inc(rstd_steps, 1)

            dve.wait_ge(consts_in, 16 * len(CONST_LOADS))
            V.tensor_copy(identity_bf[:], identity[:]).then_inc(prep_done, 1)
            V.tensor_copy(mask_bf[:], mask_f[:]).then_inc(prep_done, 1)
            dve.wait_ge(prep_products, 1)
            V.tensor_copy(w_k[:], scores[0][:]).then_inc(prep_done, 1)
            pairs = scores[0][:].rearrange("p (n two) -> p n two", two=2)
            pairs_out = w_k_turned[:].rearrange("p (n two) -> p n two", two=2)
            V.tensor_scalar(pairs_out[:, :, 0:1], pairs[:, :, 1:2], -1.0, None, ALU.mult).then_inc(prep_done, 1)
            V.tensor_copy(pairs_out[:, :, 1:2], pairs[:, :, 0:1]).then_inc(prep_done, 1)
            dve.wait_ge(prep_products, 2)
            V.tensor_copy(w_q[:], scores[1][:]).then_inc(prep_done, 1)
            dve.wait_ge(prep_products, 3)
            V.tensor_copy(w_v_lat[:].rearrange("p g c -> p (g c)"), turned[0][:]).then_inc(prep_done, 1)
            dve.wait_ge(prep_products, 4)
            V.tensor_copy(w_qk_turned[:], turned[1][:, 0:P]).then_inc(prep_done, 1)
            dve.wait_ge(prep_products, 5)
            for n, (col, bias) in enumerate(((q_col, 0), (k_col, 1), (v_col, 3))):
                V.tensor_scalar(col[:], o_ps[:, G * n:G * n + G], bias_cols[:, bias:bias + 1], None, ALU.add).then_inc(prep_done, 1)
            V.memset(o_spread[:], 0.0).then_inc(prep_done, 1)
            dve.wait_ge(prep_products, 6)
            V.tensor_copy(k_col_turned[:], down_ps[:, 0:G]).then_inc(prep_done, 1)
            V.tensor_copy(w_v[:], work[0][:, 0:C]).then_inc(prep_done, 1)
            V.tensor_scalar(o_col[:], work[1][:, 0:1], bias_cols[:, 4:5], None, ALU.add).then_inc(o_col_ready, 1)
            dve.wait_ge(o_col_ready, 1)
            dve.wait_ge(prep_done, PREP_COLUMNS)
            V.tensor_scalar(o_spread[:], o_spread[:], o_col[:], None, ALU.add).then_inc(prep_done, 1)
            dve.wait_ge(prep_products, 7)
            V.tensor_tensor(out_add[:], turned[0][:, 0:C], out_bias_rows[:], ALU.add).then_inc(prep_done, 1)
            dve.wait_ge(down_in, 16 * len(CHUNKS))
            for n, (_, m) in enumerate(CHUNKS):
                part = down_w[0:m, :, n, :]
                V.tensor_scalar(part, part, 0.5, None, ALU.mult).then_inc(down_halved, 1)

            dve.wait_ge(std_done, 1)
            steps = (
                lambda: V.reciprocal(spread[:, 2, :], spread[:, 1, :]),
                lambda: V.tensor_tensor(spread[:, 3, :], spread[:, 2, :], spread[:, 2, :], ALU.mult),
                lambda: V.scalar_tensor_tensor(spread[:, 1, :], spread[:, 3, :], -0.5, spread[:, 0, :], ALU.mult, ALU.mult),
                lambda: V.scalar_tensor_tensor(rstd[:], spread[:, 1, :], 1.5, spread[:, 2, :], ALU.add, ALU.mult),
            )
            for n, step in enumerate(steps):
                step().then_inc(rstd_steps, 1)
                dve.wait_ge(rstd_steps, n + 2)

            def norm(b, par, turn):
                wait(dve, xn_turned, b - 1)
                for t in range(NT):
                    tile = bass.ds(b * NT + t, 1)
                    V.tensor_scalar(xn[:, par, t, :], x_all[:, tile, :].rearrange("p a n -> p (a n)"),
                                    mean[:, tile], rstd[:, tile],
                                    ALU.subtract, ALU.mult).then_inc(xn_ready, 1)

            def take_logits(b, par):
                wait(dve, logits_ps, b + 1)
                V.tensor_tensor(logits[:, bass.ds(b * NT, NT), :], turned[par][:, 0:NT * 8].rearrange("p (t e) -> p t e", e=8)[:, :, 0:ROUTED],
                                rb[:].unsqueeze(1).to_broadcast([P, NT, ROUTED]), ALU.add).then_inc(logits_taken, 1)

            norm(0, 0, 0)
            norm(1, 1, 0)
            with dve.Fori(0, B // 2 - 1) as pair:
                for par in range(2):
                    take_logits(pair * 2 + par, par)
                    norm(pair * 2 + par + 2, par, 0)
            for par in range(2):
                take_logits(B - 2 + par, par)

            def over(a):
                return a.unsqueeze(2).to_broadcast([P, TILES, ROUTED])

            ranks_b = rank[:].unsqueeze(1).to_broadcast([P, TILES, ROUTED])
            top = [tops[:, n, :] for n in range(8)]
            r = [rt[:, n] for n in range(4)]
            dve.wait_ge(logits_taken, B)
            chain = (
                lambda: V.tensor_reduce(top[0], logits[:], X_AXIS, ALU.max),
                lambda: V.tensor_tensor(r[0], logits[:], over(top[0]), ALU.is_equal),
                lambda: V.tensor_tensor(r[1], r[0], ranks_b, ALU.mult),
                lambda: V.tensor_reduce(top[1], r[1], X_AXIS, ALU.max),
                lambda: V.tensor_tensor(r[2], r[1], over(top[1]), ALU.is_equal),
                lambda: V.scalar_tensor_tensor(r[3], r[2], -3e38, logits[:], ALU.mult, ALU.add),
                lambda: V.tensor_reduce(top[4], r[3], X_AXIS, ALU.max),
                lambda: V.tensor_tensor(top[2], top[4], top[0], ALU.subtract),
                lambda: V.tensor_tensor(r[0], r[3], over(top[4]), ALU.is_equal),
                lambda: V.tensor_tensor(r[1], r[0], ranks_b, ALU.mult),
                lambda: V.tensor_reduce(top[5], r[1], X_AXIS, ALU.max),
                lambda: V.tensor_tensor(r[3], r[1], over(top[5]), ALU.is_equal),
                lambda: V.tensor_scalar(top[1], top[3], 1.0, None, ALU.add),
                lambda: V.reciprocal(top[6], top[1]),
                lambda: V.tensor_tensor(top[7], top[3], top[6], ALU.mult),
                lambda: V.tensor_tensor(r[0], r[2], over(top[6]), ALU.mult),
                lambda: V.tensor_tensor(r[1], r[3], over(top[7]), ALU.mult),
                lambda: V.tensor_tensor(weights[:], r[0], r[1], ALU.add),
            )
            for n, step in enumerate(chain):
                if n == 12:
                    dve.wait_ge(gap_exp, 1)
                step().then_inc(route_steps, 1)
                dve.wait_ge(route_steps, n + 1)

            def project(n, off, what, t):
                b = n.b + off
                if what == "k":
                    wait(dve, k_low_ready, b * G + t)
                    V.scalar_tensor_tensor(k_lat[:], filled(dve, what, t, b)[:], k_col[:, t:t + 1], cos_sb[:],
                                           ALU.add, ALU.mult).then_inc(k_parts, 1)
                elif what == "k_turned":
                    V.scalar_tensor_tensor(k_sin[:], filled(dve, what, t, b)[:], k_col_turned[:, t:t + 1], sin_sb[:],
                                           ALU.add, ALU.mult).then_inc(k_parts, 1)
                elif what == "q":
                    bank = filled(dve, what, t, b)
                    wait(dve, q_wqk_ps, b * G + t - 1)
                    for part, table in ((q_cos, cos_sb), (q_sin, sin_sb)):
                        V.scalar_tensor_tensor(part[:, t % 2, :], bank[:], q_col[:, t:t + 1], table[:],
                                               ALU.add, ALU.mult).then_inc(q_parts, 1)
                elif what == "q_wqk":
                    wait(dve, q_low_ready, b * G + t - 1)
                    V.tensor_scalar(q_lat[:, t % 2, :], filled(dve, what, t, b)[:], bias_cols[:, 2:3], SCALE,
                                    ALU.add, ALU.mult).then_inc(q_ready, 1)
                elif what == "v":
                    wait(dve, pv_done, (b - 1) * G * NT)
                    V.tensor_copy(values[:, n.par(off), :, 0:HD], filled(dve, what, t, b)[:].rearrange("p (n d) -> p n d", d=HD)).then_inc(values_ready, 1)

            def take_output(n, off, g):
                b = n.b + off
                o = filled(dve, "o_turned", g, b)[:].rearrange("p (t h l) -> p t h l", t=NT, h=GH)
                V.reciprocal(o_rec[:, g % 2].unsqueeze(3), o[:, :, :, SUM:SUM + 1]).then_inc(o_rec_ready, 1)
                wait(dve, o_rec_ready, b * G + g + 1)
                if g == 0:
                    wait(dve, y_ps, b)
                V.tensor_tensor(y_sb[:, :, g * GH * HD:(g + 1) * GH * HD].rearrange("p t (h d) -> p t h d", h=GH),
                                o[:, :, :, 0:HD], o_rec[:, g % 2].unsqueeze(3).to_broadcast([P, NT, GH, HD]),
                                ALU.mult).then_inc(y_parts, 1)

            def swiglu(b, k):
                m = CHUNKS[k % 3][1]
                h = hidden[0:m, k % 3, :]
                bank = filled(dve, "gate", k, b)
                wait(dve, tanh_ready, b * SLOTS + k + 1)
                V.scalar_tensor_tensor(h, h, 1.0, bank[0:m, :], ALU.add, ALU.mult).then_inc(tanh_used, 1)
                wait(dve, tanh_used, b * SLOTS + k + 1)
                V.tensor_tensor(h, h, filled(dve, "up", k, b)[0:m, :], ALU.mult).then_inc(hidden_ready, 1)

            def body(n):
                b = n.b
                if n.exists():
                    wait(dve, expert_added, b * ACC_STEPS)
                    V.tensor_copy(w_tok[:], weights[:, bass.ds(b * NT, NT), :]).then_inc(w_tok_ready, 1)
                for s in body_steps(n):
                    if n.exists():
                        w = P * ((s // GH) % NT + 1)
                        wait(dve, scores_ready, b * UNITS + s + 1)
                        V.tensor_reduce(neg_max[:, s % 8:s % 8 + 1], scores[s % 2][:, 0:w], X_AXIS, ALU.max,
                                        negate=True).then_inc(max_ready, 1)
                    off, u = n.back(s - TURN_LAG)
                    if n.exists(off) and not on_act(u):
                        take_probs(dve, V.tensor_copy, taken_dve, b + off, u)
                    for what, i, off in PLAN.get(s - 1, ()):
                        if not n.exists(off):
                            continue
                        if what == "gate":
                            swiglu(b, i)
                        elif what == "o_turned":
                            take_output(n, off, i)
                        elif what == "y":
                            wait(dve, cproj_done, b + off)
                            V.tensor_copy(y_t[:], filled(dve, "y", 0, b + off)[:]).then_inc(y_t_ready, 1)
                        elif what != "up":
                            project(n, off, what, i)
                    if s in EXPERT_TAKEN and n.exists():
                        e = EXPERT_TAKEN[s]
                        mine = acc[:, n.par()]
                        wait(dve, down_done, b * SLOTS + (e + 1) * len(CHUNKS))
                        wait(dve, expert_added, b * ACC_STEPS + e * NT)
                        if e == 0:
                            wait(dve, acc_ready, b + 1)
                            wait(dve, w_tok_ready, b + 1)
                        if e < ROUTED:
                            for t in range(NT):
                                V.scalar_tensor_tensor(mine[:, t, :], down_ps[:, t * C:(t + 1) * C], w_tok[:, t, e:e + 1],
                                                       mine[:, t, :], ALU.mult, ALU.add).then_inc(expert_added, 1)
                        else:
                            flat = mine.rearrange("p t c -> p (t c)")
                            V.tensor_tensor(flat, down_ps[:], flat, ALU.add).then_inc(expert_added, 1)
                    if s == CPROJ_STEP + 1 and n.exists(-1):
                        flat = acc[:, n.par(-1)].rearrange("p t c -> p (t c)")
                        wait(dve, cproj_done, b)
                        wait(dve, expert_added, b * ACC_STEPS)
                        V.tensor_tensor(flat, down_ps[:], flat, ALU.add).then_inc(attention_added, 1)

            first = Batch(0, 0)
            dve.wait_ge(zeroed, 2)
            for uses in PROJECT:
                for what, t, _ in uses:
                    project(first, 0, what, t)
            bodies(dve, body)

        @block.tensor
        def _(pe):
            M = nc.tensor

            pe.wait_ge(consts_in, 16 * len(CONST_LOADS))
            M.matmul(scores[0][:], attn_rows[:, 1, :], bdkv[:], start=True, stop=True).then_inc(prep_products, 1)
            M.matmul(scores[1][:], attn_rows[:, 0, :], bdq[:], start=True, stop=True).then_inc(prep_products, 1)
            for g in range(G):
                last = M.matmul(turned[0][:, g * C:(g + 1) * C], bdkv[:, g * P:(g + 1) * P], attn_rows[:, 2, :], start=True, stop=True)
            last.then_inc(prep_products, 1)
            M.matmul(turned[1][:, 0:P], rot_sb[:], bdqk[:], start=True, stop=True).then_inc(prep_products, 1)
            for n, (bd, bias) in enumerate(((bdq, 5), (bdkv, 6), (bdkv, 7))):
                for g in range(G):
                    last = M.matmul(o_ps[:, n * G + g:n * G + g + 1], bd[:, g * P:(g + 1) * P], bias_cols[:, bias:bias + 1],
                                    start=True, stop=True)
            last.then_inc(prep_products, 1)
            pe.wait_ge(prep_done, PREP_COLUMNS)
            M.matmul(down_ps[:, 0:G], rot_t_sb[:], k_col[:], start=True, stop=True)
            for g in range(G):
                M.matmul(work[0][:, 0:C], w_v_lat[:, g, :], bdo[:, g, :], start=(g == 0), stop=(g == G - 1))
            for g in range(G):
                last = M.matmul(work[1][:, 0:1], bdo[:, g, :], v_col[:, g:g + 1], start=(g == 0), stop=(g == G - 1))
            last.then_inc(prep_products, 1)
            pe.wait_ge(prep_done, PREP_SPREAD)
            M.matmul(turned[0][:, 0:C], o_spread[:], cproj_w[:], start=True, stop=True).then_inc(prep_products, 1)
            pe.wait_ge(prep_done, PREP_ALL)

            def turn_xn(b, par):
                wait(pe, xn_ready, (b + 1) * NT)
                wait(pe, xn_t_ready, b - 1)
                for t in range(NT):
                    last = M.transpose(work[par][:, t * P:(t + 1) * P], xn[:, par, t, :], identity[:])
                last.then_inc(xn_turned, 1)

            def route(b, par):
                wait(pe, xn_t_ready, b + 1)
                wait(pe, logits_taken, b - 1)
                for t in range(NT):
                    last = M.matmul(turned[par][:, t * 8:t * 8 + ROUTED], xn_t[:, par, t * P:(t + 1) * P], wr[:], start=True, stop=True)
                last.then_inc(logits_ps, 1)

            turn_xn(0, 0)
            turn_xn(1, 1)
            for b in range(2):
                route(b, b)
                turn_xn(b + 2, b)
            with pe.Fori(1, B // 2 - 1) as pair:
                for par in range(2):
                    route(pair * 2 + par, par)
                    turn_xn(pair * 2 + par + 2, par)
            for par in range(2):
                route(B - 2 + par, par)
            pe.wait_ge(xn_t_ready, B)
            pe.wait_ge(logits_taken, B)
            pe.wait_ge(weights_in, 16)
            pe.wait_ge(down_halved, len(CHUNKS))

            def bank(n, known, what, i, off):
                before = use_before(known, what, i, off)
                if before is not None:
                    w, j, o = before
                    b = n.b + o
                    s, count = {
                        "k": (k_parts, 2 * (b * G + j) + 1), "k_turned": (k_parts, 2 * (b * G + j) + 2),
                        "q": (q_parts, 2 * (b * G + j) + 2), "q_wqk": (q_ready, b * G + j + 1), "v": (values_ready, b + 1),
                        "gate": (tanh_used, b * SLOTS + j + 1), "up": (hidden_ready, b * SLOTS + j + 1),
                        "o_turned": (y_parts, b * G + j + 1), "y": (y_t_ready, b + 1)}[w]
                    wait(pe, s, count)
                return work[bank_of(what, i)]

            def project(n, known, what, i, off):
                b, xt = n.b + off, xb[:, n.par(off), :]
                cols = slice(i * P, (i + 1) * P)
                if (what, i) == PROJECT[0][0][:2]:
                    wait(pe, xb_in[n.par(off)], n.alike(off) * 16)
                out_ps = bank(n, known, what, i, off)
                if what == "k":
                    M.matmul(out_ps[:], w_k[:, cols], xt, start=True, stop=True).then_inc(k_ps, 1)
                elif what == "k_turned":
                    M.matmul(out_ps[:], w_k_turned[:, cols], xt, start=True, stop=True).then_inc(k_ps, 1)
                elif what == "q":
                    M.matmul(out_ps[:], w_q[:, cols], xt, start=True, stop=True).then_inc(q_ps, 1)
                elif what == "q_wqk":
                    wait(pe, q_parts, 2 * (b * G + i + 1))
                    M.matmul(out_ps[:], bdqk[:], q_cos[:, i % 2, :], start=True, stop=False)
                    M.matmul(out_ps[:], w_qk_turned[:], q_sin[:, i % 2, :], start=False, stop=True).then_inc(q_wqk_ps, 1)
                elif what == "v":
                    for t in range(NT):
                        last = M.matmul(out_ps[:, t * C:(t + 1) * C], xb[:, n.par(off), t * P:(t + 1) * P], w_v[:], start=True, stop=True)
                    last.then_inc(v_ps, 1)

            def score(b, u):
                quad, r = divmod(u, GH)
                g, i = divmod(quad, NT)
                half, t = divmod(g, HG)
                w = P * (i + 1)
                wait(pe, probs_ready, b * UNITS + u - 1)
                if u % HALF_UNITS == 0:
                    wait(pe, stack_in[half], (b + 1) * STACK_COPIES * 16)
                wide = max(w, 2 * P)
                M.matmul(scores[u % 2][:, 0:wide], q_stack[:, half, r, t, i * P:w], k_stack[:, half, r, t, 0:wide], start=True, stop=False)
                M.matmul(scores[u % 2][:, w - P:w], identity_bf[:], mask_bf[:], start=False, stop=True).then_inc(scores_ready, 1)

            def turn(b, u):
                wait(pe, probs_ready, b * UNITS + u + 1)
                taken(pe, b, u - 2)
                for j in range((u // GH) % NT + 1):
                    last = M.transpose(turned[u % 2][:, j * P:(j + 1) * P], probs[:, u % PROBS, j * P:(j + 1) * P], identity[:])
                last.then_inc(probs_turned, 1)

            def heads(n, off, g, i):
                b, quad = n.b + off, g * NT + i
                taken(pe, b, quad * GH)
                taken(pe, b, quad * GH + GH - 1)
                if i == 0:
                    wait(pe, o_taken, b * G + g)
                if quad == 0:
                    wait(pe, values_ready, b + 1)
                for j in range(i + 1):
                    for r in range(GH):
                        last = M.matmul(o_ps[r * LAT:(r + 1) * LAT, i * P:(i + 1) * P], values[:, n.par(off), j * H + g * GH + r, :],
                                        probs_t[:, quad % 2, r, j * P:(j + 1) * P], start=(j == 0), stop=(j == i),
                                        skip_group_check=True)
                last.then_inc(pv_done, 1)

            def gate_or_up(n, what, k):
                e, c = divmod(k, len(CHUNKS))
                first, m = CHUNKS[c]
                which, done = (0, gate_ps) if what == "gate" else (1, up_ps)
                w = gate_up_w[:, which, e * I + first:e * I + first + m]
                M.matmul(bank(n, n.known, what, k, 0)[0:m, :], w, xb[:, n.par(), :], start=True, stop=True).then_inc(done, 1)

            def down_product(b, k):
                e, c = divmod(k, len(CHUNKS))
                m = CHUNKS[c][1]
                wait(pe, hidden_ready, b * SLOTS + k + 1)
                if c == 0:
                    wait(pe, expert_added, b * ACC_STEPS + e * NT)
                    if e == CPROJ_AFTER + 1:
                        wait(pe, attention_added, b)
                for t in range(NT):
                    last = M.matmul(down_ps[:, t * C:(t + 1) * C], hidden[0:m, k % 3, t * P:(t + 1) * P], down_w[0:m, e, c, :],
                                    start=(c == 0 and t == 0), stop=(c == len(CHUNKS) - 1), skip_group_check=True)
                last.then_inc(down_done, 1)

            def body(n):
                b = n.b
                for s in body_steps(n):
                    if n.exists():
                        score(b, s)
                    if s in DOWN_AT and n.exists():
                        down_product(b, DOWN_AT[s])
                    off, u = n.back(s - TURN_LAG)
                    if n.exists(off):
                        turn(b + off, u)
                    if s == CPROJ_STEP and n.exists(-1):
                        wait(pe, y_t_ready, b)
                        if n.exists():
                            wait(pe, expert_added, b * ACC_STEPS + (CPROJ_AFTER + 1) * NT)
                        else:
                            wait(pe, expert_added, b * ACC_STEPS)
                        for t in range(NT):
                            last = M.matmul(down_ps[:, t * C:(t + 1) * C], y_t[:, t * P:(t + 1) * P], cproj_w[:],
                                            start=True, stop=True, skip_group_check=True)
                        last.then_inc(cproj_done, 1)
                    h = heads_at(s)
                    if h is not None and n.exists(h[0]):
                        heads(n, *h)
                    for what, i, off in PLAN.get(s, ()):
                        if not n.exists(off):
                            continue
                        if what in ("gate", "up"):
                            gate_or_up(n, what, i)
                        elif what == "o_turned":
                            wait(pe, o_taken, (b + off) * G + i + 1)
                            out_ps = bank(n, n.known, what, i, off)
                            for t in range(NT):
                                last = M.transpose(out_ps[:, t * P:(t + 1) * P], o_sb[:, i % 2, t * P:(t + 1) * P], identity[:])
                            last.then_inc(o_turned_ps, 1)
                        elif what == "y":
                            wait(pe, y_parts, (b + off + 1) * G)
                            out_ps = bank(n, n.known, what, i, off)
                            for t in range(NT):
                                last = M.transpose(out_ps[:, t * P:(t + 1) * P], y_sb[:, t, :], identity[:])
                            last.then_inc(y_ps, 1)
                        else:
                            project(n, n.known, what, i, off)

            for uses in PROJECT:
                for what, t, _ in uses:
                    project(Batch(0, 0), "first", what, t, 0)
            bodies(pe, body)


def _blocks(a, n):
    out = np.zeros((a.shape[0] * n, a.shape[1] * n), a.dtype)
    for i in range(n):
        out[i * a.shape[0]:(i + 1) * a.shape[0], i * a.shape[1]:(i + 1) * a.shape[1]] = a
    return out


def _column(a, n):
    return np.tile(np.asarray(a), n).reshape(-1, 1)


def _tables():
    inv = (np.float32(1) / np.power(np.float32(10000), np.arange(0, LAT, 2, dtype=np.float32) / np.float32(LAT))).astype(np.float32)
    angles = np.repeat(np.outer(np.arange(T, dtype=np.float32), inv), 2, axis=1).T
    rot = np.zeros((P, P), np.float32)
    for i in range(0, P, 2):
        rot[i, i + 1], rot[i + 1, i] = -1, 1
    mask = np.where(np.tril(np.ones((P, P), bool)), 0, MASKED).astype(np.float32)
    ranks = np.arange(ROUTED, 0, -1, dtype=np.float32).reshape(1, ROUTED)
    return {"ident": np.eye(P, dtype=np.float32), "mask": mask, "rot": rot, "rot_t": np.ascontiguousarray(rot.T),
            "cos": np.tile(np.cos(angles), (GH, 1)), "sin": np.tile(np.sin(angles), (GH, 1)), "ranks": ranks}


def kernel(**inputs):
    import concourse.bacc as bacc
    from concourse.bass_utils import run_bass_kernel_spmd

    a = {n.removeprefix("L0_"): np.asarray(v) for n, v in inputs.items()}
    attn_b = a["attn_c_attn_b"].reshape(3, C, 1)
    arrays = {
        "x": a["attn_x"],
        "gate_up": np.stack([np.concatenate([a[r], a[s][None]]).reshape(E * I, C).T for r, s in (("ffn_rg", "ffn_sg"), ("ffn_ru", "ffn_su"))]),
        "down": np.concatenate([a["ffn_rd"], a["ffn_sd"][None]]).transpose(0, 2, 1),
        "attn_w": a["attn_c_attn_w"].reshape(3, C, C),
        "bd_q": _blocks(a["attn_q2l_w"].T, H),
        "bd_kv": _blocks(a["attn_kv2l_w"].T, H),
        "bd_qk": _blocks(a["attn_wqk_w"].T, GH),
        "bd_o": _blocks(a["attn_l2o_w"].T, H).reshape(G, P, H * HD).reshape(G * P, C),
        "cproj": a["attn_cproj_w"].T,
        "biases": np.concatenate([_column(a["attn_q2l_b"], GH), _column(a["attn_kv2l_b"], GH), _column(a["attn_wqk_b"], GH),
                                  _column(a["attn_kv2l_b"], GH), _column(a["attn_l2o_b"], H), *attn_b], axis=1),
        "out_bias": a["attn_cproj_b"].reshape(1, C),
        "router_w": a["ffn_wr"].T,
        "router_b": a["ffn_rb"].reshape(1, ROUTED),
        **_tables(),
    }
    arrays = {n: np.ascontiguousarray(v) for n, v in arrays.items()}
    nc = bacc.Bacc("TRN2", target_bir_lowering=False, num_devices=1)
    aps = {n: nc.dram_tensor(f"in_{n}", v.shape, mybir.dt.from_np(v.dtype), kind="ExternalInput").ap() for n, v in arrays.items()}
    out = nc.dram_tensor("out", (B, T, C), F32, kind="ExternalOutput").ap()
    build(nc, out=out, **aps)
    r = run_bass_kernel_spmd(nc, [{f"in_{n}": v for n, v in arrays.items()}], core_ids=[0])
    return r.results[0]["out"]
```

```python
from contextlib import ExitStack

import numpy as np

import concourse.bass as bass
from concourse import mybir

F32 = mybir.dt.float32
F32R = mybir.dt.float32r
U32 = mybir.dt.uint32
I32 = mybir.dt.int32
BF16 = mybir.dt.bfloat16
ALU = mybir.AluOpType
ACT = mybir.ActivationFunctionType
X_AXIS = mybir.AxisListType.X

P = 128
B, T, C = 16, 512, 128
NT = T // P
H, HD, LAT = 16, 8, 32
GH = P // LAT
G = H // GH
LT = H * LAT
ROUTED, I = 7, 352
E = ROUTED + 1
CHUNKS = [(0, 128), (128, 128), (256, I - 256)]
EPS = 1e-5
SCALE = float(LAT) ** -0.5
MASKED = -1e30
SUM = HD

UNITS = G * NT * GH
HALF_UNITS = UNITS // 2
HG = G // 2
TILES = B * NT
EXPERT_TILES = 2 * TILES + ROUTED - 1
RING = 4
LAGS = 3
TURN_LAG = 2
PROBS = 4
COMBINE_STEP = 20


def step_plan():
    plan = {5: [("o_turned", G - 1, -1)], 8: [("y", 0, -1)]}
    for g in range(G - 1):
        plan[GH * NT * (g + 1) + 5] = [("o_turned", g, 0)]
    project = []
    for half in range(2):
        pair = (HG * half, HG * half + 1)
        keys = [[("k", t, 1), ("k_turned", t, 1)] for t in pair]
        queries, queries_wqk = [("q", t, 1) for t in pair], [("q_wqk", t, 1) for t in pair]
        project += [keys[0], queries, keys[1], queries_wqk] + ([[("v", 0, 1)]] if half == 0 else [])
    first, last = 3, 57
    for n, uses in enumerate(project):
        plan[first + (last - first) * n // (len(project) - 1)] = uses
    return dict(sorted(plan.items())), project


PLAN, PROJECT = step_plan()
BANK = {"k": 0, "k_turned": 1, "v": 1, "y": 0}


def bank_of(what, i):
    return BANK[what] if what in BANK else i % 2


BODY_USES = [use for uses in PLAN.values() for use in uses]
FIRST_USES = [(what, i, 0) for uses in PROJECT for what, i, _ in uses]


def use_before(b, what, i, off):
    bank = bank_of(what, i)
    if b == "first":
        uses, at, body = FIRST_USES, FIRST_USES.index((what, i, off)), "first"
    else:
        uses, at, body = BODY_USES, BODY_USES.index((what, i, off)), 0
    while True:
        at -= 1
        if at < 0:
            if body == "first":
                return None
            body -= 1
            if b is not None and b + body < 0:
                uses, body = FIRST_USES, "first"
            at = len(uses) - 1
        w, n, o = uses[at]
        if bank_of(w, n) != bank:
            continue
        if body == "first":
            return w, n, (0 if b == "first" else -b)
        owner = body + o
        if b is not None and not 0 <= b + owner < B:
            continue
        return w, n, owner


CPROJ_STEP = 10
SPLIT_LAG = 3
ROUTE_STEPS = 15
GAP_STEP = 8
TAIL = CPROJ_STEP + 2


def on_act(u):
    return u % GH != 0


ACT_TAKES = [u for u in range(UNITS) if on_act(u)]
DVE_TAKES = [u for u in range(UNITS) if not on_act(u)]


class Batch:

    def __init__(self, pair, c):
        self.b, self.pair, self.c = pair * 2 + c, pair, c
        self.known = self.b if isinstance(self.b, int) else None

    def par(self, off=0):
        return (self.c + off) % 2

    def alike(self, off=0):
        return self.pair + (self.c + off) // 2 + 1

    def exists(self, off=0):
        return self.known is None or 0 <= self.known + off < B

    def back(self, step):
        return (0, step) if step >= 0 else (-1, step + UNITS)


def heads_at(step):
    q, r = divmod(step - (GH - 1) - TURN_LAG - 2, GH)
    if r:
        return None
    off, q = (0, q) if q >= 0 else (-1, q + G * NT)
    return (off, *divmod(q, NT))


def group_end(step):
    h = heads_at(step)
    return (h[0], h[1]) if h and h[2] == NT - 1 else None


def build(nc, x, gate_up, down, attn_w, bd_q, bd_kv, bd_qk, bd_o, cproj, biases, out_bias, router_w, router_b, ranks,
          ident, mask, rot, rot_t, cos, sin, before, token_no, tile_no, tile_start, out):
    xn_dram = nc.dram_tensor("normed_transposed", (B, P, T), F32, kind="Internal").ap()
    x_tiles = x.rearrange("b (t p) c -> p (b t) c", p=P)
    out_tiles = out.rearrange("b (t p) c -> b p t c", p=P)
    normed = nc.dram_tensor("normed", (TILES * P, C), F32, kind="Internal").ap()
    normed_by_batch = normed.rearrange("(b t p) c -> b p t c", p=P, t=NT)
    partial = nc.dram_tensor("partial", (B, P, NT * C), F32, kind="Internal").ap()
    sorted_tokens = nc.dram_tensor("sorted_tokens", (EXPERT_TILES * P, 1), F32, kind="Internal").ap()
    expert_out = nc.dram_tensor("expert_out", (EXPERT_TILES * P, C), F32, kind="Internal").ap()

    with ExitStack() as ctx:
        def sb(name, shape, dt=F32):
            return ctx.enter_context(nc.sbuf_tensor(name, shape, dt))

        def psum(name, shape=(P, 512)):
            return ctx.enter_context(nc.psum_tensor(name, list(shape), F32))

        def sem(name):
            return ctx.enter_context(nc.semaphore(name))

        with ExitStack() as ahead:
            def early(name, shape, dt=F32):
                return ahead.enter_context(nc.sbuf_tensor(name, shape, dt))

            x_all = early("x_all", [P, TILES, C])
            attn_rows = early("attn_rows", [P, 3, C])
            bdq = early("bdq", [P, LT])
            bdkv = early("bdkv", [P, LT])
            bdo = early("bdo", [P, G, C])
            out_bias_rows = early("out_bias_rows", [P, C])
            mask_f = early("mask_f", [P, P])
            rot_sb = early("rot_sb", [P, P])
            rot_t_sb = early("rot_t_sb", [P, P])
            w_v_lat = early("w_v_lat", [P, G, C])
            o_spread = early("o_spread", [P, P])
            stats = early("stats", [P, TILES, 6])
            mean = early("mean", [P, TILES])
            spread = early("spread", [P, 4, TILES])
            rstd = early("rstd", [P, TILES])
            xn = early("xn", [P, 2, NT, C])
            xn_t = early("xn_t", [P, 2, T])
            logits = early("logits", [P, TILES, ROUTED])
            rt = early("rt", [P, 4, TILES, ROUTED])
            tops = early("tops", [P, 8, TILES])
            wr = early("wr", [P, ROUTED])
            rb = early("rb", [P, ROUTED])
            rank = early("rank", [P, ROUTED])
            gate_up_w = early("gate_up_w", [P, 2, E * I])
            down_w = early("down_w", [P, E, len(CHUNKS), C])
            earlier = early("earlier", [P, P])
            ones = early("ones", [P, P])
            tokens = early("tokens", [P, TILES])
            tile_numbers = early("tile_numbers", [1, EXPERT_TILES])
            tile_starts = early("tile_starts", [P, TILES])
            sums = early("sums", [P, 2, TILES, ROUTED])
            places = early("places", [P, TILES, ROUTED])
            starts = early("starts", [P, 5, ROUTED])
            of_tile = early("of_tile", [1, EXPERT_TILES, ROUTED])
            of_tile_sum = early("of_tile_sum", [1, EXPERT_TILES])
            tile_expert = early("tile_expert", [1, EXPERT_TILES], I32)
            place_cols = early("place_cols", [P, RING, 2], U32)
            token_col = early("token_col", [P, RING])
            zero_tokens = early("zero_tokens", [P, EXPERT_TILES])
            token_rows = early("token_rows", [P, 2, P])
            token_of = early("token_of", [P, EXPERT_TILES], U32)
            hidden = early("hidden", [P, 3, T])
            gather_col = early("gather_col", [P, RING], U32)
            gathered = early("gathered", [P, RING, C])
            gathered_t = early("gathered_t", [P, 2, P])
            tile_hidden = early("tile_hidden", [P, 2, len(CHUNKS) * P])
            tile_hidden_t = early("tile_hidden_t", [P, 2, len(CHUNKS), P])
            tile_out = early("tile_out", [P, 2, C])
        q_stack = sb("q_stack", [P, 2, GH, HG, T], F32R)
        k_stack = sb("k_stack", [P, 2, GH, HG, T], F32R)
        k_high = sb("k_high", [P, G, T], F32R)
        k_low = sb("k_low", [P, G, T], F32R)
        q_high = sb("q_high", [P, G, T], F32R)
        q_low = sb("q_low", [P, G, T], F32R)
        probs = sb("probs", [P, PROBS, T])
        probs_t = sb("probs_t", [P, 2, GH, T])
        q_cos = sb("q_cos", [P, 2, T])
        q_sin = sb("q_sin", [P, 2, T])
        q_lat = sb("q_lat", [P, 2, T])
        o_sb = sb("o_sb", [P, 2, T])
        bdqk = sb("bdqk", [P, P])
        cproj_w = sb("cproj_w", [P, C])
        bias_cols = sb("bias_cols", [P, 8])
        identity = sb("identity", [P, P])
        identity_bf = sb("identity_bf", [P, P], BF16)
        mask_bf = sb("mask_bf", [P, P], BF16)
        cos_sb = sb("cos_sb", [P, T])
        sin_sb = sb("sin_sb", [P, T])
        w_q = sb("w_q", [P, LT])
        w_k = sb("w_k", [P, LT])
        w_k_turned = sb("w_k_turned", [P, LT])
        w_qk_turned = sb("w_qk_turned", [P, P])
        w_v = sb("w_v", [P, C])
        q_col = sb("q_col", [P, G])
        k_col = sb("k_col", [P, G])
        k_col_turned = sb("k_col_turned", [P, G])
        v_col = sb("v_col", [P, G])
        o_col = sb("o_col", [P, 1])
        out_add = sb("out_add", [P, C])
        pair_weight = sb("pair_weight", [P, 2, TILES])
        place = sb("place", [P, 2, TILES], U32)
        carrier = sb("carrier", [1, 2])
        xb = sb("xb", [P, 2, T])
        acc = sb("acc", [P, 2, NT, C])
        weight_now = sb("weight_now", [P, 2, NT])
        place_now = sb("place_now", [P, 2, NT], U32)
        picked = sb("picked", [P, 2, NT, C])
        k_lat = sb("k_lat", [P, T])
        k_sin = sb("k_sin", [P, T])
        values = sb("values", [P, 2, NT * H, LAT])
        neg_max = sb("neg_max", [P, 8])
        o_rec = sb("o_rec", [P, 2, NT, GH])
        y_sb = sb("y_sb", [P, NT, C])
        y_t = sb("y_t", [P, T])

        scores = [psum(f"scores{i}") for i in range(2)]
        turned = [psum(f"turned{i}") for i in range(2)]
        work = [psum(f"work{i}") for i in range(2)]
        o_ps = psum("o_ps")
        down_ps = psum("down_ps")

        consts_in = sem("consts_in")
        weights_in = sem("weights_in")
        down_in = sem("down_in")
        down_halved = sem("down_halved")
        o_col_ready = sem("o_col_ready")
        x_in = [sem(f"x_in{i}") for i in range(4)]
        zeroed = sem("zeroed")
        prep_products = sem("prep_products")
        prep_done = sem("prep_done")
        stats_done = sem("stats_done")
        mean_steps = sem("mean_steps")
        std_done = sem("std_done")
        rstd_steps = sem("rstd_steps")
        xn_ready = sem("xn_ready")
        xn_turned = sem("xn_turned")
        xn_t_ready = sem("xn_t_ready")
        xn_stored = [sem(f"xn_stored{i}") for i in range(2)]
        logits_ps = sem("logits_ps")
        logits_taken = sem("logits_taken")
        route_steps = sem("route_steps")
        gap_ready = sem("gap_ready")
        gap_exp = sem("gap_exp")
        xb_in = [sem(f"xb_in{i}") for i in range(2)]
        acc_in = [sem(f"acc_in{i}") for i in range(2)]
        expert_added = sem("expert_added")
        attention_added = sem("attention_added")
        stored = [sem(f"stored{i}") for i in range(2)]
        k_ps = sem("k_ps")
        q_ps = sem("q_ps")
        q_wqk_ps = sem("q_wqk_ps")
        v_ps = sem("v_ps")
        gate_ps = sem("gate_ps")
        up_ps = sem("up_ps")
        o_turned_ps = sem("o_turned_ps")
        y_ps = sem("y_ps")
        k_parts = sem("k_parts")
        k_ready = sem("k_ready")
        k_high_ready = sem("k_high_ready")
        k_low_ready = sem("k_low_ready")
        q_parts = sem("q_parts")
        q_ready = sem("q_ready")
        q_high_ready = sem("q_high_ready")
        q_low_ready = sem("q_low_ready")
        stack_in = [sem(f"stack_in{i}") for i in range(2)]
        values_ready = sem("values_ready")
        now_ready = sem("now_ready")
        weight_ready = sem("weight_ready")
        picked_in = sem("picked_in")
        rows_stored = [sem(f"rows_stored{i}") for i in range(2)]
        tokens_zeroed = sem("tokens_zeroed")
        mask_ready = sem("mask_ready")
        weight_steps = sem("weight_steps")
        counted_ps = sem("counted_ps")
        sort_steps = sem("sort_steps")
        place_copied = sem("place_copied")
        carried = sem("carried")
        scattered = [sem(f"scattered{i}") for i in range(RING)]
        token_rows_in = sem("token_rows_in")
        tokens_turned = sem("tokens_turned")
        token_of_ready = sem("token_of_ready")
        shared_added = sem("shared_added")
        residual_added = sem("residual_added")
        partial_stored = [sem(f"partial_stored{i}") for i in range(2)]
        gather_col_ready = sem("gather_col_ready")
        tile_in = [sem(f"tile_in{i}") for i in range(RING)]
        tile_turned = sem("tile_turned")
        gathered_t_ready = sem("gathered_t_ready")
        tile_gate_ps = sem("tile_gate_ps")
        tile_up_ps = sem("tile_up_ps")
        tile_tanh = sem("tile_tanh")
        tile_gated = sem("tile_gated")
        tile_hidden_ready = sem("tile_hidden_ready")
        tile_hidden_turned = sem("tile_hidden_turned")
        tile_hidden_t_ready = sem("tile_hidden_t_ready")
        tile_down = sem("tile_down")
        tile_out_ready = sem("tile_out_ready")
        tile_stored = [sem(f"tile_stored{i}") for i in range(2)]
        scores_ready = sem("scores_ready")
        max_ready = sem("max_ready")
        probs_ready = sem("probs_ready")
        probs_turned = sem("probs_turned")
        taken_act = sem("taken_act")
        taken_dve = sem("taken_dve")
        pv_done = sem("pv_done")
        o_taken = sem("o_taken")
        o_rec_ready = sem("o_rec_ready")
        y_parts = sem("y_parts")
        y_t_ready = sem("y_t_ready")
        cproj_done = sem("cproj_done")
        tanh_ready = sem("tanh_ready")
        tanh_used = sem("tanh_used")
        hidden_ready = sem("hidden_ready")
        down_done = sem("down_done")
        block = ctx.enter_context(nc.Block())

        def wait(eng, s, value):
            if not isinstance(value, int) or value > 0:
                eng.wait_ge(s, value)

        def stages(engine, step):
            for i in range(2 * RING):
                step(i, i % RING, i // RING)
            with engine.Fori(2, EXPERT_TILES // RING) as turn:
                for c in range(RING):
                    step(turn * RING + c, c, turn)
            for i in range(EXPERT_TILES // RING * RING, EXPERT_TILES + LAGS):
                step(i, i % RING, i // RING)

        def lagging(i, ring, turn, lag):
            if isinstance(i, int):
                return (i - lag, (i - lag) % RING, (i - lag) // RING) if 0 <= i - lag < EXPERT_TILES else None
            return i - lag, (ring - lag) % RING, turn + (ring - lag) // RING

        def experts_done(eng):
            for par in range(2):
                wait(eng, tile_stored[par], 16 * (EXPERT_TILES // 2))

        def batches(engine, batch):
            for b in range(2):
                batch(b, b, 0)
            with engine.Fori(1, B // 2) as pair:
                for par in range(2):
                    batch(pair * 2 + par, par, pair)

        def bodies(engine, body):
            body(Batch(0, 0))
            with engine.Fori(0, B // 2 - 1) as pair:
                for c in (1, 2):
                    body(Batch(pair, c))
            body(Batch(0, B - 1))
            body(Batch(0, B))

        def body_steps(n):
            return range(TAIL if n.known == B else UNITS)

        def taken(eng, b, u):
            if u < 0:
                b, u = b - 1, u + UNITS
            if on_act(u):
                wait(eng, taken_act, b * len(ACT_TAKES) + ACT_TAKES.index(u) + 1)
            else:
                wait(eng, taken_dve, b * len(DVE_TAKES) + DVE_TAKES.index(u) + 1)

        def take_probs(eng, copy, done, b, u):
            quad = u // GH
            n = P * (quad % NT + 1)
            wait(eng, probs_turned, b * UNITS + u + 1)
            wait(eng, pv_done, b * G * NT + quad - 1)
            copy(probs_t[:, quad % 2, u % GH, 0:n], turned[u % 2][:, 0:n]).then_inc(done, 1)

        def filled(eng, what, i, b):
            s, count = {
                "k": (k_ps, 2 * (b * G + i) + 1), "k_turned": (k_ps, 2 * (b * G + i) + 2), "q": (q_ps, b * G + i + 1),
                "q_wqk": (q_wqk_ps, b * G + i + 1), "v": (v_ps, b + 1), "o_turned": (o_turned_ps, b * G + i + 1), "y": (y_ps, b + 1)}[what]
            wait(eng, s, count)
            return work[bank_of(what, i)]

        def stacks_copied(eng, b, t):
            wait(eng, stack_in[t // HG], b * STACK_COPIES * 16)

        STACK_COPIES = 2 * GH * 4

        CONST_LOADS = (
            (attn_rows[:], attn_w.rearrange("a p c -> p a c")), (bdq[:], bd_q), (bdkv[:], bd_kv), (bdqk[:], bd_qk),
            (bdo[:], bd_o.rearrange("(g p) c -> p g c", p=P)), (cproj_w[:], cproj), (bias_cols[:], biases),
            (out_bias_rows[:], out_bias.to_broadcast([P, C])), (wr[:], router_w), (rb[:], router_b.to_broadcast([P, ROUTED])),
            (rank[:], ranks.to_broadcast([P, ROUTED])), (identity[:], ident), (mask_f[:], mask),
            (rot_sb[:], rot), (rot_t_sb[:], rot_t), (cos_sb[:], cos), (sin_sb[:], sin),
            (earlier[:], before), (tokens[:], token_no), (tile_numbers[:], tile_no), (tile_starts[:], tile_start.to_broadcast([P, TILES])),
        )
        PREP_COLUMNS = 12
        PREP_SPREAD = 15
        PREP_ALL = 16

        @block.sync
        def _(sp):
            n = TILES // len(x_in)
            for c, loaded in enumerate(x_in):
                sp.dma_start(x_all[:, c * n:(c + 1) * n, :], x_tiles[:, c * n:(c + 1) * n, :]).then_inc(loaded, 16)
            for dst, src in CONST_LOADS:
                sp.dma_start(dst, src).then_inc(consts_in, 16)
            sp.dma_start(gate_up_w[:], gate_up.rearrange("a p n -> p a n")).then_inc(weights_in, 16)
            for n, (first, m) in enumerate(CHUNKS):
                sp.dma_start(down_w[0:m, :, n, :], down[:, first:first + m, :].rearrange("e p c -> p e c")).then_inc(down_in, 16)

            def store_xn(b, par, turn):
                rows = normed_by_batch[bass.ds(b, 1)].rearrange("a p t c -> p (a t) c")
                wait(sp, xn_ready, (b + 1) * NT)
                sp.dma_start(rows, xn[:, par]).then_inc(rows_stored[par], 16)
                wait(sp, xn_t_ready, b + 1)
                sp.dma_start(xn_dram[bass.ds(b, 1)].rearrange("a p n -> p (a n)"), xn_t[:, par, :]).then_inc(xn_stored[par], 16)

            sp.wait_ge(tokens_zeroed, 1)
            sp.dma_start(sorted_tokens.rearrange("(p n) a -> p (n a)", p=P), zero_tokens[:]).then_inc(tokens_zeroed, 16)
            batches(sp, store_xn)
            for par in range(2):
                sp.wait_ge(xn_stored[par], 16 * (B // 2))
                sp.wait_ge(rows_stored[par], 16 * (B // 2))

            def load_shared(b, par, turn):
                src = xn_dram[bass.ds(b, 1)].rearrange("a p n -> p (a n)")
                wait(sp, up_ps, (b - 1) * len(CHUNKS))
                sp.dma_start(xb[:, par, :], src).then_inc(xb_in[par], 16)

            def store_partial(b, par, turn):
                dst = partial[bass.ds(b, 1)].rearrange("a p n -> p (a n)")
                wait(sp, residual_added, b + 1)
                sp.dma_start(dst, acc[:, par].rearrange("p t c -> p (t c)")).then_inc(partial_stored[par], 16)

            load_shared(0, 0, 0)
            load_shared(1, 1, 0)
            with sp.Fori(0, B // 2 - 1) as pair:
                for par in range(2):
                    store_partial(pair * 2 + par, par, pair)
                    load_shared(pair * 2 + par + 2, par, pair + 1)
            for par in range(2):
                store_partial(B - 2 + par, par, B // 2 - 1)

            for done in scattered:
                sp.wait_ge(done, 2 * 16 * (TILES // RING))
            by_tile = sorted_tokens.rearrange("(n p) a -> n (p a)", p=P)
            sp.dma_start(token_rows[:, 0, :], by_tile[0:P]).then_inc(token_rows_in, 16)
            sp.dma_start(token_rows[0:EXPERT_TILES - P, 1, :], by_tile[P:EXPERT_TILES]).then_inc(token_rows_in, 16)

            def store_tile(i, ring, turn):
                mine = lagging(i, ring, turn, LAGS)
                if mine:
                    i, ring, turn = mine
                    dst = expert_out[bass.ds(i * P, P)]
                    wait(sp, tile_out_ready, i + 1)
                    sp.dma_start(dst, tile_out[:, ring % 2, :]).then_inc(tile_stored[ring % 2], 16)

            stages(sp, store_tile)
            experts_done(sp)
            for par in range(2):
                sp.wait_ge(partial_stored[par], 16 * (B // 2))

            def load_xb(n, off):
                src = xn_dram[bass.ds(n.b + off, 1)].rearrange("a p n -> p (a n)")
                wait(sp, k_ps, 2 * (n.b + off - 1) * G)
                sp.dma_start(xb[:, n.par(off), :], src).then_inc(xb_in[n.par(off)], 16)

            def load_acc(n, off):
                src = partial[bass.ds(n.b + off, 1)].rearrange("a p n -> p (a n)")
                if off and n.exists(off - 2):
                    wait(sp, stored[n.par(off)], n.alike(off - 2) * 16)
                sp.dma_start(acc[:, n.par(off)].rearrange("p t c -> p (t c)"), src).then_inc(acc_in[n.par(off)], 16)

            counts = [nc.sync.alloc_register(f"count{i}") for i in range(4)]

            def counted(value, reg):
                if isinstance(value, int):
                    return value
                nc.sync.reg_mov(counts[reg], value)
                return nc.sync.snap(counts[reg])

            def copy_stacks(half, read, split):
                wait(sp, scores_ready, read)
                wait(sp, k_low_ready, split)
                wait(sp, q_low_ready, split)
                for stack, parts in ((q_stack, (q_high, q_high, q_low, q_low)), (k_stack, (k_high, k_low, k_high, k_low))):
                    for r in range(GH):
                        for n, part in enumerate(parts):
                            sp.dma_start(stack[n * LAT:(n + 1) * LAT, half, r].bitcast(F32),
                                         part[r * LAT:(r + 1) * LAT, half * HG:(half + 1) * HG].bitcast(F32)).then_inc(stack_in[half], 16)

            def store_out(n, off):
                dst = out_tiles[bass.ds(n.b + off, 1)].rearrange("a p t c -> p (a t) c")
                wait(sp, attention_added, n.b + off + 1)
                sp.dma_start(dst, acc[:, n.par(off)]).then_inc(stored[n.par(off)], 16)

            def body(n):
                b = n.b
                read_low = counted(b * UNITS, 0)
                split_low = counted((b + 1) * G, 1)
                read_high = counted(b * UNITS + HALF_UNITS, 2)
                split_high = counted((b + 1) * G + HG, 3)
                if n.exists(1):
                    load_xb(n, 1)
                if n.exists():
                    copy_stacks(1, read_low, split_low)
                if n.exists(-1):
                    store_out(n, -1)
                if n.exists(1):
                    load_acc(n, 1)
                    copy_stacks(0, read_high, split_high)

            first = Batch(0, 0)
            load_xb(first, 0)
            load_acc(first, 0)
            copy_stacks(0, 0, HG)
            bodies(sp, body)
            for par in range(2):
                sp.wait_ge(stored[par], 16 * (B // 2))

        @block.gpsimd
        def _(pool):
            pool.memset(values[:], 0.0).then_inc(zeroed, 1)
            pool.wait_ge(zeroed, 1)
            pool.memset(values[:, :, :, SUM:SUM + 1], 1.0).then_inc(zeroed, 1)
            pool.memset(zero_tokens[:], 0.0).then_inc(tokens_zeroed, 1)
            pool.memset(carrier[:], 0.0).then_inc(carried, 1)
            pool.memset(tile_hidden[:], 0.0).then_inc(zeroed, 1)

            def carry(count, *waits):
                wait(pool, carried, count + 1)
                for s, value in waits:
                    wait(pool, s, value)
                pool.tensor_tensor(carrier[:, 0:1], carrier[:, 0:1], carrier[:, 1:2], ALU.add).then_inc(carried, 1)

            pool.wait_ge(tokens_zeroed, 1 + 16)

            def scatter(t, ring, turn):
                carry(t, (place_copied, 2 * t + 2))
                for choice in range(2):
                    pool.indirect_dma_start(sorted_tokens, bass.IndirectOffsetOnAxis(ap=place_cols[:, ring, choice:choice + 1], axis=0),
                                            token_col[:, ring:ring + 1], None).then_inc(scattered[ring], 16)

            with pool.Fori(0, TILES // RING) as turn:
                for ring in range(RING):
                    scatter(turn * RING + ring, ring, turn)

            for par in range(2):
                pool.wait_ge(rows_stored[par], 16 * (B // 2))

            def gather(i, ring, turn):
                if isinstance(i, int) and i >= EXPERT_TILES:
                    return
                carry(i + TILES, (gather_col_ready, i + 1), (tile_turned, i - RING + 1))
                pool.indirect_dma_start(gathered[:, ring, :], None, normed,
                                        bass.IndirectOffsetOnAxis(ap=gather_col[:, ring:ring + 1], axis=0)).then_inc(tile_in[ring], 16)

            stages(pool, gather)
            experts_done(pool)

            def pick(n):
                carry(n.b + TILES + EXPERT_TILES, (now_ready, n.b + 1), (expert_added, n.b * 2 * NT))
                for choice in range(2):
                    for t in range(NT):
                        pool.indirect_dma_start(picked[:, choice, t, :], None, expert_out,
                                                bass.IndirectOffsetOnAxis(ap=place_now[:, choice, t:t + 1], axis=0)).then_inc(picked_in, 16)

            def key_tile(b, t):
                wait(pool, k_parts, 2 * (b * G + t + 1))
                pool.tensor_tensor(k_lat[:], k_lat[:], k_sin[:], ALU.add).then_inc(k_ready, 1)
                wait(pool, k_high_ready, b * G + t + 1)
                pool.tensor_tensor(k_low[:, t, :], k_lat[:], k_high[:, t, :].bitcast(F32), ALU.subtract).then_inc(k_low_ready, 1)

            def query_tile(b, t):
                wait(pool, q_high_ready, b * G + t + 1)
                pool.tensor_tensor(q_low[:, t, :], q_lat[:, t % 2, :], q_high[:, t, :].bitcast(F32), ALU.subtract).then_inc(q_low_ready, 1)

            def split(b):
                for uses in PROJECT:
                    what = uses[0][0]
                    for _, t, _ in uses:
                        if what == "q_wqk":
                            query_tile(b, t)
                    if what == "k":
                        key_tile(b, uses[0][1])

            def body(n):
                if n.exists():
                    pick(n)
                if n.exists(1):
                    split(n.b + 1)

            split(0)
            bodies(pool, body)

        @block.scalar
        def _(act):
            A = nc.scalar
            act.wait_ge(rstd_steps, 1)
            A.activation(spread[:, 1, :], spread[:, 0, :], ACT.Sqrt).then_inc(std_done, 1)

            def take_xn(b, par, turn):
                wait(act, xn_turned, b + 1)
                wait(act, logits_ps, b - 1)
                wait(act, xn_stored[par], turn * 16)
                A.copy(xn_t[:, par, :], work[par][:]).then_inc(xn_t_ready, 1)

            batches(act, take_xn)
            act.wait_ge(route_steps, GAP_STEP)
            A.activation(tops[:, 3, :], tops[:, 2, :], ACT.Exp).then_inc(gap_exp, 1)

            def shared(b, par, turn):
                for k, (_, m) in enumerate(CHUNKS):
                    n = b * len(CHUNKS) + k
                    wait(act, gate_ps, n + 1)
                    wait(act, down_done, n - 2)
                    A.activation(hidden[0:m, k, :], scores[(par * len(CHUNKS) + k) % 2][0:m, :], ACT.Tanh,
                                 scale=0.5).then_inc(tanh_ready, 1)

            batches(act, shared)

            act.wait_ge(zeroed, 3)

            def tile_stages(i, ring, turn):
                mine = lagging(i, ring, turn, 0)
                if mine:
                    j, c, _ = mine
                    wait(act, tile_turned, j + 1)
                    wait(act, tile_up_ps, j - 1)
                    A.copy(gathered_t[:, c % 2, :], turned[c % 2][:, 0:P]).then_inc(gathered_t_ready, 1)
                mine = lagging(i, ring, turn, 1)
                if mine:
                    j, c, _ = mine
                    wait(act, tile_gate_ps, j + 1)
                    wait(act, tile_hidden_turned, j - 1)
                    A.activation(tile_hidden[:, c % 2, 0:I], scores[c % 2][:, 0:I], ACT.Tanh, scale=0.5).then_inc(tile_tanh, 1)
                mine = lagging(i, ring, turn, 2)
                if mine:
                    j, c, _ = mine
                    wait(act, tile_hidden_turned, j + 1)
                    wait(act, tile_down, j - 1)
                    A.copy(tile_hidden_t[:, c % 2].rearrange("p n t -> p (n t)"), o_ps[:, 0:len(CHUNKS) * P]).then_inc(tile_hidden_t_ready, 1)
                mine = lagging(i, ring, turn, 3)
                if mine:
                    j, c, turn = mine
                    wait(act, tile_down, j + 1)
                    wait(act, tile_stored[c % 2], (turn * (RING // 2) + c // 2) * 16)
                    A.copy(tile_out[:, c % 2, :], down_ps[:, 0:C]).then_inc(tile_out_ready, 1)

            stages(act, tile_stages)
            experts_done(act)

            def split_high(b, what, t):
                lat, high, ready, done = (k_lat, k_high, k_ready, k_high_ready) if what == "k" else (q_lat, q_high, q_ready, q_high_ready)
                wait(act, ready, b * G + t + 1)
                stacks_copied(act, b, t)
                A.copy(high[:, t, :], lat[:] if what == "k" else lat[:, t % 2, :]).then_inc(done, 1)

            def body(n):
                b = n.b
                for s in body_steps(n):
                    if n.exists():
                        w = P * ((s // GH) % NT + 1)
                        wait(act, max_ready, b * UNITS + s + 1)
                        wait(act, probs_turned, b * UNITS + s - PROBS + 1)
                        A.activation(probs[:, s % PROBS, 0:w], scores[s % 2][:, 0:w], ACT.Exp,
                                     bias=neg_max[:, s % 8:s % 8 + 1]).then_inc(probs_ready, 1)
                    off, u = n.back(s - TURN_LAG)
                    if n.exists(off) and on_act(u):
                        take_probs(act, A.copy, taken_act, b + off, u)
                    for what, t, off in PLAN.get(s - SPLIT_LAG, ()):
                        if n.exists(off) and what in ("k", "q_wqk"):
                            split_high(b + off, what, t)
                    end = group_end(s)
                    if end is not None and n.exists(end[0]):
                        off, g = end
                        wait(act, pv_done, (b + off) * G * NT + NT * (g + 1))
                        wait(act, o_turned_ps, (b + off) * G + g - 1)
                        A.copy(o_sb[:, g % 2, :], o_ps[:]).then_inc(o_taken, 1)

            for uses in PROJECT:
                for what, t, _ in uses:
                    if what in ("k", "q_wqk"):
                        split_high(0, what, t)
            bodies(act, body)

        @block.vector
        def _(dve):
            V = nc.vector

            for c, loaded in enumerate(x_in):
                dve.wait_ge(loaded, 16)
                n = TILES // len(x_in)
                with dve.Fori(c * n, (c + 1) * n) as tile:
                    V.bn_stats(stats[:, bass.ds(tile, 1), :].rearrange("p a n -> p (a n)"),
                               x_all[:, bass.ds(tile, 1), :].rearrange("p a n -> p (a n)")).then_inc(stats_done, 1)
            dve.wait_ge(stats_done, TILES)
            even, odd, even_sq, odd_sq = (stats[:, :, n:n + 1].rearrange("p n a -> p (n a)") for n in (1, 4, 2, 5))
            both, apart, summed, varied = (spread[:, n, :] for n in (1, 2, 3, 0))
            V.tensor_tensor(both, even, odd, ALU.add).then_inc(mean_steps, 1)
            V.tensor_tensor(apart, even, odd, ALU.subtract).then_inc(mean_steps, 1)
            V.tensor_tensor(summed, even_sq, odd_sq, ALU.add).then_inc(mean_steps, 1)
            dve.wait_ge(mean_steps, 3)
            V.tensor_scalar(mean[:], both, 0.5, None, ALU.mult).then_inc(mean_steps, 1)
            V.scalar_tensor_tensor(apart, apart, 0.25, apart, ALU.mult, ALU.mult).then_inc(mean_steps, 1)
            V.tensor_scalar(summed, summed, 1.0 / C, EPS, ALU.mult, ALU.add).then_inc(mean_steps, 1)
            dve.wait_ge(mean_steps, 6)
            V.tensor_tensor(varied, summed, apart, ALU.add).then_inc(rstd_steps, 1)

            dve.wait_ge(consts_in, 16 * len(CONST_LOADS))
            V.tensor_copy(identity_bf[:], identity[:]).then_inc(prep_done, 1)
            V.tensor_copy(mask_bf[:], mask_f[:]).then_inc(prep_done, 1)
            dve.wait_ge(prep_products, 1)
            V.tensor_copy(w_k[:], scores[0][:]).then_inc(prep_done, 1)
            pairs = scores[0][:].rearrange("p (n two) -> p n two", two=2)
            pairs_out = w_k_turned[:].rearrange("p (n two) -> p n two", two=2)
            V.tensor_scalar(pairs_out[:, :, 0:1], pairs[:, :, 1:2], -1.0, None, ALU.mult).then_inc(prep_done, 1)
            V.tensor_copy(pairs_out[:, :, 1:2], pairs[:, :, 0:1]).then_inc(prep_done, 1)
            dve.wait_ge(prep_products, 2)
            V.tensor_copy(w_q[:], scores[1][:]).then_inc(prep_done, 1)
            dve.wait_ge(prep_products, 3)
            V.tensor_copy(w_v_lat[:].rearrange("p g c -> p (g c)"), turned[0][:]).then_inc(prep_done, 1)
            dve.wait_ge(prep_products, 4)
            V.tensor_copy(w_qk_turned[:], turned[1][:, 0:P]).then_inc(prep_done, 1)
            dve.wait_ge(prep_products, 5)
            for n, (col, bias) in enumerate(((q_col, 0), (k_col, 1), (v_col, 3))):
                V.tensor_scalar(col[:], o_ps[:, G * n:G * n + G], bias_cols[:, bias:bias + 1], None, ALU.add).then_inc(prep_done, 1)
            V.memset(o_spread[:], 0.0).then_inc(prep_done, 1)
            dve.wait_ge(prep_products, 6)
            V.tensor_copy(k_col_turned[:], down_ps[:, 0:G]).then_inc(prep_done, 1)
            V.tensor_copy(w_v[:], work[0][:, 0:C]).then_inc(prep_done, 1)
            V.tensor_scalar(o_col[:], work[1][:, 0:1], bias_cols[:, 4:5], None, ALU.add).then_inc(o_col_ready, 1)
            dve.wait_ge(o_col_ready, 1)
            dve.wait_ge(prep_done, PREP_COLUMNS)
            V.tensor_scalar(o_spread[:], o_spread[:], o_col[:], None, ALU.add).then_inc(prep_done, 1)
            dve.wait_ge(prep_products, 7)
            V.tensor_tensor(out_add[:], turned[0][:, 0:C], out_bias_rows[:], ALU.add).then_inc(prep_done, 1)
            dve.wait_ge(down_in, 16 * len(CHUNKS))
            for n, (_, m) in enumerate(CHUNKS):
                part = down_w[0:m, :, n, :]
                V.tensor_scalar(part, part, 0.5, None, ALU.mult).then_inc(down_halved, 1)

            dve.wait_ge(std_done, 1)
            steps = (
                lambda: V.reciprocal(spread[:, 2, :], spread[:, 1, :]),
                lambda: V.tensor_tensor(spread[:, 3, :], spread[:, 2, :], spread[:, 2, :], ALU.mult),
                lambda: V.scalar_tensor_tensor(spread[:, 1, :], spread[:, 3, :], -0.5, spread[:, 0, :], ALU.mult, ALU.mult),
                lambda: V.scalar_tensor_tensor(rstd[:], spread[:, 1, :], 1.5, spread[:, 2, :], ALU.add, ALU.mult),
            )
            for n, step in enumerate(steps):
                step().then_inc(rstd_steps, 1)
                dve.wait_ge(rstd_steps, n + 2)

            def norm(b, par, turn):
                wait(dve, xn_turned, b - 1)
                wait(dve, rows_stored[par], turn * 16)
                for t in range(NT):
                    tile = bass.ds(b * NT + t, 1)
                    V.tensor_scalar(xn[:, par, t, :], x_all[:, tile, :].rearrange("p a n -> p (a n)"),
                                    mean[:, tile], rstd[:, tile],
                                    ALU.subtract, ALU.mult).then_inc(xn_ready, 1)

            def take_logits(b, par):
                wait(dve, logits_ps, b + 1)
                V.tensor_tensor(logits[:, bass.ds(b * NT, NT), :], turned[par][:, 0:NT * 8].rearrange("p (t e) -> p t e", e=8)[:, :, 0:ROUTED],
                                rb[:].unsqueeze(1).to_broadcast([P, NT, ROUTED]), ALU.add).then_inc(logits_taken, 1)

            norm(0, 0, 0)
            norm(1, 1, 0)
            with dve.Fori(0, B // 2 - 1) as pair:
                for par in range(2):
                    take_logits(pair * 2 + par, par)
                    norm(pair * 2 + par + 2, par, pair + 1)
            for par in range(2):
                take_logits(B - 2 + par, par)

            def over(a):
                return a.unsqueeze(2).to_broadcast([P, TILES, ROUTED])

            def chained(done, steps):
                for n, step in enumerate(steps):
                    step().then_inc(done, 1)
                    dve.wait_ge(done, n + 1)

            ranks_b = rank[:].unsqueeze(1).to_broadcast([P, TILES, ROUTED])
            top = [tops[:, n, :] for n in range(8)]
            r = [rt[:, n] for n in range(4)]
            V.memset(ones[:], 1.0).then_inc(mask_ready, 1)
            dve.wait_ge(logits_taken, B)
            chained(route_steps, (
                lambda: V.tensor_reduce(top[0], logits[:], X_AXIS, ALU.max),
                lambda: V.tensor_tensor(r[0], logits[:], over(top[0]), ALU.is_equal),
                lambda: V.tensor_tensor(r[1], r[0], ranks_b, ALU.mult),
                lambda: V.tensor_reduce(top[1], r[1], X_AXIS, ALU.max),
                lambda: V.tensor_tensor(r[2], r[1], over(top[1]), ALU.is_equal),
                lambda: V.scalar_tensor_tensor(r[3], r[2], -3e38, logits[:], ALU.mult, ALU.add),
                lambda: V.tensor_reduce(top[4], r[3], X_AXIS, ALU.max),
                lambda: V.tensor_tensor(top[2], top[4], top[0], ALU.subtract),
                lambda: V.tensor_tensor(r[0], r[3], over(top[4]), ALU.is_equal),
                lambda: V.tensor_tensor(r[1], r[0], ranks_b, ALU.mult),
                lambda: V.tensor_reduce(top[5], r[1], X_AXIS, ALU.max),
                lambda: V.tensor_tensor(r[3], r[1], over(top[5]), ALU.is_equal),
            ))
            V.tensor_tensor(r[0], r[2], r[3], ALU.add).then_inc(mask_ready, 1)
            dve.wait_ge(gap_exp, 1)
            first_weight, second_weight = (pair_weight[:, n, :] for n in range(2))
            chained(weight_steps, (
                lambda: V.tensor_scalar(top[1], top[3], 1.0, None, ALU.add),
                lambda: V.reciprocal(first_weight, top[1]),
                lambda: V.tensor_tensor(second_weight, top[3], first_weight, ALU.mult),
            ))

            earlier_in_tile, in_tile = (work[n][:, 0:TILES * ROUTED].rearrange("p (t e) -> p t e", e=ROUTED) for n in range(2))
            by_expert = r[1].rearrange("p t e -> p (t e)").rearrange("p (e t) -> p e t", e=ROUTED)
            s = [starts[:, n, :] for n in range(5)]
            counts = sums[:, 0, TILES - 1, :]
            steps = [lambda: V.tensor_copy(sums[:, 0], in_tile)]
            for n in range(TILES.bit_length() - 1):
                k, src, dst = 1 << n, sums[:, n % 2], sums[:, 1 - n % 2]
                steps += [lambda k=k, src=src, dst=dst: V.tensor_copy(dst[:, 0:k, :], src[:, 0:k, :]),
                          lambda k=k, src=src, dst=dst: V.tensor_tensor(dst[:, k:, :], src[:, k:, :], src[:, 0:TILES - k, :], ALU.add)]
            steps += [
                lambda: V.tensor_tensor(places[:], sums[:, 0], in_tile, ALU.subtract),
                lambda: V.tensor_tensor(places[:], places[:], earlier_in_tile, ALU.add),
                lambda: V.tensor_tensor(by_expert, counts.unsqueeze(2).to_broadcast([P, ROUTED, TILES]),
                                        tile_starts[:].unsqueeze(1).to_broadcast([P, ROUTED, TILES]), ALU.is_gt),
                lambda: V.tensor_reduce(s[0], by_expert, X_AXIS, ALU.add),
                lambda: V.memset(s[1][:, 0:1], 0.0),
                lambda: V.tensor_copy(s[1][:, 1:], s[0][:, 0:ROUTED - 1]),
            ]
            for n, k in enumerate((1, 2, 4)):
                src, dst = s[n + 1], s[n + 2]
                steps += [lambda k=k, src=src, dst=dst: V.tensor_copy(dst[:, 0:k], src[:, 0:k]),
                          lambda k=k, src=src, dst=dst: V.tensor_tensor(dst[:, k:], src[:, k:], src[:, 0:ROUTED - k], ALU.add)]
            starts_b = s[4].unsqueeze(1).to_broadcast([P, TILES, ROUTED])
            steps += [
                lambda: V.scalar_tensor_tensor(places[:], starts_b, float(P), places[:], ALU.mult, ALU.add),
                lambda: V.tensor_tensor(r[1], r[2], places[:], ALU.mult),
                lambda: V.tensor_reduce(top[4], r[1], X_AXIS, ALU.add),
                lambda: V.tensor_tensor(r[1], r[3], places[:], ALU.mult),
                lambda: V.tensor_reduce(top[5], r[1], X_AXIS, ALU.add),
                lambda: V.tensor_copy(place[:], tops[:, 4:6, :]),
                lambda: V.tensor_tensor(of_tile[:], tile_numbers[:].unsqueeze(2).to_broadcast([1, EXPERT_TILES, ROUTED]),
                                        s[4][0:1].unsqueeze(1).to_broadcast([1, EXPERT_TILES, ROUTED]), ALU.is_ge),
                lambda: V.tensor_reduce(of_tile_sum[:], of_tile[:], X_AXIS, ALU.add),
                lambda: V.tensor_scalar(of_tile_sum[:], of_tile_sum[:], -1.0, None, ALU.add),
                lambda: V.tensor_copy(tile_expert[:], of_tile_sum[:]),
            ]
            dve.wait_ge(counted_ps, 1)
            chained(sort_steps, steps)

            def residual(b, par, turn):
                flat = acc[:, par].rearrange("p t c -> p (t c)")
                wait(dve, down_done, (b + 1) * len(CHUNKS))
                wait(dve, partial_stored[par], turn * 16)
                V.tensor_tensor(flat, (o_ps, down_ps)[par][:], x_all[:, bass.ds(b * NT, NT), :].rearrange("p t c -> p (t c)"),
                                ALU.add).then_inc(shared_added, 1)
                wait(dve, shared_added, b + 1)
                V.tensor_tensor(acc[:, par], acc[:, par], out_add[:].unsqueeze(1).to_broadcast([P, NT, C]),
                                ALU.add).then_inc(residual_added, 1)

            def shared(b, par, turn):
                for ring in range(RING):
                    tile = bass.ds(b * NT + ring, 1)
                    wait(dve, scattered[ring], b * 2 * 16)
                    V.tensor_copy(place_cols[:, ring:ring + 1, :].rearrange("p r c -> p c r"), place[:, :, tile]).then_inc(place_copied, 1)
                    V.tensor_copy(token_col[:, ring:ring + 1], tokens[:, tile]).then_inc(place_copied, 1)
                for k, (_, m) in enumerate(CHUNKS):
                    n, bank = b * len(CHUNKS) + k, (par * len(CHUNKS) + k) % 2
                    h = hidden[0:m, k, :]
                    wait(dve, tanh_ready, n + 1)
                    V.scalar_tensor_tensor(h, h, 1.0, scores[bank][0:m, :], ALU.add, ALU.mult).then_inc(tanh_used, 1)
                    wait(dve, tanh_used, n + 1)
                    wait(dve, up_ps, n + 1)
                    V.tensor_tensor(h, h, turned[bank][0:m, :], ALU.mult).then_inc(hidden_ready, 1)
                    if k == 0 and not (isinstance(b, int) and b == 0):
                        residual(b - 1, 1 - par, turn - 1 + par)

            assert RING == NT
            dve.wait_ge(weights_in, 16)
            batches(dve, shared)
            residual(B - 1, 1, B // 2 - 1)

            dve.wait_ge(tokens_turned, 1)
            V.tensor_copy(token_of[:], work[0][:, 0:EXPERT_TILES]).then_inc(token_of_ready, 1)
            dve.wait_ge(token_of_ready, 1)

            def gather_cols(mine):
                j, c, turn = mine
                wait(dve, tile_in[c], turn * 16)
                V.tensor_copy(gather_col[:, c:c + 1], token_of[:, bass.ds(j, 1)]).then_inc(gather_col_ready, 1)

            def tile_stages(i, ring, turn):
                mine = lagging(i, ring, turn, -2)
                if mine:
                    gather_cols(mine)
                mine = lagging(i, ring, turn, 1)
                if mine:
                    j, c, _ = mine
                    h = tile_hidden[:, c % 2, 0:I]
                    wait(dve, tile_tanh, j + 1)
                    V.scalar_tensor_tensor(h, h, 1.0, scores[c % 2][:, 0:I], ALU.add, ALU.mult).then_inc(tile_gated, 1)
                    wait(dve, tile_gated, j + 1)
                    wait(dve, tile_up_ps, j + 1)
                    V.tensor_tensor(h, h, work[c % 2][:, 0:I], ALU.mult).then_inc(tile_hidden_ready, 1)

            for j in range(2):
                gather_cols((j, j, 0))
            stages(dve, tile_stages)
            experts_done(dve)

            def project(n, off, what, t):
                b = n.b + off
                if what == "k":
                    wait(dve, k_low_ready, b * G + t)
                    V.scalar_tensor_tensor(k_lat[:], filled(dve, what, t, b)[:], k_col[:, t:t + 1], cos_sb[:],
                                           ALU.add, ALU.mult).then_inc(k_parts, 1)
                elif what == "k_turned":
                    V.scalar_tensor_tensor(k_sin[:], filled(dve, what, t, b)[:], k_col_turned[:, t:t + 1], sin_sb[:],
                                           ALU.add, ALU.mult).then_inc(k_parts, 1)
                elif what == "q":
                    bank = filled(dve, what, t, b)
                    wait(dve, q_wqk_ps, b * G + t - 1)
                    for part, table in ((q_cos, cos_sb), (q_sin, sin_sb)):
                        V.scalar_tensor_tensor(part[:, t % 2, :], bank[:], q_col[:, t:t + 1], table[:],
                                               ALU.add, ALU.mult).then_inc(q_parts, 1)
                elif what == "q_wqk":
                    wait(dve, q_low_ready, b * G + t - 1)
                    V.tensor_scalar(q_lat[:, t % 2, :], filled(dve, what, t, b)[:], bias_cols[:, 2:3], SCALE,
                                    ALU.add, ALU.mult).then_inc(q_ready, 1)
                elif what == "v":
                    wait(dve, pv_done, (b - 1) * G * NT)
                    V.tensor_copy(values[:, n.par(off), :, 0:HD], filled(dve, what, t, b)[:].rearrange("p (n d) -> p n d", d=HD)).then_inc(values_ready, 1)

            def take_output(n, off, g):
                b = n.b + off
                o = filled(dve, "o_turned", g, b)[:].rearrange("p (t h l) -> p t h l", t=NT, h=GH)
                V.reciprocal(o_rec[:, g % 2].unsqueeze(3), o[:, :, :, SUM:SUM + 1]).then_inc(o_rec_ready, 1)
                wait(dve, o_rec_ready, b * G + g + 1)
                if g == 0:
                    wait(dve, y_ps, b)
                V.tensor_tensor(y_sb[:, :, g * GH * HD:(g + 1) * GH * HD].rearrange("p t (h d) -> p t h d", h=GH),
                                o[:, :, :, 0:HD], o_rec[:, g % 2].unsqueeze(3).to_broadcast([P, NT, GH, HD]),
                                ALU.mult).then_inc(y_parts, 1)

            def body(n):
                b = n.b
                if n.exists():
                    wait(dve, picked_in, b * 2 * NT * 16)
                    wait(dve, expert_added, b * 2 * NT)
                    V.tensor_copy(weight_now[:], pair_weight[:, :, bass.ds(b * NT, NT)]).then_inc(weight_ready, 1)
                    V.tensor_copy(place_now[:], place[:, :, bass.ds(b * NT, NT)]).then_inc(now_ready, 1)
                for s in body_steps(n):
                    for what, i, off in PLAN.get(s - 1, ()):
                        if not n.exists(off):
                            continue
                        if what == "o_turned":
                            take_output(n, off, i)
                        elif what == "y":
                            wait(dve, cproj_done, b + off)
                            V.tensor_copy(y_t[:], filled(dve, "y", 0, b + off)[:]).then_inc(y_t_ready, 1)
                        else:
                            project(n, off, what, i)
                    if n.exists():
                        w = P * ((s // GH) % NT + 1)
                        wait(dve, scores_ready, b * UNITS + s + 1)
                        V.tensor_reduce(neg_max[:, s % 8:s % 8 + 1], scores[s % 2][:, 0:w], X_AXIS, ALU.max,
                                        negate=True).then_inc(max_ready, 1)
                    off, u = n.back(s - TURN_LAG)
                    if n.exists(off) and not on_act(u):
                        take_probs(dve, V.tensor_copy, taken_dve, b + off, u)
                    if COMBINE_STEP <= s < COMBINE_STEP + 2 * NT and n.exists():
                        choice, t = divmod(s - COMBINE_STEP, NT)
                        mine = acc[:, n.par(), t, :]
                        wait(dve, weight_ready, b + 1)
                        wait(dve, picked_in, (b + 1) * 2 * NT * 16)
                        wait(dve, acc_in[n.par()], n.alike() * 16)
                        wait(dve, expert_added, b * 2 * NT + choice * NT + (t if choice else 0))
                        V.scalar_tensor_tensor(mine, picked[:, choice, t, :], weight_now[:, choice, t:t + 1], mine,
                                               ALU.mult, ALU.add).then_inc(expert_added, 1)
                    if s == CPROJ_STEP + 1 and n.exists(-1):
                        flat = acc[:, n.par(-1)].rearrange("p t c -> p (t c)")
                        wait(dve, cproj_done, b)
                        wait(dve, expert_added, b * 2 * NT)
                        V.tensor_tensor(flat, down_ps[:], flat, ALU.add).then_inc(attention_added, 1)

            first = Batch(0, 0)
            dve.wait_ge(zeroed, 2)
            for uses in PROJECT:
                for what, t, _ in uses:
                    project(first, 0, what, t)
            bodies(dve, body)

        @block.tensor
        def _(pe):
            M = nc.tensor

            pe.wait_ge(consts_in, 16 * len(CONST_LOADS))
            M.matmul(scores[0][:], attn_rows[:, 1, :], bdkv[:], start=True, stop=True).then_inc(prep_products, 1)
            M.matmul(scores[1][:], attn_rows[:, 0, :], bdq[:], start=True, stop=True).then_inc(prep_products, 1)
            for g in range(G):
                last = M.matmul(turned[0][:, g * C:(g + 1) * C], bdkv[:, g * P:(g + 1) * P], attn_rows[:, 2, :], start=True, stop=True)
            last.then_inc(prep_products, 1)
            M.matmul(turned[1][:, 0:P], rot_sb[:], bdqk[:], start=True, stop=True).then_inc(prep_products, 1)
            for n, (bd, bias) in enumerate(((bdq, 5), (bdkv, 6), (bdkv, 7))):
                for g in range(G):
                    last = M.matmul(o_ps[:, n * G + g:n * G + g + 1], bd[:, g * P:(g + 1) * P], bias_cols[:, bias:bias + 1],
                                    start=True, stop=True)
            last.then_inc(prep_products, 1)
            pe.wait_ge(prep_done, PREP_COLUMNS)
            M.matmul(down_ps[:, 0:G], rot_t_sb[:], k_col[:], start=True, stop=True)
            for g in range(G):
                M.matmul(work[0][:, 0:C], w_v_lat[:, g, :], bdo[:, g, :], start=(g == 0), stop=(g == G - 1))
            for g in range(G):
                last = M.matmul(work[1][:, 0:1], bdo[:, g, :], v_col[:, g:g + 1], start=(g == 0), stop=(g == G - 1))
            last.then_inc(prep_products, 1)
            pe.wait_ge(prep_done, PREP_SPREAD)
            M.matmul(turned[0][:, 0:C], o_spread[:], cproj_w[:], start=True, stop=True).then_inc(prep_products, 1)
            pe.wait_ge(prep_done, PREP_ALL)

            def turn_xn(b, par):
                wait(pe, xn_ready, (b + 1) * NT)
                wait(pe, xn_t_ready, b - 1)
                for t in range(NT):
                    last = M.transpose(work[par][:, t * P:(t + 1) * P], xn[:, par, t, :], identity[:])
                last.then_inc(xn_turned, 1)

            def route(b, par):
                wait(pe, xn_t_ready, b + 1)
                wait(pe, logits_taken, b - 1)
                for t in range(NT):
                    last = M.matmul(turned[par][:, t * 8:t * 8 + ROUTED], xn_t[:, par, t * P:(t + 1) * P], wr[:], start=True, stop=True)
                last.then_inc(logits_ps, 1)

            turn_xn(0, 0)
            turn_xn(1, 1)
            for b in range(2):
                route(b, b)
                turn_xn(b + 2, b)
            with pe.Fori(1, B // 2 - 1) as pair:
                for par in range(2):
                    route(pair * 2 + par, par)
                    turn_xn(pair * 2 + par + 2, par)
            for par in range(2):
                route(B - 2 + par, par)
            pe.wait_ge(xn_t_ready, B)
            pe.wait_ge(logits_taken, B)
            pe.wait_ge(mask_ready, 2)
            both = rt[:, 0].rearrange("p t e -> p (t e)")
            M.matmul(work[0][:, 0:TILES * ROUTED], earlier[:], both, start=True, stop=True)
            M.matmul(work[1][:, 0:TILES * ROUTED], ones[:], both, start=True, stop=True).then_inc(counted_ps, 1)
            pe.wait_ge(weights_in, 16)
            pe.wait_ge(down_halved, len(CHUNKS))

            def shared_down(b, par, k):
                n, m = b * len(CHUNKS) + k, CHUNKS[k][1]
                wait(pe, hidden_ready, n + 1)
                if k == 0:
                    wait(pe, shared_added, b - 1)
                for t in range(NT):
                    last = M.matmul((o_ps, down_ps)[par][:, t * C:(t + 1) * C], hidden[0:m, k, t * P:(t + 1) * P], down_w[0:m, ROUTED, k, :],
                                    start=(k == 0 and t == 0), stop=(k == len(CHUNKS) - 1), skip_group_check=True)
                last.then_inc(down_done, 1)

            def shared(b, par, turn):
                wait(pe, xb_in[par], 16 * (turn + 1))
                for k, (first, m) in enumerate(CHUNKS):
                    n, bank = b * len(CHUNKS) + k, (par * len(CHUNKS) + k) % 2
                    cols = slice(ROUTED * I + first, ROUTED * I + first + m)
                    wait(pe, tanh_used, n - 1)
                    M.matmul(scores[bank][0:m, :], gate_up_w[:, 0, cols], xb[:, par, :], start=True, stop=True).then_inc(gate_ps, 1)
                    wait(pe, hidden_ready, n - 1)
                    M.matmul(turned[bank][0:m, :], gate_up_w[:, 1, cols], xb[:, par, :], start=True, stop=True).then_inc(up_ps, 1)
                    if k > 0:
                        shared_down(b, par, k - 1)
                    elif not (isinstance(b, int) and b == 0):
                        shared_down(b - 1, 1 - par, len(CHUNKS) - 1)

            batches(pe, shared)
            shared_down(B - 1, 1, len(CHUNKS) - 1)

            pe.wait_ge(token_rows_in, 32)
            M.transpose(work[0][:, 0:P], token_rows[:, 0, :], identity[:])
            M.transpose(work[0][:, P:EXPERT_TILES], token_rows[0:EXPERT_TILES - P, 1, :],
                        identity[0:EXPERT_TILES - P, 0:EXPERT_TILES - P]).then_inc(tokens_turned, 1)
            pe.wait_ge(shared_added, B)
            pe.wait_ge(token_of_ready, 1)

            def expert_of(j):
                return pe.value_load(tile_expert[0:1, bass.ds(j, 1)], min_val=0, max_val=ROUTED - 1)

            def tile_stages(i, ring, turn):
                hidden_tile, out_tile = lagging(i, ring, turn, 1), lagging(i, ring, turn, 3)
                if hidden_tile:
                    hidden_expert = expert_of(hidden_tile[0])
                if out_tile:
                    out_expert = expert_of(out_tile[0])
                mine = lagging(i, ring, turn, 0)
                if mine:
                    j, c, turn = mine
                    wait(pe, tile_in[c], 16 * (turn + 1))
                    wait(pe, gathered_t_ready, j - 1)
                    M.transpose(turned[c % 2][:, 0:P], gathered[:, c, :], identity[:]).then_inc(tile_turned, 1)
                if hidden_tile:
                    j, c, _ = hidden_tile
                    wait(pe, gathered_t_ready, j + 1)
                    wait(pe, tile_gated, j - 1)
                    M.matmul(scores[c % 2][:, 0:I], gathered_t[:, c % 2, :], gate_up_w[:, 0, bass.ds(hidden_expert * I, I)],
                             start=True, stop=True).then_inc(tile_gate_ps, 1)
                    wait(pe, tile_hidden_ready, j - 1)
                    M.matmul(work[c % 2][:, 0:I], gathered_t[:, c % 2, :], gate_up_w[:, 1, bass.ds(hidden_expert * I, I)],
                             start=True, stop=True).then_inc(tile_up_ps, 1)
                mine = lagging(i, ring, turn, 2)
                if mine:
                    j, c, _ = mine
                    wait(pe, tile_hidden_ready, j + 1)
                    wait(pe, tile_hidden_t_ready, j)
                    for n in range(len(CHUNKS)):
                        last = M.transpose(o_ps[:, n * P:(n + 1) * P], tile_hidden[:, c % 2, n * P:(n + 1) * P], identity[:])
                    last.then_inc(tile_hidden_turned, 1)
                if out_tile:
                    j, c, _ = out_tile
                    wait(pe, tile_hidden_t_ready, j + 1)
                    wait(pe, tile_out_ready, j)
                    for n, (_, m) in enumerate(CHUNKS):
                        last = M.matmul(down_ps[:, 0:C], tile_hidden_t[0:m, c % 2, n, :],
                                        down_w[0:m, bass.ds(out_expert, 1), n, :].rearrange("p a c -> p (a c)"),
                                        start=(n == 0), stop=(n == len(CHUNKS) - 1))
                    last.then_inc(tile_down, 1)

            stages(pe, tile_stages)
            experts_done(pe)


            def bank(n, known, what, i, off):
                before = use_before(known, what, i, off)
                if before is not None:
                    w, j, o = before
                    b = n.b + o
                    s, count = {
                        "k": (k_parts, 2 * (b * G + j) + 1), "k_turned": (k_parts, 2 * (b * G + j) + 2),
                        "q": (q_parts, 2 * (b * G + j) + 2), "q_wqk": (q_ready, b * G + j + 1), "v": (values_ready, b + 1),
                        "o_turned": (y_parts, b * G + j + 1), "y": (y_t_ready, b + 1)}[w]
                    wait(pe, s, count)
                return work[bank_of(what, i)]

            def project(n, known, what, i, off):
                b, xt = n.b + off, xb[:, n.par(off), :]
                cols = slice(i * P, (i + 1) * P)
                if (what, i) == PROJECT[0][0][:2]:
                    wait(pe, xb_in[n.par(off)], (B // 2 + n.alike(off)) * 16)
                out_ps = bank(n, known, what, i, off)
                if what == "k":
                    M.matmul(out_ps[:], w_k[:, cols], xt, start=True, stop=True).then_inc(k_ps, 1)
                elif what == "k_turned":
                    M.matmul(out_ps[:], w_k_turned[:, cols], xt, start=True, stop=True).then_inc(k_ps, 1)
                elif what == "q":
                    M.matmul(out_ps[:], w_q[:, cols], xt, start=True, stop=True).then_inc(q_ps, 1)
                elif what == "q_wqk":
                    wait(pe, q_parts, 2 * (b * G + i + 1))
                    M.matmul(out_ps[:], bdqk[:], q_cos[:, i % 2, :], start=True, stop=False)
                    M.matmul(out_ps[:], w_qk_turned[:], q_sin[:, i % 2, :], start=False, stop=True).then_inc(q_wqk_ps, 1)
                elif what == "v":
                    for t in range(NT):
                        last = M.matmul(out_ps[:, t * C:(t + 1) * C], xb[:, n.par(off), t * P:(t + 1) * P], w_v[:], start=True, stop=True)
                    last.then_inc(v_ps, 1)

            def score(b, u):
                quad, r = divmod(u, GH)
                g, i = divmod(quad, NT)
                half, t = divmod(g, HG)
                w = P * (i + 1)
                wait(pe, probs_ready, b * UNITS + u - 1)
                if u % HALF_UNITS == 0:
                    wait(pe, stack_in[half], (b + 1) * STACK_COPIES * 16)
                wide = max(w, 2 * P)
                M.matmul(scores[u % 2][:, 0:wide], q_stack[:, half, r, t, i * P:w], k_stack[:, half, r, t, 0:wide], start=True, stop=False)
                M.matmul(scores[u % 2][:, w - P:w], identity_bf[:], mask_bf[:], start=False, stop=True).then_inc(scores_ready, 1)

            def turn(b, u):
                wait(pe, probs_ready, b * UNITS + u + 1)
                taken(pe, b, u - 2)
                for j in range((u // GH) % NT + 1):
                    last = M.transpose(turned[u % 2][:, j * P:(j + 1) * P], probs[:, u % PROBS, j * P:(j + 1) * P], identity[:])
                last.then_inc(probs_turned, 1)

            def heads(n, off, g, i):
                b, quad = n.b + off, g * NT + i
                taken(pe, b, quad * GH)
                taken(pe, b, quad * GH + GH - 1)
                if i == 0:
                    wait(pe, o_taken, b * G + g)
                if quad == 0:
                    wait(pe, values_ready, b + 1)
                for j in range(i + 1):
                    for r in range(GH):
                        last = M.matmul(o_ps[r * LAT:(r + 1) * LAT, i * P:(i + 1) * P], values[:, n.par(off), j * H + g * GH + r, :],
                                        probs_t[:, quad % 2, r, j * P:(j + 1) * P], start=(j == 0), stop=(j == i),
                                        skip_group_check=True)
                last.then_inc(pv_done, 1)

            def body(n):
                b = n.b
                for s in body_steps(n):
                    if n.exists():
                        score(b, s)
                    off, u = n.back(s - TURN_LAG)
                    if n.exists(off):
                        turn(b + off, u)
                    if s == CPROJ_STEP and n.exists(-1):
                        wait(pe, y_t_ready, b)
                        wait(pe, attention_added, b - 1)
                        for t in range(NT):
                            last = M.matmul(down_ps[:, t * C:(t + 1) * C], y_t[:, t * P:(t + 1) * P], cproj_w[:],
                                            start=True, stop=True, skip_group_check=True)
                        last.then_inc(cproj_done, 1)
                    h = heads_at(s)
                    if h is not None and n.exists(h[0]):
                        heads(n, *h)
                    for what, i, off in PLAN.get(s, ()):
                        if not n.exists(off):
                            continue
                        if what == "o_turned":
                            wait(pe, o_taken, (b + off) * G + i + 1)
                            out_ps = bank(n, n.known, what, i, off)
                            for t in range(NT):
                                last = M.transpose(out_ps[:, t * P:(t + 1) * P], o_sb[:, i % 2, t * P:(t + 1) * P], identity[:])
                            last.then_inc(o_turned_ps, 1)
                        elif what == "y":
                            wait(pe, y_parts, (b + off + 1) * G)
                            out_ps = bank(n, n.known, what, i, off)
                            for t in range(NT):
                                last = M.transpose(out_ps[:, t * P:(t + 1) * P], y_sb[:, t, :], identity[:])
                            last.then_inc(y_ps, 1)
                        else:
                            project(n, n.known, what, i, off)

            for uses in PROJECT:
                for what, t, _ in uses:
                    project(Batch(0, 0), "first", what, t, 0)
            bodies(pe, body)


def _blocks(a, n):
    out = np.zeros((a.shape[0] * n, a.shape[1] * n), a.dtype)
    for i in range(n):
        out[i * a.shape[0]:(i + 1) * a.shape[0], i * a.shape[1]:(i + 1) * a.shape[1]] = a
    return out


def _column(a, n):
    return np.tile(np.asarray(a), n).reshape(-1, 1)


def _tables():
    inv = (np.float32(1) / np.power(np.float32(10000), np.arange(0, LAT, 2, dtype=np.float32) / np.float32(LAT))).astype(np.float32)
    angles = np.repeat(np.outer(np.arange(T, dtype=np.float32), inv), 2, axis=1).T
    rot = np.zeros((P, P), np.float32)
    for i in range(0, P, 2):
        rot[i, i + 1], rot[i + 1, i] = -1, 1
    mask = np.where(np.tril(np.ones((P, P), bool)), 0, MASKED).astype(np.float32)
    ranks = np.arange(ROUTED, 0, -1, dtype=np.float32).reshape(1, ROUTED)
    return {"ident": np.eye(P, dtype=np.float32), "mask": mask, "rot": rot, "rot_t": np.ascontiguousarray(rot.T),
            "before": np.triu(np.ones((P, P), np.float32), 1),
            "token_no": np.arange(TILES * P, dtype=np.float32).reshape(TILES, P).T,
            "tile_no": np.arange(EXPERT_TILES, dtype=np.float32).reshape(1, -1),
            "tile_start": P * np.arange(TILES, dtype=np.float32).reshape(1, -1),
            "cos": np.tile(np.cos(angles), (GH, 1)), "sin": np.tile(np.sin(angles), (GH, 1)), "ranks": ranks}


def kernel(**inputs):
    import concourse.bacc as bacc
    from concourse.bass_utils import run_bass_kernel_spmd

    a = {n.removeprefix("L0_"): np.asarray(v) for n, v in inputs.items()}
    attn_b = a["attn_c_attn_b"].reshape(3, C, 1)
    arrays = {
        "x": a["attn_x"],
        "gate_up": np.stack([np.concatenate([a[r], a[s][None]]).reshape(E * I, C).T for r, s in (("ffn_rg", "ffn_sg"), ("ffn_ru", "ffn_su"))]),
        "down": np.concatenate([a["ffn_rd"], a["ffn_sd"][None]]).transpose(0, 2, 1),
        "attn_w": a["attn_c_attn_w"].reshape(3, C, C),
        "bd_q": _blocks(a["attn_q2l_w"].T, H),
        "bd_kv": _blocks(a["attn_kv2l_w"].T, H),
        "bd_qk": _blocks(a["attn_wqk_w"].T, GH),
        "bd_o": _blocks(a["attn_l2o_w"].T, H).reshape(G, P, H * HD).reshape(G * P, C),
        "cproj": a["attn_cproj_w"].T,
        "biases": np.concatenate([_column(a["attn_q2l_b"], GH), _column(a["attn_kv2l_b"], GH), _column(a["attn_wqk_b"], GH),
                                  _column(a["attn_kv2l_b"], GH), _column(a["attn_l2o_b"], H), *attn_b], axis=1),
        "out_bias": a["attn_cproj_b"].reshape(1, C),
        "router_w": a["ffn_wr"].T,
        "router_b": a["ffn_rb"].reshape(1, ROUTED),
        **_tables(),
    }
    arrays = {n: np.ascontiguousarray(v) for n, v in arrays.items()}
    nc = bacc.Bacc("TRN2", target_bir_lowering=False, num_devices=1)
    aps = {n: nc.dram_tensor(f"in_{n}", v.shape, mybir.dt.from_np(v.dtype), kind="ExternalInput").ap() for n, v in arrays.items()}
    out = nc.dram_tensor("out", (B, T, C), F32, kind="ExternalOutput").ap()
    build(nc, out=out, **aps)
    r = run_bass_kernel_spmd(nc, [{f"in_{n}": v for n, v in arrays.items()}], core_ids=[0])
    return r.results[0]["out"]
```

```python
from contextlib import ExitStack

import numpy as np

import concourse.bass as bass
from concourse import mybir

F32 = mybir.dt.float32
F32R = mybir.dt.float32r
U32 = mybir.dt.uint32
I32 = mybir.dt.int32
BF16 = mybir.dt.bfloat16
ALU = mybir.AluOpType
ACT = mybir.ActivationFunctionType
X_AXIS = mybir.AxisListType.X

P = 128
B, T, C = 16, 512, 128
NT = T // P
H, HD, LAT = 16, 8, 32
GH = P // LAT
G = H // GH
LT = H * LAT
ROUTED, I = 7, 352
E = ROUTED + 1
CHUNKS = [(0, 128), (128, 128), (256, I - 256)]
EPS = 1e-5
SCALE = float(LAT) ** -0.5
MASKED = -1e30
SUM = HD

PAIRED = 2 * P
UNIT = [(g, i, heads) for g in range(G) for i in range(NT)
        for heads in ([(r, r + 1) for r in range(0, GH, 2)] if (i + 1) * P <= PAIRED else [(r,) for r in range(GH)])]
UNITS = len(UNIT)
LAST_UNIT = {(g, i): u for u, (g, i, _) in enumerate(UNIT)}
HALF_UNITS = UNITS // 2
HG = G // 2
TILES = B * NT
EXPERT_TILES = 2 * TILES + ROUTED - 1
RING = 4
LAGS = 3
TURN_LAG = 3
PROBS = 4
FIRST_PROJECT_STEP = 5
COMBINE_STEP = 20


def step_plan():
    plan = {6: [("o_turned", G - 1, -1)], 9: [("y", 0, -1)], 12: [("cproj", 0, -1)]}
    for g in range(G - 1):
        plan[LAST_UNIT[g, NT - 1] + 7] = [("o_turned", g, 0)]
    project = []
    for half in range(2):
        a, b = HG * half, HG * half + 1
        project += [("k", a, 1), ("k_turned", a, 1), ("q", a, 1), ("q", b, 1), ("k", b, 1), ("k_turned", b, 1),
                    ("q_wqk", a, 1), ("q_wqk", b, 1)] + ([("v", 0, 1)] if half == 0 else [])
    steps = [s for s in range(FIRST_PROJECT_STEP, UNITS - 3) if s not in plan]
    for n, use in enumerate(project):
        plan[steps[n * len(steps) // len(project)]] = [use]
    return dict(sorted(plan.items())), project


PLAN, PROJECT = step_plan()
BANK = {"k": 0, "k_turned": 1, "v": 1, "y": 0, "cproj": 1}


def bank_of(what, i):
    return BANK[what] if what in BANK else i % 2


BODY_USES = [use for uses in PLAN.values() for use in uses]
FIRST_USES = [(what, i, 0) for what, i, _ in PROJECT]


def use_before(b, what, i, off):
    bank = bank_of(what, i)
    if b == "first":
        uses, at, body = FIRST_USES, FIRST_USES.index((what, i, off)), "first"
    else:
        uses, at, body = BODY_USES, BODY_USES.index((what, i, off)), 0
    while True:
        at -= 1
        if at < 0:
            if body == "first":
                return None
            body -= 1
            if b is not None and b + body < 0:
                uses, body = FIRST_USES, "first"
            at = len(uses) - 1
        w, n, o = uses[at]
        if bank_of(w, n) != bank:
            continue
        if body == "first":
            return w, n, (0 if b == "first" else -b)
        owner = body + o
        if b is not None and not 0 <= b + owner < B:
            continue
        return w, n, owner


USE_STEP = {(what, i): s for s, uses in PLAN.items() for what, i, _ in uses}
SPLIT_LAG = 3
GAP_STEP = 8
TAIL = USE_STEP["cproj", 0] + 2


def score_bank(u):
    return u % 3


assert UNITS % 3 == 0


def on_act(u):
    return u % GH != 0


ACT_TAKES = [u for u in range(UNITS) if on_act(u)]
DVE_TAKES = [u for u in range(UNITS) if not on_act(u)]


class Batch:

    def __init__(self, pair, c):
        self.b, self.pair, self.c = pair * 2 + c, pair, c
        self.known = self.b if isinstance(self.b, int) else None

    def par(self, off=0):
        return (self.c + off) % 2

    def alike(self, off=0):
        return self.pair + (self.c + off) // 2 + 1

    def exists(self, off=0):
        return self.known is None or 0 <= self.known + off < B

    def back(self, step):
        return (0, step) if step >= 0 else (-1, step + UNITS)


def heads_at(step):
    off, u = divmod(step - TURN_LAG - 2, UNITS)
    g, i, _ = UNIT[u]
    return (off, g, i) if LAST_UNIT[g, i] == u else None


def group_end(step):
    h = heads_at(step)
    return (h[0], h[1]) if h and h[2] == NT - 1 else None


def build(nc, x, gate_up, down, attn_w, bd_q, bd_kv, bd_qk, bd_o, cproj, biases, out_bias, router_w, router_b, ranks,
          ident, mask, rot, rot_t, cos, sin, before, token_no, tile_no, tile_start, out):
    xn_dram = nc.dram_tensor("normed_transposed", (B, P, T), F32, kind="Internal").ap()
    x_tiles = x.rearrange("b (t p) c -> p (b t) c", p=P)
    out_tiles = out.rearrange("b (t p) c -> b p t c", p=P)
    normed = nc.dram_tensor("normed", (TILES * P, C), F32, kind="Internal").ap()
    normed_by_batch = normed.rearrange("(b t p) c -> b p t c", p=P, t=NT)
    partial = nc.dram_tensor("partial", (B, P, NT * C), F32, kind="Internal").ap()
    sorted_tokens = nc.dram_tensor("sorted_tokens", (EXPERT_TILES * P, 1), F32, kind="Internal").ap()
    expert_out = nc.dram_tensor("expert_out", (EXPERT_TILES * P, C), F32, kind="Internal").ap()

    with ExitStack() as ctx:
        def sb(name, shape, dt=F32):
            return ctx.enter_context(nc.sbuf_tensor(name, shape, dt))

        def psum(name, shape=(P, 512)):
            return ctx.enter_context(nc.psum_tensor(name, list(shape), F32))

        def sem(name):
            return ctx.enter_context(nc.semaphore(name))

        with ExitStack() as ahead:
            def early(name, shape, dt=F32):
                return ahead.enter_context(nc.sbuf_tensor(name, shape, dt))

            x_all = early("x_all", [P, TILES, C])
            attn_rows = early("attn_rows", [P, 3, C])
            bdq = early("bdq", [P, LT])
            bdkv = early("bdkv", [P, LT])
            bdo = early("bdo", [P, G, C])
            out_bias_rows = early("out_bias_rows", [P, C])
            mask_f = early("mask_f", [P, P])
            rot_sb = early("rot_sb", [P, P])
            rot_t_sb = early("rot_t_sb", [P, P])
            w_v_lat = early("w_v_lat", [P, G, C])
            o_spread = early("o_spread", [P, P])
            stats = early("stats", [P, TILES, 6])
            mean = early("mean", [P, TILES])
            spread = early("spread", [P, 4, TILES])
            rstd = early("rstd", [P, TILES])
            xn = early("xn", [P, 2, NT, C])
            xn_t = early("xn_t", [P, 2, T])
            logits = early("logits", [P, TILES, ROUTED])
            rt = early("rt", [P, 4, TILES, ROUTED])
            tops = early("tops", [P, 8, TILES])
            wr = early("wr", [P, ROUTED])
            rb = early("rb", [P, ROUTED])
            rank = early("rank", [P, ROUTED])
            gate_up_w = early("gate_up_w", [P, 2, E * I])
            gate_up_high = early("gate_up_high", [P, 2, ROUTED * I], F32R)
            down_w = early("down_w", [P, E, len(CHUNKS), C])
            earlier = early("earlier", [P, P])
            ones = early("ones", [P, P])
            tokens = early("tokens", [P, TILES])
            tile_numbers = early("tile_numbers", [1, EXPERT_TILES])
            tile_starts = early("tile_starts", [P, TILES])
            sums = early("sums", [P, 2, TILES, ROUTED])
            places = early("places", [P, TILES, ROUTED])
            starts = early("starts", [P, 5, ROUTED])
            of_tile = early("of_tile", [1, EXPERT_TILES, ROUTED])
            of_tile_sum = early("of_tile_sum", [1, EXPERT_TILES])
            weight_cols_f = early("weight_cols_f", [1, 2, EXPERT_TILES])
            weight_cols = early("weight_cols", [1, 2, EXPERT_TILES], I32)
            place_cols = early("place_cols", [P, RING, 2], U32)
            token_col = early("token_col", [P, RING])
            zero_tokens = early("zero_tokens", [P, EXPERT_TILES])
            token_rows = early("token_rows", [P, 2, P])
            token_of = early("token_of", [P, EXPERT_TILES], U32)
            hidden = early("hidden", [P, 3, T])
            gather_col = early("gather_col", [P, RING], U32)
            gathered = early("gathered", [P, RING, C])
            gathered_high = early("gathered_high", [P, 2, P], F32R)
            gathered_low = early("gathered_low", [P, 2, P], F32R)
            tile_hidden = early("tile_hidden", [P, 2, len(CHUNKS) * P])
            tile_hidden_t = early("tile_hidden_t", [P, 2, len(CHUNKS), P])
            tile_out = early("tile_out", [P, 2, C])
        q_stack = sb("q_stack", [P, 2, GH, HG, T], F32R)
        k_stack = sb("k_stack", [P, 2, GH, HG, T], F32R)
        k_high = sb("k_high", [P, G, T], F32R)
        k_low = sb("k_low", [P, G, T], F32R)
        q_high = sb("q_high", [P, G, T], F32R)
        q_low = sb("q_low", [P, G, T], F32R)
        probs = sb("probs", [P, PROBS, T])
        probs_t = sb("probs_t", [P, 2, GH, T])
        q_cos = sb("q_cos", [P, 2, T])
        q_sin = sb("q_sin", [P, 2, T])
        q_lat = sb("q_lat", [P, 2, T])
        o_sb = sb("o_sb", [P, 2, T])
        k_lat = sb("k_lat", [P, T])
        k_sin = sb("k_sin", [P, T])
        y_sb = sb("y_sb", [P, NT, C])
        y_t = sb("y_t", [P, T])
        picked = sb("picked", [P, 2, NT, C])
        xb_high = sb("xb_high", [P, 2, T], F32R)
        xb_low = sb("xb_low", [P, 2, T], F32R)
        bdqk = sb("bdqk", [P, P])
        cproj_w = sb("cproj_w", [P, C])
        bias_cols = sb("bias_cols", [P, 8])
        identity = sb("identity", [P, P])
        identity_bf = sb("identity_bf", [P, P], BF16)
        mask_bf = sb("mask_bf", [P, P], BF16)
        cos_sb = sb("cos_sb", [P, T])
        sin_sb = sb("sin_sb", [P, T])
        w_q = sb("w_q", [P, LT])
        w_k = sb("w_k", [P, LT])
        w_k_turned = sb("w_k_turned", [P, LT])
        w_qk_turned = sb("w_qk_turned", [P, P])
        w_v = sb("w_v", [P, C])
        w_high = sb("w_high", [P, 3, LT], F32R)
        w_low = sb("w_low", [P, 3, LT], F32R)
        q_col = sb("q_col", [P, G])
        k_col = sb("k_col", [P, G])
        k_col_turned = sb("k_col_turned", [P, G])
        v_col = sb("v_col", [P, G])
        o_col = sb("o_col", [P, 1])
        out_add = sb("out_add", [P, C])
        pair_weight = sb("pair_weight", [P, 2, TILES])
        place = sb("place", [P, 2, TILES], U32)
        carrier = sb("carrier", [1, 2])
        xb = sb("xb", [P, 2, T])
        acc = sb("acc", [P, 2, NT, C])
        weight_now = sb("weight_now", [P, 2, NT])
        place_now = sb("place_now", [P, 2, NT], U32)
        values = sb("values", [P, 2, NT * H, LAT])
        neg_max = sb("neg_max", [P, 8, 2])
        o_rec = sb("o_rec", [P, 2, NT, GH])

        scores = [psum(f"scores{i}") for i in range(2)]
        turned = [psum(f"turned{i}") for i in range(2)]
        work = [psum(f"work{i}") for i in range(2)]
        o_ps = psum("o_ps")
        down_ps = psum("down_ps")

        consts_in = sem("consts_in")
        weights_in = sem("weights_in")
        down_in = sem("down_in")
        down_halved = sem("down_halved")
        o_col_ready = sem("o_col_ready")
        x_in = [sem(f"x_in{i}") for i in range(4)]
        zeroed = sem("zeroed")
        prep_products = sem("prep_products")
        prep_done = sem("prep_done")
        stats_done = sem("stats_done")
        mean_steps = sem("mean_steps")
        std_done = sem("std_done")
        rstd_steps = sem("rstd_steps")
        xn_ready = sem("xn_ready")
        xn_turned = sem("xn_turned")
        xn_t_ready = sem("xn_t_ready")
        xn_stored = [sem(f"xn_stored{i}") for i in range(2)]
        logits_ps = sem("logits_ps")
        logits_taken = sem("logits_taken")
        route_steps = sem("route_steps")
        gap_exp = sem("gap_exp")
        xb_in = [sem(f"xb_in{i}") for i in range(2)]
        acc_in = [sem(f"acc_in{i}") for i in range(2)]
        expert_added = sem("expert_added")
        attention_added = sem("attention_added")
        stored = [sem(f"stored{i}") for i in range(2)]
        k_ps = sem("k_ps")
        q_ps = sem("q_ps")
        q_wqk_ps = sem("q_wqk_ps")
        v_ps = sem("v_ps")
        gate_ps = sem("gate_ps")
        up_ps = sem("up_ps")
        o_turned_ps = sem("o_turned_ps")
        y_ps = sem("y_ps")
        k_parts = sem("k_parts")
        k_ready = sem("k_ready")
        k_high_ready = sem("k_high_ready")
        k_low_ready = sem("k_low_ready")
        q_parts = sem("q_parts")
        q_ready = sem("q_ready")
        q_high_ready = sem("q_high_ready")
        q_low_ready = sem("q_low_ready")
        stack_in = [sem(f"stack_in{i}") for i in range(2)]
        values_ready = sem("values_ready")
        w_high_ready = sem("w_high_ready")
        w_low_ready = sem("w_low_ready")
        xb_high_ready = sem("xb_high_ready")
        xb_low_ready = sem("xb_low_ready")
        now_ready = sem("now_ready")
        weight_ready = sem("weight_ready")
        picked_in = sem("picked_in")
        rows_stored = [sem(f"rows_stored{i}") for i in range(2)]
        tokens_zeroed = sem("tokens_zeroed")
        mask_ready = sem("mask_ready")
        weight_steps = sem("weight_steps")
        counted_ps = sem("counted_ps")
        sort_steps = sem("sort_steps")
        tile_expert_steps = sem("tile_expert_steps")
        place_copied = sem("place_copied")
        carried = sem("carried")
        scattered = [sem(f"scattered{i}") for i in range(RING)]
        token_rows_in = sem("token_rows_in")
        tokens_turned = sem("tokens_turned")
        token_of_ready = sem("token_of_ready")
        shared_added = sem("shared_added")
        residual_added = sem("residual_added")
        partial_stored = [sem(f"partial_stored{i}") for i in range(2)]
        gather_col_ready = sem("gather_col_ready")
        tile_in = [sem(f"tile_in{i}") for i in range(RING)]
        tile_turned = sem("tile_turned")
        gate_up_split = sem("gate_up_split")
        gathered_high_ready = sem("gathered_high_ready")
        gathered_low_ready = sem("gathered_low_ready")
        tile_gate_ps = sem("tile_gate_ps")
        tile_up_ps = sem("tile_up_ps")
        tile_tanh = sem("tile_tanh")
        tile_gated = sem("tile_gated")
        tile_hidden_ready = sem("tile_hidden_ready")
        tile_hidden_turned = sem("tile_hidden_turned")
        tile_hidden_t_ready = sem("tile_hidden_t_ready")
        tile_down = sem("tile_down")
        tile_out_ready = sem("tile_out_ready")
        tile_stored = [sem(f"tile_stored{i}") for i in range(2)]
        scores_ready = sem("scores_ready")
        max_ready = sem("max_ready")
        probs_ready = sem("probs_ready")
        probs_turned = sem("probs_turned")
        taken_act = sem("taken_act")
        taken_dve = sem("taken_dve")
        pv_done = sem("pv_done")
        o_taken = sem("o_taken")
        o_rec_ready = sem("o_rec_ready")
        y_parts = sem("y_parts")
        y_t_ready = sem("y_t_ready")
        cproj_done = sem("cproj_done")
        tanh_ready = sem("tanh_ready")
        tanh_used = sem("tanh_used")
        hidden_ready = sem("hidden_ready")
        down_done = sem("down_done")
        block = ctx.enter_context(nc.Block())
        score_banks = (scores[0], scores[1], down_ps)

        def wait(eng, s, value):
            if not isinstance(value, int) or value > 0:
                eng.wait_ge(s, value)

        def stages(engine, step):
            for i in range(2 * RING):
                step(i, i % RING, i // RING)
            with engine.Fori(2, EXPERT_TILES // RING - 1) as turn:
                for c in range(RING):
                    step(turn * RING + c, c, turn)
            for i in range((EXPERT_TILES // RING - 1) * RING, EXPERT_TILES + LAGS):
                step(i, i % RING, i // RING)

        def lagging(i, ring, turn, lag):
            if isinstance(i, int):
                return (i - lag, (i - lag) % RING, (i - lag) // RING) if 0 <= i - lag < EXPERT_TILES else None
            return i - lag, (ring - lag) % RING, turn + (ring - lag) // RING

        def experts_done(eng):
            for par in range(2):
                wait(eng, tile_stored[par], 16 * (EXPERT_TILES // 2))

        def batches(engine, batch):
            for b in range(2):
                batch(b, b, 0)
            with engine.Fori(1, B // 2) as pair:
                for par in range(2):
                    batch(pair * 2 + par, par, pair)

        def bodies(engine, body):
            body(Batch(0, 0))
            with engine.Fori(0, B // 2 - 1) as pair:
                for c in (1, 2):
                    body(Batch(pair, c))
            body(Batch(0, B - 1))
            body(Batch(0, B))

        def body_steps(n):
            return range(TAIL if n.known == B else UNITS)

        def taken(eng, b, u):
            if u < 0:
                b, u = b - 1, u + UNITS
            if on_act(u):
                wait(eng, taken_act, b * len(ACT_TAKES) + ACT_TAKES.index(u) + 1)
            else:
                wait(eng, taken_dve, b * len(DVE_TAKES) + DVE_TAKES.index(u) + 1)

        def take_probs(eng, copy, done, b, u):
            g, i, heads = UNIT[u]
            quad, n = g * NT + i, P * (i + 1)
            wait(eng, probs_turned, b * UNITS + u + 1)
            wait(eng, pv_done, b * G * NT + quad - 1)
            copy(probs_t[:, quad % 2, heads[0]:heads[-1] + 1, 0:n],
                 turned[u % 2][:, 0:len(heads) * n].rearrange("p (h n) -> p h n", n=n)).then_inc(done, 1)

        def filled(eng, what, i, b):
            s, count = {
                "k": (k_ps, 2 * (b * G + i) + 1), "k_turned": (k_ps, 2 * (b * G + i) + 2), "q": (q_ps, b * G + i + 1),
                "q_wqk": (q_wqk_ps, b * G + i + 1), "v": (v_ps, b + 1), "o_turned": (o_turned_ps, b * G + i + 1), "y": (y_ps, b + 1),
                "cproj": (cproj_done, b + 1)}[what]
            wait(eng, s, count)
            return work[bank_of(what, i)]

        def stacks_copied(eng, b, t):
            wait(eng, stack_in[t // HG], b * STACK_COPIES * 16)

        STACK_COPIES = 2 * GH * 4

        CONST_LOADS = (
            (attn_rows[:], attn_w.rearrange("a p c -> p a c")), (bdq[:], bd_q), (bdkv[:], bd_kv), (bdqk[:], bd_qk),
            (bdo[:], bd_o.rearrange("(g p) c -> p g c", p=P)), (cproj_w[:], cproj), (bias_cols[:], biases),
            (out_bias_rows[:], out_bias.to_broadcast([P, C])), (wr[:], router_w), (rb[:], router_b.to_broadcast([P, ROUTED])),
            (rank[:], ranks.to_broadcast([P, ROUTED])), (identity[:], ident), (mask_f[:], mask),
            (rot_sb[:], rot), (rot_t_sb[:], rot_t), (cos_sb[:], cos), (sin_sb[:], sin),
            (earlier[:], before), (tokens[:], token_no), (tile_numbers[:], tile_no), (tile_starts[:], tile_start.to_broadcast([P, TILES])),
        )
        PREP_COLUMNS = 12
        PREP_SPREAD = 15
        PREP_ALL = 16

        @block.sync
        def _(sp):
            n = TILES // len(x_in)
            for c, loaded in enumerate(x_in):
                sp.dma_start(x_all[:, c * n:(c + 1) * n, :], x_tiles[:, c * n:(c + 1) * n, :]).then_inc(loaded, 16)
            for dst, src in CONST_LOADS:
                sp.dma_start(dst, src).then_inc(consts_in, 16)
            sp.dma_start(gate_up_w[:], gate_up.rearrange("a p n -> p a n")).then_inc(weights_in, 16)
            for n, (first, m) in enumerate(CHUNKS):
                sp.dma_start(down_w[0:m, :, n, :], down[:, first:first + m, :].rearrange("e p c -> p e c")).then_inc(down_in, 16)

            def store_xn(b, par, turn):
                rows = normed_by_batch[bass.ds(b, 1)].rearrange("a p t c -> p (a t) c")
                wait(sp, xn_ready, (b + 1) * NT)
                sp.dma_start(rows, xn[:, par]).then_inc(rows_stored[par], 16)
                wait(sp, xn_t_ready, b + 1)
                sp.dma_start(xn_dram[bass.ds(b, 1)].rearrange("a p n -> p (a n)"), xn_t[:, par, :]).then_inc(xn_stored[par], 16)

            sp.wait_ge(tokens_zeroed, 1)
            sp.dma_start(sorted_tokens.rearrange("(p n) a -> p (n a)", p=P), zero_tokens[:]).then_inc(tokens_zeroed, 16)
            batches(sp, store_xn)
            for par in range(2):
                sp.wait_ge(xn_stored[par], 16 * (B // 2))
                sp.wait_ge(rows_stored[par], 16 * (B // 2))

            def load_shared(b, par, turn):
                src = xn_dram[bass.ds(b, 1)].rearrange("a p n -> p (a n)")
                wait(sp, up_ps, (b - 1) * len(CHUNKS))
                sp.dma_start(xb[:, par, :], src).then_inc(xb_in[par], 16)

            def store_partial(b, par, turn):
                dst = partial[bass.ds(b, 1)].rearrange("a p n -> p (a n)")
                wait(sp, residual_added, b + 1)
                sp.dma_start(dst, acc[:, par].rearrange("p t c -> p (t c)")).then_inc(partial_stored[par], 16)

            load_shared(0, 0, 0)
            load_shared(1, 1, 0)
            with sp.Fori(0, B // 2 - 1) as pair:
                for par in range(2):
                    store_partial(pair * 2 + par, par, pair)
                    load_shared(pair * 2 + par + 2, par, pair + 1)
            for par in range(2):
                store_partial(B - 2 + par, par, B // 2 - 1)

            for done in scattered:
                sp.wait_ge(done, 2 * 16 * (TILES // RING))
            by_tile = sorted_tokens.rearrange("(n p) a -> n (p a)", p=P)
            sp.dma_start(token_rows[:, 0, :], by_tile[0:P]).then_inc(token_rows_in, 16)
            sp.dma_start(token_rows[0:EXPERT_TILES - P, 1, :], by_tile[P:EXPERT_TILES]).then_inc(token_rows_in, 16)

            def store_tile(i, ring, turn):
                mine = lagging(i, ring, turn, LAGS)
                if mine:
                    i, ring, turn = mine
                    dst = expert_out[bass.ds(i * P, P)]
                    wait(sp, tile_out_ready, i + 1)
                    sp.dma_start(dst, tile_out[:, ring % 2, :]).then_inc(tile_stored[ring % 2], 16)

            stages(sp, store_tile)
            experts_done(sp)
            for par in range(2):
                sp.wait_ge(partial_stored[par], 16 * (B // 2))

            def load_xb(n, off):
                src = xn_dram[bass.ds(n.b + off, 1)].rearrange("a p n -> p (a n)")
                wait(sp, k_ps, 2 * (n.b + off - 1) * G)
                sp.dma_start(xb[:, n.par(off), :], src).then_inc(xb_in[n.par(off)], 16)

            def load_acc(n, off):
                src = partial[bass.ds(n.b + off, 1)].rearrange("a p n -> p (a n)")
                if off and n.exists(off - 2):
                    wait(sp, stored[n.par(off)], n.alike(off - 2) * 16)
                sp.dma_start(acc[:, n.par(off)].rearrange("p t c -> p (t c)"), src).then_inc(acc_in[n.par(off)], 16)

            counts = [nc.sync.alloc_register(f"count{i}") for i in range(4)]

            def counted(value, reg):
                if isinstance(value, int):
                    return value
                nc.sync.reg_mov(counts[reg], value)
                return nc.sync.snap(counts[reg])

            def copy_stacks(half, read, split, keys_first=False):
                keys = (k_low_ready, k_stack, (k_high, k_low, k_high, k_low))
                queries = (q_low_ready, q_stack, (q_high, q_high, q_low, q_low))
                wait(sp, scores_ready, read)
                if not keys_first:
                    wait(sp, k_low_ready, split)
                for split_done, stack, parts in ((keys, queries) if keys_first else (queries, keys)):
                    if keys_first or stack is q_stack:
                        wait(sp, split_done, split)
                    for r in range(GH):
                        for n, part in enumerate(parts):
                            sp.dma_start(stack[n * LAT:(n + 1) * LAT, half, r].bitcast(F32),
                                         part[r * LAT:(r + 1) * LAT, half * HG:(half + 1) * HG].bitcast(F32)).then_inc(stack_in[half], 16)

            def store_out(n, off):
                dst = out_tiles[bass.ds(n.b + off, 1)].rearrange("a p t c -> p (a t) c")
                wait(sp, attention_added, n.b + off + 1)
                sp.dma_start(dst, acc[:, n.par(off)]).then_inc(stored[n.par(off)], 16)

            def body(n):
                b = n.b
                read_low = counted(b * UNITS, 0)
                split_low = counted((b + 1) * G, 1)
                read_high = counted(b * UNITS + HALF_UNITS, 2)
                split_high = counted((b + 1) * G + HG, 3)
                if n.exists(1):
                    load_xb(n, 1)
                if n.exists():
                    copy_stacks(1, read_low, split_low)
                if n.exists(-1):
                    store_out(n, -1)
                if n.exists(1):
                    load_acc(n, 1)
                    copy_stacks(0, read_high, split_high)

            first = Batch(0, 0)
            load_xb(first, 0)
            load_acc(first, 0)
            copy_stacks(0, 0, HG, keys_first=True)
            bodies(sp, body)
            for par in range(2):
                sp.wait_ge(stored[par], 16 * (B // 2))

        @block.gpsimd
        def _(pool):
            pool.memset(values[:], 0.0).then_inc(zeroed, 1)
            pool.wait_ge(zeroed, 1)
            pool.memset(values[:, :, :, SUM:SUM + 1], 1.0).then_inc(zeroed, 1)
            pool.memset(zero_tokens[:], 0.0).then_inc(tokens_zeroed, 1)
            pool.memset(carrier[:], 0.0).then_inc(carried, 1)
            pool.memset(tile_hidden[:], 0.0).then_inc(zeroed, 1)

            def carry(count, *waits):
                wait(pool, carried, count + 1)
                for s, value in waits:
                    wait(pool, s, value)
                pool.tensor_tensor(carrier[:, 0:1], carrier[:, 0:1], carrier[:, 1:2], ALU.add).then_inc(carried, 1)

            pool.wait_ge(gate_up_split, 2)
            for which in range(2):
                w = gate_up_w[:, which, 0:ROUTED * I]
                pool.tensor_tensor(w.bitcast(F32R), w, gate_up_high[:, which, :].bitcast(F32), ALU.subtract).then_inc(gate_up_split, 1)

            pool.wait_ge(tokens_zeroed, 1 + 16)

            def scatter(t, ring, turn):
                carry(t, (place_copied, 2 * t + 2))
                for choice in range(2):
                    pool.indirect_dma_start(sorted_tokens, bass.IndirectOffsetOnAxis(ap=place_cols[:, ring, choice:choice + 1], axis=0),
                                            token_col[:, ring:ring + 1], None).then_inc(scattered[ring], 16)

            with pool.Fori(0, TILES // RING) as turn:
                for ring in range(RING):
                    scatter(turn * RING + ring, ring, turn)

            for par in range(2):
                pool.wait_ge(rows_stored[par], 16 * (B // 2))

            def gather(i, ring, turn):
                if isinstance(i, int) and i >= EXPERT_TILES:
                    return
                carry(i + TILES, (gather_col_ready, i + 1), (tile_turned, i - RING + 1))
                pool.indirect_dma_start(gathered[:, ring, :], None, normed,
                                        bass.IndirectOffsetOnAxis(ap=gather_col[:, ring:ring + 1], axis=0)).then_inc(tile_in[ring], 16)

            stages(pool, gather)
            experts_done(pool)

            def tokens_low(n, off):
                par = n.par(off)
                wait(pool, xb_high_ready, n.b + off + 1)
                pool.tensor_tensor(xb_low[:, par, :], xb[:, par, :], xb_high[:, par, :].bitcast(F32), ALU.subtract).then_inc(xb_low_ready, 1)

            def pick(n):
                carry(n.b + TILES + EXPERT_TILES, (now_ready, n.b + 1), (expert_added, n.b * 2 * NT))
                for choice in range(2):
                    for t in range(NT):
                        pool.indirect_dma_start(picked[:, choice, t, :], None, expert_out,
                                                bass.IndirectOffsetOnAxis(ap=place_now[:, choice, t:t + 1], axis=0)).then_inc(picked_in, 16)

            def key_tile(b, t):
                wait(pool, k_parts, 2 * (b * G + t + 1))
                pool.tensor_tensor(k_lat[:], k_lat[:], k_sin[:], ALU.add).then_inc(k_ready, 1)
                wait(pool, k_high_ready, b * G + t + 1)
                pool.tensor_tensor(k_low[:, t, :], k_lat[:], k_high[:, t, :].bitcast(F32), ALU.subtract).then_inc(k_low_ready, 1)

            def query_tile(b, t):
                wait(pool, q_high_ready, b * G + t + 1)
                pool.tensor_tensor(q_low[:, t, :], q_lat[:, t % 2, :], q_high[:, t, :].bitcast(F32), ALU.subtract).then_inc(q_low_ready, 1)

            def split(b):
                for what, t, _ in PROJECT:
                    if what == "q_wqk":
                        query_tile(b, t)
                    elif what == "k_turned":
                        key_tile(b, t)

            def body(n):
                if n.exists(1):
                    tokens_low(n, 1)
                if n.exists():
                    pick(n)
                if n.exists(1):
                    split(n.b + 1)

            tokens_low(Batch(0, 0), 0)
            split(0)
            bodies(pool, body)

        @block.scalar
        def _(act):
            A = nc.scalar
            act.wait_ge(rstd_steps, 1)
            A.activation(spread[:, 1, :], spread[:, 0, :], ACT.Sqrt).then_inc(std_done, 1)

            def take_xn(b, par, turn):
                wait(act, xn_turned, b + 1)
                wait(act, logits_ps, b - 1)
                wait(act, xn_stored[par], turn * 16)
                A.copy(xn_t[:, par, :], work[par][:]).then_inc(xn_t_ready, 1)

            batches(act, take_xn)
            act.wait_ge(route_steps, GAP_STEP)
            A.activation(tops[:, 3, :], tops[:, 2, :], ACT.Exp).then_inc(gap_exp, 1)

            act.wait_ge(weights_in, 16)
            for which in range(2):
                A.copy(gate_up_high[:, which, :], gate_up_w[:, which, 0:ROUTED * I]).then_inc(gate_up_split, 1)

            def shared(b, par, turn):
                for k, (_, m) in enumerate(CHUNKS):
                    n = b * len(CHUNKS) + k
                    wait(act, gate_ps, n + 1)
                    wait(act, down_done, n - 2)
                    A.activation(hidden[0:m, k, :], scores[(par * len(CHUNKS) + k) % 2][0:m, :], ACT.Tanh,
                                 scale=0.5).then_inc(tanh_ready, 1)

            batches(act, shared)
            act.wait_ge(prep_done, PREP_ALL)
            for n, w in enumerate((w_k, w_k_turned, w_q)):
                A.copy(w_high[:, n, :], w[:]).then_inc(w_high_ready, 1)

            act.wait_ge(zeroed, 3)

            def tile_stages(i, ring, turn):
                mine = lagging(i, ring, turn, 0)
                if mine:
                    j, c, _ = mine
                    wait(act, tile_turned, j + 1)
                    wait(act, tile_up_ps, j - 1)
                    A.copy(gathered_high[:, c % 2, :], turned[c % 2][:, 0:P]).then_inc(gathered_high_ready, 1)
                mine = lagging(i, ring, turn, 1)
                if mine:
                    j, c, _ = mine
                    wait(act, tile_gate_ps, j + 1)
                    wait(act, tile_hidden_turned, j - 1)
                    A.activation(tile_hidden[:, c % 2, 0:I], scores[c % 2][:, 0:I], ACT.Tanh, scale=0.5).then_inc(tile_tanh, 1)
                mine = lagging(i, ring, turn, 2)
                if mine:
                    j, c, _ = mine
                    wait(act, tile_hidden_turned, j + 1)
                    wait(act, tile_down, j - 1)
                    A.copy(tile_hidden_t[:, c % 2].rearrange("p n t -> p (n t)"), o_ps[:, 0:len(CHUNKS) * P]).then_inc(tile_hidden_t_ready, 1)
                mine = lagging(i, ring, turn, 3)
                if mine:
                    j, c, turn = mine
                    wait(act, tile_down, j + 1)
                    wait(act, tile_stored[c % 2], (turn * (RING // 2) + c // 2) * 16)
                    A.copy(tile_out[:, c % 2, :], down_ps[:, 0:C]).then_inc(tile_out_ready, 1)

            stages(act, tile_stages)
            experts_done(act)

            def tokens_high(n, off):
                wait(act, xb_in[n.par(off)], (B // 2 + n.alike(off)) * 16)
                wait(act, k_ps, 2 * (n.b + off - 1) * G)
                A.copy(xb_high[:, n.par(off), :], xb[:, n.par(off), :]).then_inc(xb_high_ready, 1)

            def split_high(b, what, t):
                lat, high, ready, done = (k_lat, k_high, k_ready, k_high_ready) if what == "k_turned" else (q_lat, q_high, q_ready, q_high_ready)
                wait(act, ready, b * G + t + 1)
                stacks_copied(act, b, t)
                A.copy(high[:, t, :], lat[:] if what == "k_turned" else lat[:, t % 2, :]).then_inc(done, 1)

            def body(n):
                b = n.b
                if n.exists(1):
                    tokens_high(n, 1)
                for s in body_steps(n):
                    off, u = n.back(s - TURN_LAG)
                    if n.exists(off) and on_act(u):
                        take_probs(act, A.copy, taken_act, b + off, u)
                    if n.exists():
                        _, i, heads = UNIT[s]
                        wait(act, max_ready, b * UNITS + s + 1)
                        wait(act, probs_turned, b * UNITS + s - PROBS + 1)
                        for k in range(len(heads)):
                            cols = slice(k * PAIRED, k * PAIRED + (i + 1) * P)
                            last = A.activation(probs[:, s % PROBS, cols], score_banks[score_bank(s)][:, cols], ACT.Exp,
                                                bias=neg_max[:, s % 8, k:k + 1])
                        last.then_inc(probs_ready, 1)
                    for what, t, off in PLAN.get(s - SPLIT_LAG, ()):
                        if n.exists(off) and what in ("k_turned", "q_wqk"):
                            split_high(b + off, what, t)
                    end = group_end(s)
                    if end is not None and n.exists(end[0]):
                        off, g = end
                        wait(act, pv_done, (b + off) * G * NT + NT * (g + 1))
                        wait(act, o_turned_ps, (b + off) * G + g - 1)
                        A.copy(o_sb[:, g % 2, :], o_ps[:]).then_inc(o_taken, 1)

            tokens_high(Batch(0, 0), 0)
            for what, t, _ in PROJECT:
                if what in ("k_turned", "q_wqk"):
                    split_high(0, what, t)
            bodies(act, body)

        @block.vector
        def _(dve):
            V = nc.vector

            for c, loaded in enumerate(x_in):
                dve.wait_ge(loaded, 16)
                n = TILES // len(x_in)
                with dve.Fori(c * n // NT, (c + 1) * n // NT) as b:
                    for t in range(NT):
                        tile = bass.ds(b * NT + t, 1)
                        V.bn_stats(stats[:, tile, :].rearrange("p a n -> p (a n)"),
                                   x_all[:, tile, :].rearrange("p a n -> p (a n)")).then_inc(stats_done, 1)
            dve.wait_ge(stats_done, TILES)
            even, odd, even_sq, odd_sq = (stats[:, :, n:n + 1].rearrange("p n a -> p (n a)") for n in (1, 4, 2, 5))
            both, apart, summed, varied = (spread[:, n, :] for n in (1, 2, 3, 0))
            V.tensor_tensor(both, even, odd, ALU.add).then_inc(mean_steps, 1)
            V.tensor_tensor(apart, even, odd, ALU.subtract).then_inc(mean_steps, 1)
            V.tensor_tensor(summed, even_sq, odd_sq, ALU.add).then_inc(mean_steps, 1)
            dve.wait_ge(mean_steps, 3)
            V.tensor_scalar(mean[:], both, 0.5, None, ALU.mult).then_inc(mean_steps, 1)
            V.scalar_tensor_tensor(apart, apart, 0.25, apart, ALU.mult, ALU.mult).then_inc(mean_steps, 1)
            V.tensor_scalar(summed, summed, 1.0 / C, EPS, ALU.mult, ALU.add).then_inc(mean_steps, 1)
            dve.wait_ge(mean_steps, 6)
            V.tensor_tensor(varied, summed, apart, ALU.add).then_inc(rstd_steps, 1)

            dve.wait_ge(std_done, 1)
            steps = (
                lambda: V.reciprocal(spread[:, 2, :], spread[:, 1, :]),
                lambda: V.tensor_tensor(spread[:, 3, :], spread[:, 2, :], spread[:, 2, :], ALU.mult),
                lambda: V.scalar_tensor_tensor(spread[:, 1, :], spread[:, 3, :], -0.5, spread[:, 0, :], ALU.mult, ALU.mult),
                lambda: V.scalar_tensor_tensor(rstd[:], spread[:, 1, :], 1.5, spread[:, 2, :], ALU.add, ALU.mult),
            )
            for n, step in enumerate(steps):
                step().then_inc(rstd_steps, 1)
                dve.wait_ge(rstd_steps, n + 2)

            def norm(b, par, turn):
                wait(dve, xn_turned, b - 1)
                wait(dve, rows_stored[par], turn * 16)
                for t in range(NT):
                    tile = bass.ds(b * NT + t, 1)
                    V.tensor_scalar(xn[:, par, t, :], x_all[:, tile, :].rearrange("p a n -> p (a n)"),
                                    mean[:, tile], rstd[:, tile],
                                    ALU.subtract, ALU.mult).then_inc(xn_ready, 1)

            def take_logits(b, par):
                wait(dve, logits_ps, b + 1)
                V.tensor_tensor(logits[:, bass.ds(b * NT, NT), :], turned[par][:, 0:NT * 8].rearrange("p (t e) -> p t e", e=8)[:, :, 0:ROUTED],
                                rb[:].unsqueeze(1).to_broadcast([P, NT, ROUTED]), ALU.add).then_inc(logits_taken, 1)

            dve.wait_ge(consts_in, 16 * len(CONST_LOADS))
            norm(0, 0, 0)
            norm(1, 1, 0)
            with dve.Fori(0, B // 2 - 1) as pair:
                for par in range(2):
                    norm(pair * 2 + par + 2, par, pair + 1)
                    take_logits(pair * 2 + par, par)
            for par in range(2):
                take_logits(B - 2 + par, par)

            def over(a):
                return a.unsqueeze(2).to_broadcast([P, TILES, ROUTED])

            def chained(done, steps):
                for n, step in enumerate(steps):
                    step().then_inc(done, 1)
                    dve.wait_ge(done, n + 1)

            ranks_b = rank[:].unsqueeze(1).to_broadcast([P, TILES, ROUTED])
            top = [tops[:, n, :] for n in range(8)]
            r = [rt[:, n] for n in range(4)]
            V.memset(ones[:], 1.0).then_inc(mask_ready, 1)
            dve.wait_ge(logits_taken, B)
            chained(route_steps, (
                lambda: V.tensor_reduce(top[0], logits[:], X_AXIS, ALU.max),
                lambda: V.tensor_tensor(r[0], logits[:], over(top[0]), ALU.is_equal),
                lambda: V.tensor_tensor(r[1], r[0], ranks_b, ALU.mult),
                lambda: V.tensor_reduce(top[1], r[1], X_AXIS, ALU.max),
                lambda: V.tensor_tensor(r[2], r[1], over(top[1]), ALU.is_equal),
                lambda: V.scalar_tensor_tensor(r[3], r[2], -3e38, logits[:], ALU.mult, ALU.add),
                lambda: V.tensor_reduce(top[4], r[3], X_AXIS, ALU.max),
                lambda: V.tensor_tensor(top[2], top[4], top[0], ALU.subtract),
                lambda: V.tensor_tensor(r[0], r[3], over(top[4]), ALU.is_equal),
                lambda: V.tensor_tensor(r[1], r[0], ranks_b, ALU.mult),
                lambda: V.tensor_reduce(top[5], r[1], X_AXIS, ALU.max),
                lambda: V.tensor_tensor(r[3], r[1], over(top[5]), ALU.is_equal),
            ))
            V.tensor_tensor(r[0], r[2], r[3], ALU.add).then_inc(mask_ready, 1)
            dve.wait_ge(gap_exp, 1)
            first_weight, second_weight = (pair_weight[:, n, :] for n in range(2))
            chained(weight_steps, (
                lambda: V.tensor_scalar(top[1], top[3], 1.0, None, ALU.add),
                lambda: V.reciprocal(first_weight, top[1]),
                lambda: V.tensor_tensor(second_weight, top[3], first_weight, ALU.mult),
            ))

            earlier_in_tile, in_tile = (work[n][:, 0:TILES * ROUTED].rearrange("p (t e) -> p t e", e=ROUTED) for n in range(2))
            by_expert = r[1].rearrange("p t e -> p (t e)").rearrange("p (e t) -> p e t", e=ROUTED)
            s = [starts[:, n, :] for n in range(5)]
            counts = sums[:, 0, TILES - 1, :]
            steps = [lambda: V.tensor_copy(sums[:, 0], in_tile)]
            for n in range(TILES.bit_length() - 1):
                k, src, dst = 1 << n, sums[:, n % 2], sums[:, 1 - n % 2]
                steps += [lambda k=k, src=src, dst=dst: V.tensor_copy(dst[:, 0:k, :], src[:, 0:k, :]),
                          lambda k=k, src=src, dst=dst: V.tensor_tensor(dst[:, k:, :], src[:, k:, :], src[:, 0:TILES - k, :], ALU.add)]
            steps += [
                lambda: V.tensor_tensor(places[:], sums[:, 0], in_tile, ALU.subtract),
                lambda: V.tensor_tensor(places[:], places[:], earlier_in_tile, ALU.add),
                lambda: V.tensor_tensor(by_expert, counts.unsqueeze(2).to_broadcast([P, ROUTED, TILES]),
                                        tile_starts[:].unsqueeze(1).to_broadcast([P, ROUTED, TILES]), ALU.is_gt),
                lambda: V.tensor_reduce(s[0], by_expert, X_AXIS, ALU.add),
                lambda: V.memset(s[1][:, 0:1], 0.0),
                lambda: V.tensor_copy(s[1][:, 1:], s[0][:, 0:ROUTED - 1]),
            ]
            for n, k in enumerate((1, 2, 4)):
                src, dst = s[n + 1], s[n + 2]
                steps += [lambda k=k, src=src, dst=dst: V.tensor_copy(dst[:, 0:k], src[:, 0:k]),
                          lambda k=k, src=src, dst=dst: V.tensor_tensor(dst[:, k:], src[:, k:], src[:, 0:ROUTED - k], ALU.add)]
            starts_b = s[4].unsqueeze(1).to_broadcast([P, TILES, ROUTED])
            steps += [
                lambda: V.scalar_tensor_tensor(places[:], starts_b, float(P), places[:], ALU.mult, ALU.add),
                lambda: V.tensor_tensor(r[1], r[2], places[:], ALU.mult),
                lambda: V.tensor_reduce(top[4], r[1], X_AXIS, ALU.add),
                lambda: V.tensor_tensor(r[1], r[3], places[:], ALU.mult),
                lambda: V.tensor_reduce(top[5], r[1], X_AXIS, ALU.add),
                lambda: V.tensor_copy(place[:], tops[:, 4:6, :]),
            ]
            dve.wait_ge(counted_ps, 1)
            chained(sort_steps, steps)
            expert_steps = (
                lambda: V.tensor_tensor(of_tile[:], tile_numbers[:].unsqueeze(2).to_broadcast([1, EXPERT_TILES, ROUTED]),
                                        s[4][0:1].unsqueeze(1).to_broadcast([1, EXPERT_TILES, ROUTED]), ALU.is_ge),
                lambda: V.tensor_reduce(of_tile_sum[:], of_tile[:], X_AXIS, ALU.add),
                lambda: V.tensor_scalar(weight_cols_f[:, 0, :], of_tile_sum[:], -1.0, float(I), ALU.add, ALU.mult),
                lambda: V.tensor_scalar(weight_cols_f[:, 1, :], of_tile_sum[:], -1.0, float(len(CHUNKS) * C), ALU.add, ALU.mult),
                lambda: V.tensor_copy(weight_cols[:], weight_cols_f[:]),
            )

            def residual(b, par, turn):
                flat = acc[:, par].rearrange("p t c -> p (t c)")
                wait(dve, down_done, (b + 1) * len(CHUNKS))
                wait(dve, partial_stored[par], turn * 16)
                V.tensor_tensor(flat, (o_ps, down_ps)[par][:], x_all[:, bass.ds(b * NT, NT), :].rearrange("p t c -> p (t c)"),
                                ALU.add).then_inc(shared_added, 1)
                wait(dve, shared_added, b + 1)
                V.tensor_tensor(acc[:, par], acc[:, par], out_add[:].unsqueeze(1).to_broadcast([P, NT, C]),
                                ALU.add).then_inc(residual_added, 1)

            def give_places(b):
                for ring in range(RING):
                    tile = bass.ds(b * NT + ring, 1)
                    wait(dve, scattered[ring], b * 2 * 16)
                    V.tensor_copy(place_cols[:, ring:ring + 1, :].rearrange("p r c -> p c r"), place[:, :, tile]).then_inc(place_copied, 1)
                    V.tensor_copy(token_col[:, ring:ring + 1], tokens[:, tile]).then_inc(place_copied, 1)
            def combine_weights():
                dve.wait_ge(consts_in, 16 * len(CONST_LOADS))
                V.tensor_copy(identity_bf[:], identity[:]).then_inc(prep_done, 1)
                V.tensor_copy(mask_bf[:], mask_f[:]).then_inc(prep_done, 1)
                dve.wait_ge(prep_products, 1)
                V.tensor_copy(w_k[:], scores[0][:]).then_inc(prep_done, 1)
                pairs = scores[0][:].rearrange("p (n two) -> p n two", two=2)
                pairs_out = w_k_turned[:].rearrange("p (n two) -> p n two", two=2)
                V.tensor_scalar(pairs_out[:, :, 0:1], pairs[:, :, 1:2], -1.0, None, ALU.mult).then_inc(prep_done, 1)
                V.tensor_copy(pairs_out[:, :, 1:2], pairs[:, :, 0:1]).then_inc(prep_done, 1)
                dve.wait_ge(prep_products, 2)
                V.tensor_copy(w_q[:], scores[1][:]).then_inc(prep_done, 1)
                dve.wait_ge(prep_products, 3)
                V.tensor_copy(w_v_lat[:].rearrange("p g c -> p (g c)"), turned[0][:]).then_inc(prep_done, 1)
                dve.wait_ge(prep_products, 4)
                V.tensor_copy(w_qk_turned[:], turned[1][:, 0:P]).then_inc(prep_done, 1)
                dve.wait_ge(prep_products, 5)
                for n, (col, bias) in enumerate(((q_col, 0), (k_col, 1), (v_col, 3))):
                    V.tensor_scalar(col[:], o_ps[:, G * n:G * n + G], bias_cols[:, bias:bias + 1], None, ALU.add).then_inc(prep_done, 1)
                V.memset(o_spread[:], 0.0).then_inc(prep_done, 1)
                dve.wait_ge(prep_products, 6)
                V.tensor_copy(k_col_turned[:], down_ps[:, 0:G]).then_inc(prep_done, 1)
                V.tensor_copy(w_v[:], work[0][:, 0:C]).then_inc(prep_done, 1)
                V.tensor_scalar(o_col[:], work[1][:, 0:1], bias_cols[:, 4:5], None, ALU.add).then_inc(o_col_ready, 1)
                dve.wait_ge(o_col_ready, 1)
                dve.wait_ge(prep_done, PREP_COLUMNS)
                V.tensor_scalar(o_spread[:], o_spread[:], o_col[:], None, ALU.add).then_inc(prep_done, 1)
                dve.wait_ge(prep_products, 7)
                V.tensor_tensor(out_add[:], turned[0][:, 0:C], out_bias_rows[:], ALU.add).then_inc(prep_done, 1)
                dve.wait_ge(down_in, 16 * len(CHUNKS))
                for n, (_, m) in enumerate(CHUNKS):
                    part = down_w[0:m, :, n, :]
                    V.tensor_scalar(part, part, 0.5, None, ALU.mult).then_inc(down_halved, 1)

            def shared(b, par, turn):
                if isinstance(b, int) and b == 0:
                    give_places(0)
                    combine_weights()
                    chained(tile_expert_steps, expert_steps)
                    give_places(1)
                elif not (isinstance(b, int) and b == 1):
                    give_places(b)
                for k, (_, m) in enumerate(CHUNKS):
                    n, bank = b * len(CHUNKS) + k, (par * len(CHUNKS) + k) % 2
                    h = hidden[0:m, k, :]
                    wait(dve, tanh_ready, n + 1)
                    V.scalar_tensor_tensor(h, h, 1.0, scores[bank][0:m, :], ALU.add, ALU.mult).then_inc(tanh_used, 1)
                    wait(dve, tanh_used, n + 1)
                    wait(dve, up_ps, n + 1)
                    V.tensor_tensor(h, h, turned[bank][0:m, :], ALU.mult).then_inc(hidden_ready, 1)
                    if k == 0 and not (isinstance(b, int) and b == 0):
                        residual(b - 1, 1 - par, turn - 1 + par)

            assert RING == NT
            dve.wait_ge(weights_in, 16)
            batches(dve, shared)
            residual(B - 1, 1, B // 2 - 1)

            dve.wait_ge(w_high_ready, 3)
            for n, w in enumerate((w_k, w_k_turned, w_q)):
                V.tensor_tensor(w_low[:, n, :], w[:], w_high[:, n, :].bitcast(F32), ALU.subtract).then_inc(w_low_ready, 1)

            dve.wait_ge(tokens_turned, 1)
            V.tensor_copy(token_of[:], work[0][:, 0:EXPERT_TILES]).then_inc(token_of_ready, 1)
            dve.wait_ge(token_of_ready, 1)

            def gather_cols(mine):
                j, c, turn = mine
                wait(dve, tile_in[c], turn * 16)
                V.tensor_copy(gather_col[:, c:c + 1], token_of[:, bass.ds(j, 1)]).then_inc(gather_col_ready, 1)

            def tile_stages(i, ring, turn):
                mine = lagging(i, ring, turn, -3)
                if mine:
                    gather_cols(mine)
                mine = lagging(i, ring, turn, 0)
                if mine:
                    j, c, _ = mine
                    wait(dve, gathered_high_ready, j + 1)
                    V.tensor_tensor(gathered_low[:, c % 2, :], turned[c % 2][:, 0:P], gathered_high[:, c % 2, :].bitcast(F32),
                                    ALU.subtract).then_inc(gathered_low_ready, 1)
                mine = lagging(i, ring, turn, 1)
                if mine:
                    j, c, _ = mine
                    h = tile_hidden[:, c % 2, 0:I]
                    wait(dve, tile_tanh, j + 1)
                    V.scalar_tensor_tensor(h, h, 1.0, scores[c % 2][:, 0:I], ALU.add, ALU.mult).then_inc(tile_gated, 1)
                    wait(dve, tile_gated, j + 1)
                    wait(dve, tile_up_ps, j + 1)
                    V.tensor_tensor(h, h, work[c % 2][:, 0:I], ALU.mult).then_inc(tile_hidden_ready, 1)

            for j in range(3):
                gather_cols((j, j, 0))
            stages(dve, tile_stages)
            experts_done(dve)

            def project(n, off, what, t):
                b = n.b + off
                if what == "k":
                    wait(dve, k_low_ready, b * G + t)
                    V.scalar_tensor_tensor(k_lat[:], filled(dve, what, t, b)[:], k_col[:, t:t + 1], cos_sb[:],
                                           ALU.add, ALU.mult).then_inc(k_parts, 1)
                elif what == "k_turned":
                    V.scalar_tensor_tensor(k_sin[:], filled(dve, what, t, b)[:], k_col_turned[:, t:t + 1], sin_sb[:],
                                           ALU.add, ALU.mult).then_inc(k_parts, 1)
                elif what == "q":
                    bank = filled(dve, what, t, b)
                    wait(dve, q_wqk_ps, b * G + t - 1)
                    for part, table in ((q_cos, cos_sb), (q_sin, sin_sb)):
                        V.scalar_tensor_tensor(part[:, t % 2, :], bank[:], q_col[:, t:t + 1], table[:],
                                               ALU.add, ALU.mult).then_inc(q_parts, 1)
                elif what == "q_wqk":
                    wait(dve, q_low_ready, b * G + t - 1)
                    V.tensor_scalar(q_lat[:, t % 2, :], filled(dve, what, t, b)[:], bias_cols[:, 2:3], SCALE,
                                    ALU.add, ALU.mult).then_inc(q_ready, 1)
                elif what == "v":
                    wait(dve, pv_done, (b - 1) * G * NT)
                    bank = filled(dve, what, t, b)[:].rearrange("p (n d) -> p n d", d=HD)
                    V.tensor_copy(values[:, n.par(off), :, 0:HD], bank).then_inc(values_ready, 1)

            def take_output(n, off, g):
                b = n.b + off
                o = filled(dve, "o_turned", g, b)[:].rearrange("p (t h l) -> p t h l", t=NT, h=GH)
                V.reciprocal(o_rec[:, g % 2].unsqueeze(3), o[:, :, :, SUM:SUM + 1]).then_inc(o_rec_ready, 1)
                wait(dve, o_rec_ready, b * G + g + 1)
                if g == 0:
                    wait(dve, y_ps, b)
                V.tensor_tensor(y_sb[:, :, g * GH * HD:(g + 1) * GH * HD].rearrange("p t (h d) -> p t h d", h=GH),
                                o[:, :, :, 0:HD], o_rec[:, g % 2].unsqueeze(3).to_broadcast([P, NT, GH, HD]),
                                ALU.mult).then_inc(y_parts, 1)

            def body(n):
                b = n.b
                if n.exists():
                    wait(dve, picked_in, b * 2 * NT * 16)
                    wait(dve, expert_added, b * 2 * NT)
                    V.tensor_copy(weight_now[:], pair_weight[:, :, bass.ds(b * NT, NT)]).then_inc(weight_ready, 1)
                    V.tensor_copy(place_now[:], place[:, :, bass.ds(b * NT, NT)]).then_inc(now_ready, 1)
                for s in body_steps(n):
                    for what, i, off in PLAN.get(s - 1, ()):
                        if not n.exists(off):
                            continue
                        if what == "o_turned":
                            take_output(n, off, i)
                        elif what == "y":
                            wait(dve, cproj_done, b + off)
                            V.tensor_copy(y_t[:], filled(dve, "y", 0, b + off)[:]).then_inc(y_t_ready, 1)
                        elif what == "cproj":
                            flat = acc[:, n.par(off)].rearrange("p t c -> p (t c)")
                            wait(dve, expert_added, (b + off + 1) * 2 * NT)
                            V.tensor_tensor(flat, filled(dve, what, i, b + off)[:], flat, ALU.add).then_inc(attention_added, 1)
                        else:
                            project(n, off, what, i)
                    if n.exists():
                        _, i, heads = UNIT[s]
                        wait(dve, scores_ready, b * UNITS + s + 1)
                        bank = score_banks[score_bank(s)]
                        if len(heads) == 1:
                            V.tensor_reduce(neg_max[:, s % 8, 0:1], bank[:, 0:(i + 1) * P], X_AXIS, ALU.max, negate=True).then_inc(max_ready, 1)
                        else:
                            V.tensor_reduce(neg_max[:, s % 8, :], bank[:].rearrange("p (h w) -> p h w", w=PAIRED)[:, :, 0:(i + 1) * P],
                                            X_AXIS, ALU.max, negate=True).then_inc(max_ready, 1)
                    off, u = n.back(s - TURN_LAG)
                    if n.exists(off) and not on_act(u):
                        take_probs(dve, V.tensor_copy, taken_dve, b + off, u)
                    if COMBINE_STEP <= s < COMBINE_STEP + 2 * NT and n.exists():
                        choice, t = divmod(s - COMBINE_STEP, NT)
                        mine = acc[:, n.par(), t, :]
                        wait(dve, weight_ready, b + 1)
                        wait(dve, picked_in, (b + 1) * 2 * NT * 16)
                        wait(dve, acc_in[n.par()], n.alike() * 16)
                        wait(dve, expert_added, b * 2 * NT + choice * NT + (t if choice else 0))
                        V.scalar_tensor_tensor(mine, picked[:, choice, t, :], weight_now[:, choice, t:t + 1], mine,
                                               ALU.mult, ALU.add).then_inc(expert_added, 1)

            first = Batch(0, 0)
            dve.wait_ge(zeroed, 2)
            for what, t, _ in PROJECT:
                project(first, 0, what, t)
            bodies(dve, body)

        @block.tensor
        def _(pe):
            M = nc.tensor

            pe.wait_ge(consts_in, 16 * len(CONST_LOADS))
            def turn_xn(b, par):
                wait(pe, xn_ready, (b + 1) * NT)
                wait(pe, xn_t_ready, b - 1)
                for t in range(NT):
                    last = M.transpose(work[par][:, t * P:(t + 1) * P], xn[:, par, t, :], identity[:])
                last.then_inc(xn_turned, 1)

            def route(b, par):
                wait(pe, xn_t_ready, b + 1)
                wait(pe, logits_taken, b - 1)
                for t in range(NT):
                    last = M.matmul(turned[par][:, t * 8:t * 8 + ROUTED], xn_t[:, par, t * P:(t + 1) * P], wr[:], start=True, stop=True)
                last.then_inc(logits_ps, 1)

            turn_xn(0, 0)
            turn_xn(1, 1)
            for b in range(2):
                route(b, b)
                turn_xn(b + 2, b)
            with pe.Fori(1, B // 2 - 1) as pair:
                for par in range(2):
                    route(pair * 2 + par, par)
                    turn_xn(pair * 2 + par + 2, par)
            for par in range(2):
                route(B - 2 + par, par)
            pe.wait_ge(xn_t_ready, B)
            pe.wait_ge(logits_taken, B)

            M.matmul(scores[0][:], attn_rows[:, 1, :], bdkv[:], start=True, stop=True).then_inc(prep_products, 1)
            M.matmul(scores[1][:], attn_rows[:, 0, :], bdq[:], start=True, stop=True).then_inc(prep_products, 1)
            for g in range(G):
                last = M.matmul(turned[0][:, g * C:(g + 1) * C], bdkv[:, g * P:(g + 1) * P], attn_rows[:, 2, :], start=True, stop=True)
            last.then_inc(prep_products, 1)
            M.matmul(turned[1][:, 0:P], rot_sb[:], bdqk[:], start=True, stop=True).then_inc(prep_products, 1)
            for n, (bd, bias) in enumerate(((bdq, 5), (bdkv, 6), (bdkv, 7))):
                for g in range(G):
                    last = M.matmul(o_ps[:, n * G + g:n * G + g + 1], bd[:, g * P:(g + 1) * P], bias_cols[:, bias:bias + 1],
                                    start=True, stop=True)
            last.then_inc(prep_products, 1)
            pe.wait_ge(mask_ready, 2)
            both = rt[:, 0].rearrange("p t e -> p (t e)")
            M.matmul(work[0][:, 0:TILES * ROUTED], earlier[:], both, start=True, stop=True)
            M.matmul(work[1][:, 0:TILES * ROUTED], ones[:], both, start=True, stop=True).then_inc(counted_ps, 1)
            pe.wait_ge(prep_done, PREP_COLUMNS)
            M.matmul(down_ps[:, 0:G], rot_t_sb[:], k_col[:], start=True, stop=True)
            for g in range(G):
                M.matmul(work[0][:, 0:C], w_v_lat[:, g, :], bdo[:, g, :], start=(g == 0), stop=(g == G - 1))
            for g in range(G):
                last = M.matmul(work[1][:, 0:1], bdo[:, g, :], v_col[:, g:g + 1], start=(g == 0), stop=(g == G - 1))
            last.then_inc(prep_products, 1)
            pe.wait_ge(prep_done, PREP_SPREAD)
            M.matmul(turned[0][:, 0:C], o_spread[:], cproj_w[:], start=True, stop=True).then_inc(prep_products, 1)
            pe.wait_ge(prep_done, PREP_ALL)
            pe.wait_ge(weights_in, 16)
            pe.wait_ge(down_halved, len(CHUNKS))

            def shared_down(b, par, k):
                n, m = b * len(CHUNKS) + k, CHUNKS[k][1]
                wait(pe, hidden_ready, n + 1)
                if k == 0:
                    wait(pe, shared_added, b - 1)
                for t in range(NT):
                    last = M.matmul((o_ps, down_ps)[par][:, t * C:(t + 1) * C], hidden[0:m, k, t * P:(t + 1) * P], down_w[0:m, ROUTED, k, :],
                                    start=(k == 0 and t == 0), stop=(k == len(CHUNKS) - 1), skip_group_check=True)
                last.then_inc(down_done, 1)

            def shared(b, par, turn):
                wait(pe, xb_in[par], 16 * (turn + 1))
                for k, (first, m) in enumerate(CHUNKS):
                    n, bank = b * len(CHUNKS) + k, (par * len(CHUNKS) + k) % 2
                    cols = slice(ROUTED * I + first, ROUTED * I + first + m)
                    wait(pe, tanh_used, n - 1)
                    M.matmul(scores[bank][0:m, :], gate_up_w[:, 0, cols], xb[:, par, :], start=True, stop=True).then_inc(gate_ps, 1)
                    wait(pe, hidden_ready, n - 1)
                    M.matmul(turned[bank][0:m, :], gate_up_w[:, 1, cols], xb[:, par, :], start=True, stop=True).then_inc(up_ps, 1)
                    if k > 0:
                        shared_down(b, par, k - 1)
                    elif not (isinstance(b, int) and b == 0):
                        shared_down(b - 1, 1 - par, len(CHUNKS) - 1)

            batches(pe, shared)
            shared_down(B - 1, 1, len(CHUNKS) - 1)

            pe.wait_ge(token_rows_in, 32)
            M.transpose(work[0][:, 0:P], token_rows[:, 0, :], identity[:])
            M.transpose(work[0][:, P:EXPERT_TILES], token_rows[0:EXPERT_TILES - P, 1, :],
                        identity[0:EXPERT_TILES - P, 0:EXPERT_TILES - P]).then_inc(tokens_turned, 1)
            pe.wait_ge(shared_added, B)
            pe.wait_ge(token_of_ready, 1)

            gate_up_low = gate_up_w[:].bitcast(F32R)
            pe.wait_ge(gate_up_split, 4)
            pe.wait_ge(tile_expert_steps, 5)
            down_flat = down_w[:].rearrange("p e n c -> p (e n c)")

            def expert_at(which, j):
                return pe.value_load(weight_cols[0:1, which, bass.ds(j, 1)], min_val=0, max_val=(ROUTED - 1) * (I, len(CHUNKS) * C)[which])

            def tile_stages(i, ring, turn):
                hidden_tile, out_tile = lagging(i, ring, turn, 1), lagging(i, ring, turn, 3)
                if hidden_tile:
                    gate_up_at = expert_at(0, hidden_tile[0])
                if out_tile:
                    down_at = expert_at(1, out_tile[0])
                mine = lagging(i, ring, turn, 0)
                if mine:
                    j, c, turn = mine
                    wait(pe, tile_in[c], 16 * (turn + 1))
                    M.transpose(turned[c % 2][:, 0:P], gathered[:, c, :], identity[:]).then_inc(tile_turned, 1)
                if hidden_tile:
                    j, c, _ = hidden_tile
                    wait(pe, gathered_low_ready, j + 1)
                    for which, bank, done in ((0, scores[c % 2], tile_gate_ps), (1, work[c % 2], tile_up_ps)):
                        w_high, w_low = gate_up_high[:, which, bass.ds(gate_up_at, I)], gate_up_low[:, which, bass.ds(gate_up_at, I)]
                        M.matmul(bank[:, 0:I], gathered_high[:, c % 2, :], w_high, start=True, stop=False)
                        M.matmul(bank[:, 0:I], gathered_high[:, c % 2, :], w_low, start=False, stop=False)
                        M.matmul(bank[:, 0:I], gathered_low[:, c % 2, :], w_high, start=False, stop=True).then_inc(done, 1)
                if out_tile:
                    j, c, _ = out_tile
                    wait(pe, tile_hidden_t_ready, j + 1)
                    wait(pe, tile_out_ready, j)
                    for n, (_, m) in enumerate(CHUNKS):
                        last = M.matmul(down_ps[:, 0:C], tile_hidden_t[0:m, c % 2, n, :],
                                        down_flat[0:m, bass.ds(down_at + n * C, C)],
                                        start=(n == 0), stop=(n == len(CHUNKS) - 1))
                    last.then_inc(tile_down, 1)
                mine = lagging(i, ring, turn, 2)
                if mine:
                    j, c, _ = mine
                    wait(pe, tile_hidden_ready, j + 1)
                    for n in range(len(CHUNKS)):
                        last = M.transpose(o_ps[:, n * P:(n + 1) * P], tile_hidden[:, c % 2, n * P:(n + 1) * P], identity[:])
                    last.then_inc(tile_hidden_turned, 1)

            stages(pe, tile_stages)
            experts_done(pe)
            pe.wait_ge(w_low_ready, 3)


            def bank(n, known, what, i, off):
                before = use_before(known, what, i, off)
                if before is not None:
                    w, j, o = before
                    b = n.b + o
                    s, count = {
                        "k": (k_parts, 2 * (b * G + j) + 1), "k_turned": (k_parts, 2 * (b * G + j) + 2),
                        "q": (q_parts, 2 * (b * G + j) + 2), "q_wqk": (q_ready, b * G + j + 1), "v": (values_ready, b + 1),
                        "o_turned": (y_parts, b * G + j + 1), "y": (y_t_ready, b + 1),
                        "cproj": (attention_added, b + 1)}[w]
                    wait(pe, s, count)
                return work[bank_of(what, i)]

            def project(n, known, what, i, off):
                b, par = n.b + off, n.par(off)
                if (what, i) == PROJECT[0][:2]:
                    wait(pe, xb_in[par], (B // 2 + n.alike(off)) * 16)
                    wait(pe, xb_low_ready, b + 1)
                out_ps = bank(n, known, what, i, off)
                if what in ("k", "k_turned", "q"):
                    w = ("k", "k_turned", "q").index(what)
                    high, low = (part[:, w, i * P:(i + 1) * P] for part in (w_high, w_low))
                    M.matmul(out_ps[:], high, xb_high[:, par, :], start=True, stop=False)
                    M.matmul(out_ps[:], high, xb_low[:, par, :], start=False, stop=False)
                    M.matmul(out_ps[:], low, xb_high[:, par, :], start=False, stop=True).then_inc(q_ps if what == "q" else k_ps, 1)
                elif what == "q_wqk":
                    wait(pe, q_parts, 2 * (b * G + i + 1))
                    M.matmul(out_ps[:], bdqk[:], q_cos[:, i % 2, :], start=True, stop=False)
                    M.matmul(out_ps[:], w_qk_turned[:], q_sin[:, i % 2, :], start=False, stop=True).then_inc(q_wqk_ps, 1)
                elif what == "v":
                    for t in range(NT):
                        last = M.matmul(out_ps[:, t * C:(t + 1) * C], xb[:, n.par(off), t * P:(t + 1) * P], w_v[:], start=True, stop=True)
                    last.then_inc(v_ps, 1)

            def score(b, u):
                g, i, heads = UNIT[u]
                half, t = divmod(g, HG)
                w = P * (i + 1)
                bank = score_banks[score_bank(u)]
                wait(pe, probs_ready, b * UNITS + u - 2)
                if u % HALF_UNITS == 0:
                    wait(pe, stack_in[half], (b + 1) * STACK_COPIES * 16)
                wide = max(w, 2 * P)
                for k, r in enumerate(heads):
                    at = k * PAIRED
                    M.matmul(bank[:, at:at + wide], q_stack[:, half, r, t, i * P:w], k_stack[:, half, r, t, 0:wide], start=True, stop=False)
                    last = M.matmul(bank[:, at + w - P:at + w], identity_bf[:], mask_bf[:], start=False, stop=True)
                last.then_inc(scores_ready, 1)

            def turn(b, u):
                _, i, heads = UNIT[u]
                wait(pe, probs_ready, b * UNITS + u + 1)
                taken(pe, b, u - 2)
                for k in range(len(heads)):
                    for j in range(i + 1):
                        to, at = (k * (i + 1) + j) * P, k * PAIRED + j * P
                        last = M.transpose(turned[u % 2][:, to:to + P], probs[:, u % PROBS, at:at + P], identity[:])
                last.then_inc(probs_turned, 1)

            def heads(n, off, g, i):
                b, quad = n.b + off, g * NT + i
                units = [u for u, unit in enumerate(UNIT) if unit[:2] == (g, i)]
                for mine in ([u for u in units if on_act(u)], [u for u in units if not on_act(u)]):
                    if mine:
                        taken(pe, b, mine[-1])
                if i == 0:
                    wait(pe, o_taken, b * G + g)
                if quad == 0:
                    wait(pe, values_ready, b + 1)
                for j in range(i + 1):
                    for r in range(GH):
                        last = M.matmul(o_ps[r * LAT:(r + 1) * LAT, i * P:(i + 1) * P], values[:, n.par(off), j * H + g * GH + r, :],
                                        probs_t[:, quad % 2, r, j * P:(j + 1) * P], start=(j == 0), stop=(j == i),
                                        skip_group_check=True)
                last.then_inc(pv_done, 1)

            def body(n):
                b = n.b
                for s in body_steps(n):
                    if n.exists():
                        score(b, s)
                    off, u = n.back(s - TURN_LAG)
                    if n.exists(off):
                        turn(b + off, u)
                    h = heads_at(s)
                    if h is not None and n.exists(h[0]):
                        heads(n, *h)
                    for what, i, off in PLAN.get(s, ()):
                        if not n.exists(off):
                            continue
                        if what == "o_turned":
                            wait(pe, o_taken, (b + off) * G + i + 1)
                            out_ps = bank(n, n.known, what, i, off)
                            for t in range(NT):
                                last = M.transpose(out_ps[:, t * P:(t + 1) * P], o_sb[:, i % 2, t * P:(t + 1) * P], identity[:])
                            last.then_inc(o_turned_ps, 1)
                        elif what == "cproj":
                            wait(pe, y_t_ready, b + off + 1)
                            out_ps = bank(n, n.known, what, i, off)
                            for t in range(NT):
                                last = M.matmul(out_ps[:, t * C:(t + 1) * C], y_t[:, t * P:(t + 1) * P], cproj_w[:], start=True, stop=True)
                            last.then_inc(cproj_done, 1)
                        elif what == "y":
                            wait(pe, y_parts, (b + off + 1) * G)
                            out_ps = bank(n, n.known, what, i, off)
                            for t in range(NT):
                                last = M.transpose(out_ps[:, t * P:(t + 1) * P], y_sb[:, t, :], identity[:])
                            last.then_inc(y_ps, 1)
                        else:
                            project(n, n.known, what, i, off)

            for what, t, _ in PROJECT:
                project(Batch(0, 0), "first", what, t, 0)
            bodies(pe, body)


def _blocks(a, n):
    out = np.zeros((a.shape[0] * n, a.shape[1] * n), a.dtype)
    for i in range(n):
        out[i * a.shape[0]:(i + 1) * a.shape[0], i * a.shape[1]:(i + 1) * a.shape[1]] = a
    return out


def _column(a, n):
    return np.tile(np.asarray(a), n).reshape(-1, 1)


def _tables():
    inv = (np.float32(1) / np.power(np.float32(10000), np.arange(0, LAT, 2, dtype=np.float32) / np.float32(LAT))).astype(np.float32)
    angles = np.repeat(np.outer(np.arange(T, dtype=np.float32), inv), 2, axis=1).T
    rot = np.zeros((P, P), np.float32)
    for i in range(0, P, 2):
        rot[i, i + 1], rot[i + 1, i] = -1, 1
    mask = np.where(np.tril(np.ones((P, P), bool)), 0, MASKED).astype(np.float32)
    ranks = np.arange(ROUTED, 0, -1, dtype=np.float32).reshape(1, ROUTED)
    return {"ident": np.eye(P, dtype=np.float32), "mask": mask, "rot": rot, "rot_t": np.ascontiguousarray(rot.T),
            "before": np.triu(np.ones((P, P), np.float32), 1),
            "token_no": np.arange(TILES * P, dtype=np.float32).reshape(TILES, P).T,
            "tile_no": np.arange(EXPERT_TILES, dtype=np.float32).reshape(1, -1),
            "tile_start": P * np.arange(TILES, dtype=np.float32).reshape(1, -1),
            "cos": np.tile(np.cos(angles), (GH, 1)), "sin": np.tile(np.sin(angles), (GH, 1)), "ranks": ranks}


def kernel(**inputs):
    import concourse.bacc as bacc
    from concourse.bass_utils import run_bass_kernel_spmd

    a = {n.removeprefix("L0_"): np.asarray(v) for n, v in inputs.items()}
    attn_b = a["attn_c_attn_b"].reshape(3, C, 1)
    arrays = {
        "x": a["attn_x"],
        "gate_up": np.stack([np.concatenate([a[r], a[s][None]]).reshape(E * I, C).T for r, s in (("ffn_rg", "ffn_sg"), ("ffn_ru", "ffn_su"))]),
        "down": np.concatenate([a["ffn_rd"], a["ffn_sd"][None]]).transpose(0, 2, 1),
        "attn_w": a["attn_c_attn_w"].reshape(3, C, C),
        "bd_q": _blocks(a["attn_q2l_w"].T, H),
        "bd_kv": _blocks(a["attn_kv2l_w"].T, H),
        "bd_qk": _blocks(a["attn_wqk_w"].T, GH),
        "bd_o": _blocks(a["attn_l2o_w"].T, H).reshape(G, P, H * HD).reshape(G * P, C),
        "cproj": a["attn_cproj_w"].T,
        "biases": np.concatenate([_column(a["attn_q2l_b"], GH), _column(a["attn_kv2l_b"], GH), _column(a["attn_wqk_b"], GH),
                                  _column(a["attn_kv2l_b"], GH), _column(a["attn_l2o_b"], H), *attn_b], axis=1),
        "out_bias": a["attn_cproj_b"].reshape(1, C),
        "router_w": a["ffn_wr"].T,
        "router_b": a["ffn_rb"].reshape(1, ROUTED),
        **_tables(),
    }
    arrays = {n: np.ascontiguousarray(v) for n, v in arrays.items()}
    nc = bacc.Bacc("TRN2", target_bir_lowering=False, num_devices=1)
    aps = {n: nc.dram_tensor(f"in_{n}", v.shape, mybir.dt.from_np(v.dtype), kind="ExternalInput").ap() for n, v in arrays.items()}
    out = nc.dram_tensor("out", (B, T, C), F32, kind="ExternalOutput").ap()
    build(nc, out=out, **aps)
    r = run_bass_kernel_spmd(nc, [{f"in_{n}": v for n, v in arrays.items()}], core_ids=[0])
    return r.results[0]["out"]
```
